# Optimizing a Trainium2 kernel written in Bass

```python
import numpy as np
import jax
import jax.numpy as jnp

def _softmax(x, axis=-1):
    return jax.nn.softmax(x, axis=axis)

def _gelu(x):
    return jax.nn.gelu(x, approximate=True)

def _silu(x):
    return jax.nn.silu(x)

def _sigmoid(x):
    return jax.nn.sigmoid(x)

def _layernorm(x, axis=-1, eps=1e-05):
    m = jnp.mean(x, axis=axis, keepdims=True)
    v = jnp.var(x, axis=axis, keepdims=True)
    return (x - m) / jnp.sqrt(v + eps)

def _scatter_add(tgt, idx, src, axis=0):
    return tgt.at[idx].add(src)

def _segment_sum(src, seg, n):
    return jax.ops.segment_sum(src, seg, n)
kernel_name = 'mk_gnn_preln_d4_gnn_r64_fe96eb'

def setup_inputs(seed: int=0):
    np.random.seed(seed)
    _w = jnp.asarray

    def _rec_inputs():
        import jax
        import jax.numpy as jnp
        _gk = jax.random.key(seed)
        x = -0.0005121 + 1.001 * jax.random.normal(jax.random.fold_in(_gk, 1), (100000, 64), jnp.float32)
        src = jax.random.randint(jax.random.fold_in(_gk, 2), (50000,), 0, 100000, jnp.int32)
        dst = jnp.minimum((100000 * jax.random.uniform(jax.random.fold_in(_gk, 3), (50000,)) ** 2.0).astype(jnp.int32), 99999)
        _o = jnp.argsort(dst, stable=True)
        src = src[_o]
        dst = dst[_o]
        edge_type_8 = jax.random.randint(jax.random.fold_in(_gk, 13), (50000,), 0, 8, jnp.int32)
        return (x, src, dst, edge_type_8)
    x, src, dst, edge_type_8 = _rec_inputs()

    def _L0_gnn_setup():
        import jax, jax.numpy as jnp
        import numpy as np
        N_NODES = 50000
        N_EDGES = 12500
        HIDDEN = 64

        def gcn_conv(x, src, dst, W, b, n_nodes):
            ones = jnp.ones(src.shape[0], dtype=x.dtype)
            deg = jax.ops.segment_sum(ones, dst, num_segments=n_nodes)
            dinv = jnp.where(deg > 0, jax.lax.rsqrt(jnp.maximum(deg, 1.0)), 0.0)
            norm = dinv[src] * dinv[dst]
            h = x @ W
            msg = h[src] * norm[:, None]
            out = jax.ops.segment_sum(msg, dst, num_segments=n_nodes)
            return out + b
        key = jax.random.key(seed)
        k1, k2, k3, k4 = jax.random.split(key, 4)
        scale = 1.0 / np.sqrt(HIDDEN)
        x = jax.random.normal(k1, (N_NODES, HIDDEN), dtype=jnp.float32)
        edge_index = jax.random.randint(k2, (2, N_EDGES), 0, N_NODES, dtype=jnp.int64)
        W1 = jax.random.normal(k3, (HIDDEN, HIDDEN), dtype=jnp.float32) * scale
        W2 = jax.random.normal(k4, (HIDDEN, HIDDEN), dtype=jnp.float32) * scale
        b1 = jnp.zeros((HIDDEN,), dtype=jnp.float32)
        b2 = jnp.zeros((HIDDEN,), dtype=jnp.float32)
        return {'x': x, 'edge_index': edge_index, 'W1': W1, 'b1': b1, 'W2': W2, 'b2': b2}
    _L0_gnn_all = _L0_gnn_setup()
    _L0_gnn_in = {k: v for k, v in _L0_gnn_all.items() if k in ('W1', 'b1', 'W2', 'b2')}
    del _L0_gnn_all

    def _L1_gnn_setup():
        import jax, jax.numpy as jnp
        import numpy as np
        N_NODES = 50000
        N_EDGES = 12500
        IN_DIM = 64
        OUT_DIM = 64
        N_REL = 8
        N_RULES = 32
        N_ACTIVE = 4
        LN_EPS = 1e-05

        def _seg_softmax(scores, seg, num_segments):
            m = jax.ops.segment_max(scores, seg, num_segments=num_segments)
            e = jnp.exp(scores - m[seg])
            d = jax.ops.segment_sum(e, seg, num_segments=num_segments)
            return e / d[seg]
        key = jax.random.key(seed)
        ks = jax.random.split(key, 12)
        x = jax.random.normal(ks[0], (N_NODES, IN_DIM), dtype=jnp.float32)
        edge_index = jax.random.randint(ks[1], (2, N_EDGES), 0, N_NODES, dtype=jnp.int64)
        edge_type = jax.random.randint(ks[2], (N_EDGES,), 0, N_REL, dtype=jnp.int64)
        rule_ids = jax.random.randint(ks[3], (N_ACTIVE,), 0, N_RULES, dtype=jnp.int64)
        W_r = jax.random.normal(ks[4], (N_REL, IN_DIM, OUT_DIM), dtype=jnp.float32) * (2.0 / (IN_DIM + OUT_DIM)) ** 0.5
        Wq_w = jax.random.normal(ks[5], (IN_DIM, OUT_DIM), dtype=jnp.float32) * (1.0 / IN_DIM) ** 0.5
        Wq_bias = jnp.zeros((OUT_DIM,), dtype=jnp.float32)
        Wk_w = jax.random.normal(ks[6], (3 * IN_DIM, OUT_DIM), dtype=jnp.float32) * (1.0 / (3 * IN_DIM)) ** 0.5
        Wk_bias = jnp.zeros((OUT_DIM,), dtype=jnp.float32)
        rule_emb = jax.random.normal(ks[7], (N_RULES, IN_DIM), dtype=jnp.float32) * (2.0 / (N_RULES + IN_DIM)) ** 0.5
        bias = jnp.zeros((OUT_DIM,), dtype=jnp.float32)
        ln_g = jnp.ones((OUT_DIM,), dtype=jnp.float32)
        ln_b = jnp.zeros((OUT_DIM,), dtype=jnp.float32)
        return {'x': x, 'edge_index': edge_index, 'edge_type': edge_type, 'rule_ids': rule_ids, 'W_r': W_r, 'Wq_w': Wq_w, 'Wq_bias': Wq_bias, 'Wk_w': Wk_w, 'Wk_bias': Wk_bias, 'rule_emb': rule_emb, 'bias': bias, 'ln_g': ln_g, 'ln_b': ln_b}
    _L1_gnn_all = _L1_gnn_setup()
    _L1_gnn_in = {k: v for k, v in _L1_gnn_all.items() if k in ('rule_ids', 'W_r', 'Wq_w', 'Wq_bias', 'Wk_w', 'Wk_bias', 'rule_emb', 'bias', 'ln_g', 'ln_b')}
    del _L1_gnn_all

    def _L2_gnn_setup():
        import jax, jax.numpy as jnp
        import numpy as np
        N = 100000
        E = 25000
        D_IN = 64
        D_HID = 64
        D_OUT = 64
        R = 8
        BN_EPS = 1e-05

        def rgcn_conv(x, edge_index, edge_type, W, root, bias):
            n, d = x.shape
            src, dst = (edge_index[0], edge_index[1])
            seg = dst * R + edge_type
            msg = x[src]
            agg = jax.ops.segment_sum(msg, seg, num_segments=n * R).reshape(n, R, d)
            cnt = jax.ops.segment_sum(jnp.ones((src.shape[0],), x.dtype), seg, num_segments=n * R).reshape(n, R, 1)
            mean = agg / jnp.maximum(cnt, 1.0)
            return jnp.einsum('nrd,rdo->no', mean, W) + x @ root + bias

        def batch_norm(h, gamma, beta):
            mu = h.mean(axis=0)
            var = h.var(axis=0)
            return gamma * (h - mu) * jax.lax.rsqrt(var + BN_EPS) + beta
        key = jax.random.key(seed)
        ks = jax.random.split(key, 12)
        x = jax.random.normal(ks[0], (N, D_IN), dtype=jnp.float32)
        edge_index = jax.random.randint(ks[1], (2, E), 0, N, dtype=jnp.int64)
        edge_type = jax.random.randint(ks[2], (E,), 0, R, dtype=jnp.int64)
        s1 = 1.0 / np.sqrt(D_IN)
        s2 = 1.0 / np.sqrt(D_HID)
        w1 = jax.random.uniform(ks[3], (R, D_IN, D_HID), jnp.float32, -s1, s1)
        root1 = jax.random.uniform(ks[4], (D_IN, D_HID), jnp.float32, -s1, s1)
        b1 = jnp.zeros((D_HID,), jnp.float32)
        gamma1 = jnp.ones((D_HID,), jnp.float32)
        beta1 = jnp.zeros((D_HID,), jnp.float32)
        w2 = jax.random.uniform(ks[5], (R, D_HID, D_OUT), jnp.float32, -s2, s2)
        root2 = jax.random.uniform(ks[6], (D_HID, D_OUT), jnp.float32, -s2, s2)
        b2 = jnp.zeros((D_OUT,), jnp.float32)
        return {'x': x, 'edge_index': edge_index, 'edge_type': edge_type, 'w1': w1, 'root1': root1, 'b1': b1, 'gamma1': gamma1, 'beta1': beta1, 'w2': w2, 'root2': root2, 'b2': b2}
    _L2_gnn_all = _L2_gnn_setup()
    _L2_gnn_in = {k: v for k, v in _L2_gnn_all.items() if k in ('w1', 'root1', 'b1', 'gamma1', 'beta1', 'w2', 'root2', 'b2')}
    del _L2_gnn_all

    def _L3_gnn_setup():
        import jax, jax.numpy as jnp
        import numpy as np
        N_NODES = 100000
        N_EDGES = 20000
        D = 64
        key = jax.random.key(seed)
        k1, k2, k3, k4, k5, k6 = jax.random.split(key, 6)
        feat = jax.random.normal(k1, (N_NODES, D), dtype=jnp.float32)
        W_attn = jax.random.normal(k2, (D, 2 * D), dtype=jnp.float32) * 0.1
        b_attn = jax.random.normal(k3, (D,), dtype=jnp.float32) * 0.1
        w_out = jax.random.normal(k4, (D,), dtype=jnp.float32) * 0.1
        src = jax.random.randint(k5, (N_EDGES,), 0, N_NODES, dtype=jnp.int32)
        dst = jax.random.randint(k6, (N_EDGES,), 0, N_NODES, dtype=jnp.int32)
        return {'feat': feat, 'W_attn': W_attn, 'b_attn': b_attn, 'w_out': w_out, 'src': src, 'dst': dst}
    _L3_gnn_all = _L3_gnn_setup()
    _L3_gnn_in = {k: v for k, v in _L3_gnn_all.items() if k in ('W_attn', 'b_attn', 'w_out')}
    del _L3_gnn_all
    return {'x': x, 'src': src, 'dst': dst, 'edge_type_8': edge_type_8, 'L0_gnn_W1': _L0_gnn_in['W1'], 'L0_gnn_b1': _L0_gnn_in['b1'], 'L0_gnn_W2': _L0_gnn_in['W2'], 'L0_gnn_b2': _L0_gnn_in['b2'], 'L1_gnn_rule_ids': _L1_gnn_in['rule_ids'], 'L1_gnn_W_r': _L1_gnn_in['W_r'], 'L1_gnn_Wq_w': _L1_gnn_in['Wq_w'], 'L1_gnn_Wq_bias': _L1_gnn_in['Wq_bias'], 'L1_gnn_Wk_w': _L1_gnn_in['Wk_w'], 'L1_gnn_Wk_bias': _L1_gnn_in['Wk_bias'], 'L1_gnn_rule_emb': _L1_gnn_in['rule_emb'], 'L1_gnn_bias': _L1_gnn_in['bias'], 'L1_gnn_ln_g': _L1_gnn_in['ln_g'], 'L1_gnn_ln_b': _L1_gnn_in['ln_b'], 'L2_gnn_w1': _L2_gnn_in['w1'], 'L2_gnn_root1': _L2_gnn_in['root1'], 'L2_gnn_b1': _L2_gnn_in['b1'], 'L2_gnn_gamma1': _L2_gnn_in['gamma1'], 'L2_gnn_beta1': _L2_gnn_in['beta1'], 'L2_gnn_w2': _L2_gnn_in['w2'], 'L2_gnn_root2': _L2_gnn_in['root2'], 'L2_gnn_b2': _L2_gnn_in['b2'], 'L3_gnn_W_attn': _L3_gnn_in['W_attn'], 'L3_gnn_b_attn': _L3_gnn_in['b_attn'], 'L3_gnn_w_out': _L3_gnn_in['w_out']}

def reference(x, src, dst, edge_type_8, L0_gnn_W1, L0_gnn_b1, L0_gnn_W2, L0_gnn_b2, L1_gnn_rule_ids, L1_gnn_W_r, L1_gnn_Wq_w, L1_gnn_Wq_bias, L1_gnn_Wk_w, L1_gnn_Wk_bias, L1_gnn_rule_emb, L1_gnn_bias, L1_gnn_ln_g, L1_gnn_ln_b, L2_gnn_w1, L2_gnn_root1, L2_gnn_b1, L2_gnn_gamma1, L2_gnn_beta1, L2_gnn_w2, L2_gnn_root2, L2_gnn_b2, L3_gnn_W_attn, L3_gnn_b_attn, L3_gnn_w_out):
    import jax
    import jax.numpy as jnp

    def _L0_gnn_ref(x, edge_index, W1, b1, W2, b2):
        import jax, jax.numpy as jnp
        import numpy as np
        N_NODES = 50000
        N_EDGES = 12500
        HIDDEN = 64

        def gcn_conv(x, src, dst, W, b, n_nodes):
            ones = jnp.ones(src.shape[0], dtype=x.dtype)
            deg = jax.ops.segment_sum(ones, dst, num_segments=n_nodes)
            dinv = jnp.where(deg > 0, jax.lax.rsqrt(jnp.maximum(deg, 1.0)), 0.0)
            norm = dinv[src] * dinv[dst]
            h = x @ W
            msg = h[src] * norm[:, None]
            out = jax.ops.segment_sum(msg, dst, num_segments=n_nodes)
            return out + b
        n = x.shape[0]
        src, dst = (edge_index[0], edge_index[1])
        h = jax.nn.relu(gcn_conv(x, src, dst, W1, b1, n))
        return gcn_conv(h, src, dst, W2, b2, n)

    def _L1_gnn_ref(x, edge_index, edge_type, rule_ids, W_r, Wq_w, Wq_bias, Wk_w, Wk_bias, rule_emb, bias, ln_g, ln_b):
        import jax, jax.numpy as jnp
        import numpy as np
        N_NODES = 50000
        N_EDGES = 12500
        IN_DIM = 64
        OUT_DIM = 64
        N_REL = 8
        N_RULES = 32
        N_ACTIVE = 4
        LN_EPS = 1e-05

        def _seg_softmax(scores, seg, num_segments):
            m = jax.ops.segment_max(scores, seg, num_segments=num_segments)
            e = jnp.exp(scores - m[seg])
            d = jax.ops.segment_sum(e, seg, num_segments=num_segments)
            return e / d[seg]
        src, dst = (edge_index[0], edge_index[1])
        num_nodes, in_dim = x.shape
        num_rel, _, out_dim = W_r.shape
        x_src = x[src]
        q = x[dst] @ Wq_w + Wq_bias
        rel_emb = W_r.mean(axis=-1)[edge_type]
        Wk1, Wk2, Wk3 = (Wk_w[:in_dim], Wk_w[in_dim:2 * in_dim], Wk_w[2 * in_dim:])
        key_base = x_src @ Wk1 + rel_emb @ Wk2 + Wk_bias
        h_R = rule_emb[rule_ids]
        key_rule = h_R @ Wk3
        scale = 1.0 / out_dim ** 0.5
        score_base = jnp.einsum('eo,eo->e', q, key_base)
        score_rule = jnp.einsum('eo,ro->er', q, key_rule)
        scores = (score_base[:, None] + score_rule) * scale
        attn = jax.vmap(lambda s: _seg_softmax(s, dst, num_nodes), in_axes=1, out_axes=1)(scores)
        mean_attn = attn.mean(axis=1)
        msg = jnp.zeros((x_src.shape[0], out_dim), dtype=x.dtype)
        for r in range(num_rel):
            msg = jnp.where((edge_type == r)[:, None], x_src @ W_r[r], msg)
        out = jax.ops.segment_sum(msg * mean_attn[:, None], dst, num_segments=num_nodes)
        out = out + bias
        mu = out.mean(axis=-1, keepdims=True)
        var = ((out - mu) ** 2).mean(axis=-1, keepdims=True)
        out = (out - mu) * jax.lax.rsqrt(var + LN_EPS) * ln_g + ln_b
        return jax.nn.relu(out)

    def _L2_gnn_ref(x, edge_index, edge_type, w1, root1, b1, gamma1, beta1, w2, root2, b2):
        import jax, jax.numpy as jnp
        import numpy as np
        N = 100000
        E = 25000
        D_IN = 64
        D_HID = 64
        D_OUT = 64
        R = 8
        BN_EPS = 1e-05

        def rgcn_conv(x, edge_index, edge_type, W, root, bias):
            n, d = x.shape
            src, dst = (edge_index[0], edge_index[1])
            seg = dst * R + edge_type
            msg = x[src]
            agg = jax.ops.segment_sum(msg, seg, num_segments=n * R).reshape(n, R, d)
            cnt = jax.ops.segment_sum(jnp.ones((src.shape[0],), x.dtype), seg, num_segments=n * R).reshape(n, R, 1)
            mean = agg / jnp.maximum(cnt, 1.0)
            return jnp.einsum('nrd,rdo->no', mean, W) + x @ root + bias

        def batch_norm(h, gamma, beta):
            mu = h.mean(axis=0)
            var = h.var(axis=0)
            return gamma * (h - mu) * jax.lax.rsqrt(var + BN_EPS) + beta
        h = rgcn_conv(x, edge_index, edge_type, w1, root1, b1)
        h = jax.nn.relu(batch_norm(h, gamma1, beta1))
        out = rgcn_conv(h, edge_index, edge_type, w2, root2, b2)
        return out

    def _L3_gnn_ref(feat, W_attn, b_attn, w_out, src, dst):
        import jax, jax.numpy as jnp
        import numpy as np
        N_NODES = 100000
        N_EDGES = 20000
        D = 64
        N = feat.shape[0]
        h_src = feat[src]
        h_dst = feat[dst]
        hc = jnp.concatenate([h_src, h_dst], axis=-1)
        hc = jnp.tanh(hc @ W_attn.T + b_attn)
        e = hc @ w_out
        m = jax.ops.segment_max(e, dst, num_segments=N)
        m = jnp.where(jnp.isfinite(m), m, 0.0)
        ex = jnp.exp(e - m[dst])
        denom = jax.ops.segment_sum(ex, dst, num_segments=N)
        alpha = ex / jnp.where(denom == 0.0, 1.0, denom)[dst]
        z = jax.ops.segment_sum(alpha[:, None] * h_src, dst, num_segments=N)
        return z
    edge_index = jnp.stack([src, dst])
    h = jnp.maximum(_layernorm(x, axis=-1), 0.0)
    x = x + _L0_gnn_ref(h, edge_index, L0_gnn_W1, L0_gnn_b1, L0_gnn_W2, L0_gnn_b2)
    h = jnp.maximum(_layernorm(x, axis=-1), 0.0)
    x = x + _L1_gnn_ref(h, edge_index, edge_type_8, L1_gnn_rule_ids, L1_gnn_W_r, L1_gnn_Wq_w, L1_gnn_Wq_bias, L1_gnn_Wk_w, L1_gnn_Wk_bias, L1_gnn_rule_emb, L1_gnn_bias, L1_gnn_ln_g, L1_gnn_ln_b)
    h = jnp.maximum(_layernorm(x, axis=-1), 0.0)
    x = x + _L2_gnn_ref(h, edge_index, edge_type_8, L2_gnn_w1, L2_gnn_root1, L2_gnn_b1, L2_gnn_gamma1, L2_gnn_beta1, L2_gnn_w2, L2_gnn_root2, L2_gnn_b2)
    h = jnp.maximum(_layernorm(x, axis=-1), 0.0)
    x = x + _L3_gnn_ref(h, L3_gnn_W_attn, L3_gnn_b_attn, L3_gnn_w_out, src, dst)
    return x

_drawn_inputs = setup_inputs


def setup_inputs(seed=0):
    import zlib

    import numpy as np

    out = dict(_drawn_inputs(seed))
    spreads = {'L0_gnn_b1': (0.0, 0.381),
     'L0_gnn_b2': (0.0, 0.1),
     'L1_gnn_Wq_bias': (0.0, 2.0),
     'L1_gnn_Wk_bias': (0.0, 2.0),
     'L1_gnn_bias': (0.0, 0.1),
     'L1_gnn_ln_g': (1.0, 0.2),
     'L1_gnn_ln_b': (0.0, 0.1),
     'L2_gnn_b1': (0.0, 2.0),
     'L2_gnn_gamma1': (1.0, 0.2),
     'L2_gnn_beta1': (0.0, 0.1),
     'L2_gnn_b2': (0.0, 0.1)}
    factors = {'L1_gnn_rule_emb': 64.0,
     'L3_gnn_W_attn': 3.554,
     'L3_gnn_b_attn': 8.0,
     'L3_gnn_w_out': 3.661}
    for name, (base, spread) in spreads.items():
        noise = np.random.default_rng([zlib.crc32(name.encode()), seed]).standard_normal(out[name].shape)
        drawn = base * np.exp(spread * noise) if base else spread * noise
        out[name] = jnp.asarray(drawn.astype(out[name].dtype))
    for name, factor in factors.items():
        out[name] = (out[name] * factor).astype(out[name].dtype)
    return out
```

```python
import numpy as np
import concourse.bass as bass
from concourse import mybir
from contextlib import ExitStack

F32 = mybir.dt.float32
I32 = mybir.dt.int32
BF16 = mybir.dt.bfloat16
ALU = mybir.AluOpType
ACT = mybir.ActivationFunctionType
AX = mybir.AxisListType

P = 128
D = 64
REL = 8
RULES = 4
T = 8
HUGE = 1.0e30
OUT_OF_RANGE = 1.0e6
EPS = 1e-5

SAME_PREV, SAME_NEXT, LAST, DINV_SRC, DINV_DST, REL_WEIGHT, ATTENTION, COUNTED = range(8)
SLOTS = 8
(B1_L0, B2_L0, BQ, BIAS_L1, LN_G, LN_B, B1_L2, GAMMA, BETA, B2_L2, B_ATT, W_OUT,
 INACTIVE_L1, BN_SCALE, BN_SHIFT, INACTIVE_X2, INACTIVE_OUT) = range(17)


class Chunk:

    def __init__(self, half, parity):
        self.half, self.k = half, parity
        self.index = half * 2 + parity


def at(i, k):
    return Chunk(i + k // 2, k % 2)


PASSED = []


def hold(eng, sem, value):
    eng.wait_ge(sem, value)
    if eng.engine == mybir.EngineType.SP:
        eng.sem_inc(PASSED[0], 1)


def settle(dve):
    dve.sem_inc(PASSED[1], 1)


def ready(eng, sems, c, each=1):
    hold(eng, sems[c.k], (c.half + 1) * each)


def free(eng, sems, c, each=1):
    if not (isinstance(c.half, int) and c.half == 0):
        hold(eng, sems[c.k], c.half * each)


def each_chunk(eng, chunks, step):
    pairs = chunks // 2
    step(at(0, 0))
    step(at(0, 1))
    with eng.Fori(1, pairs) as i:
        step(at(i, 0))
        step(at(i, 1))
    if chunks % 2:
        step(at(pairs, 0))


def leading(eng, chunks, first, second):
    pairs = chunks // 2
    first(at(0, 0))
    for k in range(2):
        first(at(0, k + 1))
        second(at(0, k))
    with eng.Fori(1, pairs) as i:
        for k in range(2):
            first(at(i, k + 1))
            second(at(i, k))
    second(at(pairs, 0))


def streamed(eng, chunks, loads, early, late):
    pairs = chunks // 2
    loads(at(0, 0))
    loads(at(0, 1))
    early(at(0, 0))
    loads(at(1, 0))
    early(at(0, 1))
    loads(at(1, 1))
    early(at(1, 0))
    late(at(0, 0))
    with eng.Fori(2, pairs) as i:
        for k in range(2):
            loads(at(i, k))
            early(at(i, k - 1))
            late(at(i, k - 3))
    loads(at(pairs, 0))
    early(at(pairs, -1))
    late(at(pairs, -3))
    early(at(pairs, 0))
    late(at(pairs, -2))
    late(at(pairs, -1))
    late(at(pairs, 0))


class Steps:

    def __init__(self, eng, sem):
        self.eng, self.sem, self.n, self.before = eng, sem, 0, 0

    def mark(self, ins):
        self.n += 1
        return ins.then_inc(self.sem, 1)

    def wait(self):
        self.eng.wait_ge(self.sem, self.before + self.n)

    def link(self, ins):
        self.mark(ins)
        self.wait()

    def repeat(self, i, first, per):
        self.before = (i - first) * per

    def repeated(self, trips, per):
        self.before = 0
        self.n += (trips - 1) * per


def skewed(dve, st, chunks, front, middle, back, finish):
    pairs = chunks // 2
    assert chunks == 2 * pairs + 1
    front(at(0, 0))
    back(at(0, 0))
    front(at(0, 1))
    middle(at(0, 0))
    back(at(0, 1))
    n = st.n
    front(at(0, 2))
    middle(at(0, 1))
    back(at(0, 2))
    finish(at(0, 0))
    per = 2 * (st.n - n)
    with dve.Fori(1, pairs) as i:
        st.repeat(i, 1, per)
        n = st.n
        for k in range(2):
            front(at(i, k + 1))
            middle(at(i, k))
            back(at(i, k + 1))
            finish(at(i, k - 1))
        assert st.n - n == per
    st.repeated(pairs - 1, per)
    middle(at(pairs, 0))
    finish(at(pairs, -1))
    finish(at(pairs, 0))


def build(nc, A, out):
    N = A["x"].shape[0]
    E = A["src"].shape[0]
    STEPS = -(-E // (P * T)) * T
    CH = STEPS // T
    EP = P * STEPS
    TN = 2 * T
    NODES = P * TN
    REST = (N - (CH - 1) * NODES) // TN
    assert 0 < N - (CH - 1) * NODES <= NODES and (N - (CH - 1) * NODES) % TN == 0 and CH % 2 == 1

    def dram(name, shape, dt=F32):
        return nc.dram_tensor(name, shape, dt).ap()

    dst_pad = dram("dst_pad", (EP + 2,), I32)
    idx_src = dram("idx_src", (P, STEPS), I32)
    idx_dst = dram("idx_dst", (P, STEPS), I32)
    idx_last = dram("idx_last", (P, STEPS), I32)
    idx_out = dram("idx_out", (P, STEPS), I32)
    info_src = dram("info_src", (P, STEPS, 2), I32)
    types_t = dram("types_t", (STEPS, P), BF16)
    node_info = dram("node_info", (N, 2), I32)
    x_info = dram("x_info", (N, D + 2))
    z_nodes = dram("z_nodes", (CH, P, TN * D))

    def table(name):
        return dram(name, (EP + 1, D))

    def rows(t):
        return t[0:EP, :].rearrange("(p t) d -> p t d", p=P)

    sum0a, sum0b, raw1, act1, sum2a, sum2b, fin = [
        table(n) for n in ("sum0a", "sum0b", "raw1", "act1", "sum2a", "sum2b", "fin")]
    xs, xd, x1s, x1d, msg, x2s, x2d, zs, zd, p3s, p3d, hs3, x3d = [
        dram(n, (EP, D)) for n in ("xs", "xd", "x1s", "x1d", "msg", "x2s", "x2d", "zs", "zd", "p3s", "p3d", "hs3", "x3d")]

    top = ExitStack()
    with top:
        def sb(name, shape, dt=F32, ctx=top):
            return ctx.enter_context(nc.sbuf_tensor(name, shape, dt))

        def ps(name, shape, ctx, dt=F32):
            return ctx.enter_context(nc.psum_tensor(name, shape, dt))

        in_phase = {}

        def sem(name, ctx):
            if ctx is top:
                return ctx.enter_context(nc.semaphore(name))
            if id(ctx) not in in_phase:
                in_phase[id(ctx)] = []
                ctx.callback(clear, ctx)
            in_phase[id(ctx)].append(nc.alloc_semaphore(name))
            return in_phase[id(ctx)][-1]

        def clear(ctx):
            nc.clear_and_free_semaphores(in_phase.pop(id(ctx)))
            nc.all_engine_barrier()

        def sems(name, ctx):
            return [sem(f"{name}{k}", ctx) for k in range(2)]

        PASSED[:] = [sem("sp_passed", top), sem("dve_passed", top)]

        slots = sb("slots", [P, CH, SLOTS, T])
        ident = sb("ident", [P, P])
        row = sb("row", [P, 17, D])
        wblock = sb("wblock", [P, 5, P])
        W1_L0, W2_L0, ROOT1, ROOT2, WQ = range(5)
        wrel = sb("wrel", [P, 3, REL // 2, D])
        wk1 = sb("wk1", [D, D])
        relk = sb("relk", [REL, D])
        wrule = sb("wrule", [P, 2 * RULES])
        brule = sb("brule", [P, RULES])
        watt = sb("watt", [P, D])
        relid = sb("relid", [P, REL // 2])
        relrow = sb("relrow", [P, 1])
        eps = sb("eps", [P, 1])
        lead_idx = sb("lead_idx", [P, 1], I32)
        seed_idx = sb("seed_idx", [P, 1], I32)
        lead_has = sb("lead_has", [P, 1])
        bk_rows = sb("bk_rows", [REL, D])
        rid_lane = sb("rid_lane", [P, 1], I32)
        lead_out = sb("lead_out", [P, 1], I32)
        prefix = sb("prefix", [P, STEPS])
        suffix = sb("suffix", [P, STEPS])
        same_prev = sb("same_prev", [P, STEPS])
        same_next = sb("same_next", [P, STEPS])
        join_prev = sb("join_prev", [P, P])
        join_next = sb("join_next", [P, P])
        pass_prev = sb("pass_prev", [P, P])
        pass_next = sb("pass_next", [P, P])
        scores = sb("scores", [P, STEPS, RULES])
        turn = sb("turn", [P, P])
        chain = sb("chain", [P, P])
        chain_in = sb("chain_in", [P, P])
        tail = sb("tail", [P, D])
        carried = sb("carried", [P, D])
        lead = sb("lead", [P, D])
        seed = sb("seed", [P, D])
        seed2 = sb("seed2", [P, D])
        node_stats = sb("node_stats", [P, 2 * CH, 6])
        bn_sums = sb("bn_sums", [P, 2, 2 * D])
        bn_col = sb("bn_col", [P, 2])

        def bc(v, n):
            return v[:, :, None].broadcast_to([P, n, D])

        def rb(which, n):
            return row[:, which, None, :].broadcast_to([P, n, D])

        def slot(which):
            return slots[:, :, which, :]

        def flat(v):
            return v.rearrange("p (c t) -> p c t", t=T)

        class Turner:

            def __init__(self, dve, st, asked, turned, result):
                self.dve, self.st, self.asked, self.turned, self.result, self.n = dve, st, asked, turned, result, 0

            def __call__(self):
                self.st.wait()
                self.dve.sem_inc(self.asked, 1)
                self.n += 1
                self.dve.wait_ge(self.turned, self.n)
                return self.result

        def turn_all(pe, asked, turned, result, n):
            for j in range(n):
                pe.wait_ge(asked, j + 1)
                nc.tensor.transpose(result[:, 0:P], turn[:, :], ident[:, :]).then_inc(turned, 1)

        def carry_sum(dve, st, turner, columns, result, backward=False):
            n = columns.shape[-1]
            join, passed = (join_next, pass_next) if backward else (join_prev, pass_prev)
            st.link(dve.tensor_copy(turn[:, 0:n], columns))
            t = turner()
            a, b = (slice(0, P - 1), slice(1, P)) if backward else (slice(1, P), slice(0, P - 1))
            st.link(dve.tensor_tensor(chain_in[:, a], join[:, a], t[:, b], ALU.mult))
            edge = slice(P - 1, P) if backward else slice(0, 1)
            st.link(dve.memset(chain_in[:, edge], 0.0))
            if backward:
                st.link(dve.tensor_tensor_scan(turn[:, ::-1], passed[:, ::-1], chain_in[:, ::-1], 0.0,
                                               ALU.mult, ALU.add))
            else:
                st.link(dve.tensor_tensor_scan(turn[:, :], passed[:, :], chain_in[:, :], 0.0,
                                               ALU.mult, ALU.add))
            t = turner()
            st.link(dve.tensor_copy(result, t[:, 0:n]))

        def carry_max(dve, st, turner, columns, result, backward=False):
            n = columns.shape[-1]
            join, passed = (join_next, pass_next) if backward else (join_prev, pass_prev)
            st.link(dve.tensor_copy(turn[:, 0:n], columns))
            t = turner()
            a, b = (slice(0, P - 1), slice(1, P)) if backward else (slice(1, P), slice(0, P - 1))
            st.link(dve.tensor_scalar(chain[:, :], join[:, :], 1.0, HUGE, ALU.subtract, ALU.mult))
            st.link(dve.memset(chain_in[:, :], -HUGE))
            st.link(dve.tensor_tensor(chain_in[:, a], chain[:, a], t[:, b], ALU.add))
            st.link(dve.tensor_scalar(chain[:, :], passed[:, :], 1.0, HUGE, ALU.subtract, ALU.mult))
            if backward:
                st.link(dve.tensor_tensor_scan(turn[:, ::-1], chain[:, ::-1], chain_in[:, ::-1], -HUGE,
                                               ALU.add, ALU.max))
            else:
                st.link(dve.tensor_tensor_scan(turn[:, :], chain[:, :], chain_in[:, :], -HUGE,
                                               ALU.add, ALU.max))
            t = turner()
            st.link(dve.tensor_copy(result, t[:, 0:n]))

        def clear_turn(dve, st):
            st.link(dve.memset(turn[:, :], 0.0))

        def edge_structure():
            ctx = ExitStack()
            with ctx:
                H = 1 + REL
                dst_i = sb("dst_i", [P, STEPS], I32, ctx)
                src_i = sb("src_i", [P, STEPS], I32, ctx)
                type_i = sb("type_i", [P, STEPS], I32, ctx)
                prev_i = sb("prev_i", [P, STEPS], I32, ctx)
                next_i = sb("next_i", [P, STEPS], I32, ctx)
                dst_f = sb("dst_f", [P, STEPS], F32, ctx)
                type_f = sb("type_f", [P, STEPS + P], F32, ctx)
                other = sb("other", [P, STEPS], F32, ctx)
                edge_no = sb("edge_no", [P, STEPS], F32, ctx)
                last = sb("last", [P, STEPS], F32, ctx)
                one = sb("one", [P, STEPS], F32, ctx)
                val = sb("val", [P, H, STEPS], F32, ctx)
                fwd = sb("fwd", [P, H, STEPS], F32, ctx)
                bwd = sb("bwd", [P, H, STEPS], F32, ctx)
                cf = sb("cf", [P, H], F32, ctx)
                cb = sb("cb", [P, H], F32, ctx)
                ends = sb("ends", [P, H], F32, ctx)
                tmp = sb("tmp", [P, STEPS], F32, ctx)
                tot = sb("tot", [P, STEPS], F32, ctx)
                weight = sb("weight", [P, STEPS], F32, ctx)
                root = sb("root", [P, STEPS], F32, ctx)
                idx_i = sb("idx_i", [P, STEPS], I32, ctx)
                idx_j = sb("idx_j", [P, STEPS], I32, ctx)
                types_b = sb("types_b", [P, 4, P], BF16, ctx)
                marks = sb("marks", [1, 2], I32, ctx)
                info = sb("info", [80, N // 80, 2], I32, ctx)
                info_rows = sb("info_rows", [P, STEPS, 2], I32, ctx)
                info_f = info_rows[:, :, :].bitcast(F32)
                out_idx = sb("out_idx", [P, STEPS], I32, ctx)
                zero = sb("zero", [1, D], F32, ctx)
                turned_ps = ps("turned_ps", [P, 512], ctx)
                step = sem("es_step", ctx)
                blank = sem("es_blank", ctx)
                loaded = sem("es_loaded", ctx)
                padded = sem("es_padded", ctx)
                shifted = sem("es_shifted", ctx)
                asked = sem("es_asked", ctx)
                turned = sem("es_turned", ctx)
                made = sem("es_made", ctx)
                deg = sem("es_deg", ctx)
                rooted = sem("es_rooted", ctx)
                types_ready = sem("es_types", ctx)
                idx_ready = sem("es_idx", ctx)
                stored = sem("es_stored", ctx)
                listed = sem("es_listed", ctx)
                info_set = sem("es_info", ctx)
                full = E // STEPS
                part = E - full * STEPS
                wide = full // 16 * 16
                block = ctx.enter_context(nc.Block())

                @block.sync
                def _(sp):
                    sp.wait_ge(blank, 7)
                    for dram_v, tile in ((A["dst"], dst_i), (A["src"], src_i), (A["edge_type_8"], type_i)):
                        v = dram_v[0:full * STEPS].rearrange("(p t) -> p t", t=STEPS)
                        sp.dma_start(tile[0:wide, :], v[0:wide, :]).then_inc(loaded, 16)
                        sp.dma_start(tile[wide:full, :], v[wide:full, :]).then_inc(loaded, 16)
                        sp.dma_start(tile[full:full + 1, 0:part],
                                     dram_v[full * STEPS:E].rearrange("(p t) -> p t", p=1)).then_inc(loaded, 16)
                    sp.dma_start(node_info.rearrange("(p r) c -> p r c", p=80), info[:, :, :]).then_inc(info_set, 16)
                    sp.wait_ge(loaded, 144)
                    sp.dma_start(dst_pad[1:EP + 1].rearrange("(p t) -> p t", p=P), dst_i[:, :]).then_inc(padded, 16)
                    sp.dma_start(dst_pad[0:1].rearrange("(p t) -> p t", p=1), marks[:, 0:1]).then_inc(padded, 16)
                    sp.dma_start(dst_pad[EP + 1:EP + 2].rearrange("(p t) -> p t", p=1),
                                 marks[:, 1:2]).then_inc(padded, 16)
                    sp.dma_start(idx_src, src_i[:, :]).then_inc(stored, 16)
                    for t in (sum0a, sum0b, raw1, sum2a, sum2b, fin):
                        sp.dma_start(t[EP:EP + 1, :], zero[:, :]).then_inc(stored, 16)
                    sp.wait_ge(padded, 48)
                    sp.dma_start(prev_i[:, :], dst_pad[0:EP].rearrange("(p t) -> p t", p=P)).then_inc(shifted, 16)
                    sp.dma_start(next_i[:, :], dst_pad[2:EP + 2].rearrange("(p t) -> p t", p=P)).then_inc(shifted, 16)
                    sp.wait_ge(types_ready, 4)
                    for j in range(4):
                        n = min(P, STEPS - j * P)
                        sp.dma_start(types_t[j * P:j * P + n, :], types_b[0:n, j, :]).then_inc(stored, 16)
                    sp.wait_ge(idx_ready, 1)
                    sp.dma_start(idx_dst, idx_j[:, :]).then_inc(stored, 16)
                    sp.wait_ge(listed, 1)
                    sp.dma_start(idx_out, out_idx[:, :]).then_inc(stored, 16)
                    sp.dma_start(info_src, info_rows[:, :, :]).then_inc(stored, 16)
                    sp.wait_ge(stored, 16 * 14)
                    sp.wait_ge(info_set, 16)

                @block.gpsimd
                def _(pool):
                    pool.memset(ident[:, :], 0.0).then_inc(made, 1)
                    pool.wait_ge(made, 1)
                    pool.affine_select(out=ident[:, :], in_=ident[:, :], compare_op=ALU.not_equal, fill=1.0,
                                       base=0, pattern=[[-1, P]], channel_multiplier=1).then_inc(made, 1)
                    pool.iota(idx_i[:, :], pattern=[[1, STEPS]], base=0, channel_multiplier=STEPS).then_inc(made, 1)

                @block.scalar
                def _(act):
                    act.wait_ge(deg, 1)
                    nc.scalar.activation(root[:, :], tot[:, :], ACT.Sqrt).then_inc(rooted, 1)

                @block.tensor
                def _(pe):
                    pe.wait_ge(made, 2)
                    turn_all(pe, asked, turned, turned_ps, 12)

                @block.vector
                def _(dve):
                    st = Steps(dve, step)
                    turner = Turner(dve, st, asked, turned, turned_ps)
                    dve.memset(dst_i[:, :], N).then_inc(blank, 1)
                    dve.memset(src_i[:, :], 0).then_inc(blank, 1)
                    dve.memset(type_i[:, :], 0).then_inc(blank, 1)
                    dve.memset(info[:, :, 0], EP).then_inc(blank, 1)
                    dve.memset(info[:, :, 1], 0).then_inc(blank, 1)
                    dve.memset(zero[:, :], 0.0).then_inc(blank, 1)
                    dve.memset(marks[:, :], -1).then_inc(blank, 1)
                    st.mark(dve.memset(slots[:, :, :, :], 0.0))
                    st.mark(dve.memset(one[:, :], 1.0))
                    st.mark(dve.memset(eps[:, :], EPS))
                    st.mark(dve.memset(type_f[:, STEPS:STEPS + P], 0.0))
                    for rr in range(REL // 2):
                        st.mark(dve.memset(relid[0:D, rr:rr + 1], 2.0 * rr))
                        st.mark(dve.memset(relid[D:P, rr:rr + 1], 2.0 * rr + 1.0))
                    dve.wait_ge(loaded, 144)
                    st.mark(dve.tensor_copy(dst_f[:, :], dst_i[:, :]))
                    st.link(dve.tensor_copy(type_f[:, 0:STEPS], type_i[:, :]))
                    dve.tensor_scalar(idx_j[:, :], dst_f[:, :], float(N - 1), None, ALU.min).then_inc(idx_ready, 1)
                    for j in range(4):
                        st.link(dve.tensor_copy(turn[:, :], type_f[:, j * P:(j + 1) * P]))
                        turner()
                        dve.tensor_copy(types_b[:, j, :], turned_ps[:, 0:P]).then_inc(types_ready, 1)
                        dve.wait_ge(types_ready, j + 1)
                    dve.wait_ge(shifted, 32)
                    st.link(dve.tensor_copy(other[:, :], prev_i[:, :]))
                    st.link(dve.tensor_tensor(same_prev[:, :], dst_f[:, :], other[:, :], ALU.is_equal))
                    st.link(dve.tensor_copy(other[:, :], next_i[:, :]))
                    st.link(dve.tensor_tensor(same_next[:, :], dst_f[:, :], other[:, :], ALU.is_equal))
                    st.link(dve.tensor_scalar(last[:, :], same_next[:, :], -1.0, 1.0, ALU.mult, ALU.add))
                    st.link(dve.scalar_tensor_tensor(last[:, :], dst_f[:, :], float(N), last[:, :],
                                                     ALU.is_lt, ALU.mult))
                    st.link(dve.tensor_tensor_scan(prefix[:, :], same_prev[:, :], one[:, :], 1.0, ALU.mult, ALU.mult))
                    st.link(dve.tensor_tensor_scan(suffix[:, ::-1], same_next[:, ::-1], one[:, ::-1], 1.0,
                                                   ALU.mult, ALU.mult))
                    for v, to in ((same_prev[:, 0:1], join_prev), (prefix[:, STEPS - 1:STEPS], pass_prev),
                                  (same_next[:, STEPS - 1:STEPS], join_next), (suffix[:, 0:1], pass_next)):
                        st.link(dve.tensor_copy(turn[:, :], v.broadcast_to([P, P])))
                        t = turner()
                        st.link(dve.tensor_copy(to[:, :], t[:, 0:P]))
                    st.link(dve.tensor_copy(chain[:, :], pass_prev[:, :]))
                    st.link(dve.tensor_tensor(pass_prev[:, 1:P], join_prev[:, 1:P], chain[:, 0:P - 1], ALU.mult))
                    st.link(dve.memset(pass_prev[:, 0:1], 0.0))
                    st.link(dve.tensor_copy(chain[:, :], pass_next[:, :]))
                    st.link(dve.tensor_tensor(pass_next[:, 0:P - 1], join_next[:, 0:P - 1], chain[:, 1:P], ALU.mult))
                    st.link(dve.memset(pass_next[:, P - 1:P], 0.0))
                    st.mark(dve.memset(val[:, 0, :], 1.0))
                    for r in range(REL):
                        st.mark(dve.tensor_scalar(val[:, 1 + r, :], type_f[:, 0:STEPS], float(r), None, ALU.is_equal))
                    st.wait()
                    for h in range(H):
                        st.mark(dve.tensor_tensor_scan(fwd[:, h, :], same_prev[:, :], val[:, h, :], 0.0,
                                                       ALU.mult, ALU.add))
                        st.mark(dve.tensor_tensor_scan(bwd[:, h, ::-1], same_next[:, ::-1], val[:, h, ::-1], 0.0,
                                                       ALU.mult, ALU.add))
                    st.wait()
                    clear_turn(dve, st)
                    st.link(dve.tensor_copy(ends[:, :], fwd[:, :, STEPS - 1]))
                    carry_sum(dve, st, turner, ends[:, :], cf[:, :])
                    clear_turn(dve, st)
                    st.link(dve.tensor_copy(ends[:, :], bwd[:, :, 0]))
                    carry_sum(dve, st, turner, ends[:, :], cb[:, :], backward=True)

                    def total(h):
                        st.link(dve.tensor_tensor(tot[:, :], fwd[:, h, :], bwd[:, h, :], ALU.add))
                        st.link(dve.tensor_tensor(tot[:, :], tot[:, :], val[:, h, :], ALU.subtract))
                        st.link(dve.scalar_tensor_tensor(tot[:, :], prefix[:, :], cf[:, h:h + 1], tot[:, :],
                                                         ALU.mult, ALU.add))
                        st.link(dve.scalar_tensor_tensor(tot[:, :], suffix[:, :], cb[:, h:h + 1], tot[:, :],
                                                         ALU.mult, ALU.add))

                    for h in range(1, H):
                        total(h)
                        if h == 1:
                            st.link(dve.tensor_tensor(weight[:, :], tot[:, :], val[:, h, :], ALU.mult))
                        else:
                            st.link(dve.tensor_tensor(tot[:, :], tot[:, :], val[:, h, :], ALU.mult))
                            st.link(dve.tensor_tensor(weight[:, :], weight[:, :], tot[:, :], ALU.add))
                    st.link(dve.reciprocal(tmp[:, :], weight[:, :]))
                    st.link(dve.tensor_copy(slot(REL_WEIGHT), flat(tmp[:, :])))
                    total(0)
                    dve.sem_inc(deg, 1)
                    dve.wait_ge(rooted, 1)
                    st.link(dve.reciprocal(tmp[:, :], root[:, :]))
                    st.link(dve.tensor_copy(slot(DINV_DST), flat(tmp[:, :])))
                    st.mark(dve.tensor_copy(info_f[:, :, 1], tmp[:, :]))
                    st.mark(dve.tensor_copy(slot(SAME_PREV), flat(same_prev[:, :])))
                    st.mark(dve.tensor_copy(slot(SAME_NEXT), flat(same_next[:, :])))
                    st.mark(dve.tensor_copy(slot(LAST), flat(last[:, :])))
                    dve.wait_ge(made, 3)
                    st.mark(dve.tensor_copy(info_rows[:, :, 0], idx_i[:, :]))
                    st.link(dve.tensor_copy(edge_no[:, :], idx_i[:, :]))
                    def where(result, value, present):
                        st.link(dve.tensor_tensor(tmp[:, :], value, present, ALU.mult))
                        st.link(dve.tensor_scalar(other[:, :], present, -OUT_OF_RANGE, OUT_OF_RANGE,
                                                  ALU.mult, ALU.add))
                        st.link(dve.tensor_tensor(result, tmp[:, :], other[:, :], ALU.add))
                    where(out_idx[:, :], dst_f[:, :], last[:, :])
                    dve.sem_inc(listed, 1)
                    st.link(dve.tensor_tensor(tot[:, :], prefix[:, :], last[:, :], ALU.mult))
                    st.link(dve.tensor_tensor(weight[:, :], last[:, :], tot[:, :], ALU.subtract))
                    st.mark(dve.tensor_copy(slot(COUNTED), flat(weight[:, :])))
                    st.link(dve.reduce_sum(lead_has[:, :], tot[:, :], AX.X))
                    for value, result in ((edge_no, lead_idx), (dst_f, lead_out)):
                        st.link(dve.tensor_tensor(weight[:, :], value[:, :], tot[:, :], ALU.mult))
                        st.link(dve.reduce_sum(ends[:, 0:1], weight[:, :], AX.X))
                        st.link(dve.tensor_scalar(ends[:, 1:2], lead_has[:, :], -OUT_OF_RANGE, OUT_OF_RANGE,
                                                  ALU.mult, ALU.add))
                        st.link(dve.tensor_tensor(result[:, :], ends[:, 0:1], ends[:, 1:2], ALU.add))
                    st.link(dve.tensor_tensor(ends[:, 0:1], cb[:, 0:1], suffix[:, STEPS - 1:STEPS], ALU.mult))
                    st.link(dve.tensor_tensor(seed_idx[:, :], ends[:, 0:1], edge_no[:, STEPS - 1:STEPS], ALU.add))
                    st.wait()
                return

        def pool_rows(pool, begun, io, sides, done, c):
            pool.sem_inc(begun, 1)
            for t in range(T):
                io(t).then_inc(done[c.k], 16)

        def gather(pool, tile, dram_t, idx):
            return pool.indirect_dma_start(out=tile, out_offset=None, in_=dram_t,
                                           in_offset=bass.IndirectOffsetOnAxis(ap=idx, axis=0))

        def gather_valid(pool, tile, dram_t, idx):
            return pool.indirect_dma_start(out=tile, out_offset=None, in_=dram_t,
                                           in_offset=bass.IndirectOffsetOnAxis(ap=idx, axis=0),
                                           bounds_check=dram_t.shape[0] - 1, oob_is_err=False)

        def scatter_valid(pool, dram_t, idx, tile):
            return pool.indirect_dma_start(out=dram_t, out_offset=bass.IndirectOffsetOnAxis(ap=idx, axis=0),
                                           in_=tile, in_offset=None,
                                           bounds_check=dram_t.shape[0] - 1, oob_is_err=False)

        def edge_cols(v, c):
            return v[:, bass.ds(c.index * T, T)]

        def node_links():
            ctx = ExitStack()
            with ctx:
                idx = [sb(f"nl_idx{k}", [P, T], I32, ctx) for k in range(2)]
                rows_in = [sb(f"nl_rows{k}", [P, T, 2], I32, ctx) for k in range(2)]
                wk2 = sb("wk2", [P, D], F32, ctx)
                wk3 = sb("wk3", [D, D], F32, ctx)
                wq = sb("wq", [D, D], F32, ctx)
                wmean = sb("wmean", [P, REL // 2], F32, ctx)
                wsel = sb("wsel", [P, REL], F32, ctx)
                hrule = sb("hrule", [P, D], F32, ctx)
                hrule_t = sb("hrule_t", [D, RULES], F32, ctx)
                krule = sb("krule", [D, RULES], F32, ctx)
                wq_t = sb("wq_t", [D, D], F32, ctx)
                bq_col = sb("bq_col", [D, 1], F32, ctx)
                bq_all = sb("bq_all", [D, P], F32, ctx)
                wa = sb("wa", [P, P], F32, ctx)
                rid = sb("rid", [RULES, 1], I32, ctx)
                xc = sb("nl_xc", [P, D], F32, ctx)
                sq = sb("nl_sq", [P, D], F32, ctx)
                stat = sb("nl_stat", [P, 4], F32, ctx)
                lane = sb("nl_lane", [P, 1], F32, ctx)
                t_ps = ps("nl_t_ps", [P, 512], ctx)
                m_ps = ps("nl_m_ps", [P, 512], ctx)
                step = sem("nl_step", ctx)
                loaded = sems("nl_loaded", ctx)
                scattered = sems("nl_scattered", ctx)
                begun = sem("nl_begun", ctx)
                zeroed = sem("nl_zeroed", ctx)
                weights = sem("nl_weights", ctx)
                ruled = sem("nl_ruled", ctx)
                rid_in = sem("nl_rid", ctx)
                asked = sem("nl_asked", ctx)
                turned = sem("nl_turned", ctx)
                mm_ask = sem("nl_mm_ask", ctx)
                mm_done = sem("nl_mm_done", ctx)
                numbered = sem("nl_numbered", ctx)
                centred = sem("nl_centred", ctx)
                squared = sem("nl_squared", ctx)
                summed = sem("nl_summed", ctx)
                rooted = sem("nl_rooted", ctx)
                act_done = sem("nl_act_done", ctx)
                stored = sem("nl_stored", ctx)
                block = ctx.enter_context(nc.Block())

                @block.sync
                def _(sp):
                    def load(c):
                        free(sp, scattered, c, 16 * T)
                        sp.dma_start(idx[c.k][:, :], edge_cols(idx_out, c)).then_inc(loaded[c.k], 16)
                        sp.dma_start(rows_in[c.k][:, :, :], edge_cols(info_src, c)).then_inc(loaded[c.k], 16)
                    each_chunk(sp, CH, load)
                    sp.wait_ge(act_done, 1)
                    sp.dma_start(act1[EP:EP + 1, :], row[0:1, INACTIVE_L1, :]).then_inc(stored, 16)
                    sp.wait_ge(stored, 16)

                @block.gpsimd
                def _(pool):
                    pool.iota(rid_lane[:, :], pattern=[[1, 1]], base=0, channel_multiplier=1).then_inc(numbered, 1)
                    pool.wait_ge(rid_in, 16)
                    pool.wait_ge(zeroed, 1)
                    pool.sem_inc(begun, 1)
                    gather(pool, hrule[0:RULES, :], A["L1_gnn_rule_emb"], rid[:, :]).then_inc(ruled, 16)

                    def scatter(c):
                        ready(pool, loaded, c, 32)
                        pool_rows(pool, begun, lambda t: scatter_valid(
                            pool, node_info, idx[c.k][:, t:t + 1], rows_in[c.k][:, t, :]), 0, scattered, c)
                    each_chunk(pool, CH, scatter)
                    for k in range(2):
                        pool.wait_ge(scattered[k], 16 * T * (CH // 2 + (1 - k) * (CH % 2)))

                @block.scalar
                def _(act):
                    act.wait_ge(zeroed, 1)
                    n = 0
                    loads = []
                    for j, name in enumerate(("L0_gnn_W1", "L0_gnn_W2", "L2_gnn_root1", "L2_gnn_root2", "L1_gnn_Wq_w")):
                        for h in range(2):
                            loads.append((wblock[h * D:(h + 1) * D, j, h * D:(h + 1) * D], A[name]))
                    for j, name in enumerate(("L1_gnn_W_r", "L2_gnn_w1", "L2_gnn_w2")):
                        loads.append((wrel[:, j, :, :], A[name].rearrange("(a b) i o -> (b i) a o", b=2)))
                    loads += [(wk1[:, :], A["L1_gnn_Wk_w"][0:D, :]),
                              (wk2[0:D, :], A["L1_gnn_Wk_w"][D:2 * D, :]),
                              (wk2[D:P, :], A["L1_gnn_Wk_w"][D:2 * D, :]),
                              (wk3[:, :], A["L1_gnn_Wk_w"][2 * D:3 * D, :]),
                              (wq[:, :], A["L1_gnn_Wq_w"]),
                              (wa[0:D, :], A["L3_gnn_W_attn"]),
                              (bq_col[:, :], A["L1_gnn_Wq_bias"].rearrange("(d o) -> d o", o=1))]
                    for j, name in ((B1_L0, "L0_gnn_b1"), (B2_L0, "L0_gnn_b2"), (BQ, "L1_gnn_Wq_bias"),
                                    (BIAS_L1, "L1_gnn_bias"), (LN_G, "L1_gnn_ln_g"), (LN_B, "L1_gnn_ln_b"),
                                    (B1_L2, "L2_gnn_b1"), (GAMMA, "L2_gnn_gamma1"), (BETA, "L2_gnn_beta1"),
                                    (B2_L2, "L2_gnn_b2"), (B_ATT, "L3_gnn_b_attn"), (W_OUT, "L3_gnn_w_out")):
                        loads.append((row[:, j, :], A[name].rearrange("(o d) -> o d", o=1).broadcast_to([P, D])))
                    loads.append((bk_rows[:, :], A["L1_gnn_Wk_bias"].rearrange("(o d) -> o d", o=1).broadcast_to([REL, D])))
                    act.dma_start(rid[:, :], A["L1_gnn_rule_ids"].rearrange("(r o) -> r o", o=1)).then_inc(rid_in, 16)
                    for to, of in loads:
                        act.dma_start(to, of).then_inc(weights, 16)
                        n += 16
                    assert n == WEIGHTS
                    act.wait_ge(centred, 1)
                    nc.scalar.activation(sq[:, :], xc[:, :], ACT.Square).then_inc(squared, 1)
                    act.wait_ge(summed, 1)
                    nc.scalar.activation(stat[:, 2:3], stat[:, 1:2], ACT.Sqrt, bias=eps[:, :],
                                         scale=1.0 / D).then_inc(rooted, 1)

                @block.tensor
                def _(pe):
                    pe.wait_ge(mm_ask, 1)
                    nc.tensor.matmul(m_ps[0:REL, 0:D], wsel[:, :], wk2[:, :], start=True, stop=True).then_inc(mm_done, 1)
                    pe.wait_ge(asked, 1)
                    nc.tensor.transpose(t_ps[:, 0:P], turn[:, :], ident[:, :]).then_inc(turned, 1)
                    pe.wait_ge(mm_ask, 2)
                    nc.tensor.matmul(m_ps[0:D, 64:64 + RULES], wk3[:, :], hrule_t[:, :],
                                     start=True, stop=True).then_inc(mm_done, 1)
                    pe.wait_ge(asked, 2)
                    nc.tensor.transpose(t_ps[:, 0:P], turn[:, :], ident[:, :]).then_inc(turned, 1)
                    pe.wait_ge(mm_ask, 3)
                    nc.tensor.matmul(m_ps[0:D, 96:96 + RULES], wq_t[:, :], krule[:, :],
                                     start=True, stop=True).then_inc(mm_done, 1)
                    nc.tensor.matmul(m_ps[:, 128:128 + RULES], bq_all[:, :], krule[:, :],
                                     start=True, stop=True).then_inc(mm_done, 1)
                    pe.wait_ge(asked, 3)
                    nc.tensor.transpose(t_ps[:, 0:P], turn[:, :], ident[:, :]).then_inc(turned, 1)

                @block.vector
                def _(dve):
                    st = Steps(dve, step)
                    turner = Turner(dve, st, asked, turned, t_ps)
                    st.mark(dve.memset(wblock[:, :, :], 0.0))
                    st.mark(dve.memset(wsel[:, :], 0.0))
                    st.mark(dve.memset(wrule[:, :], 0.0))
                    st.mark(dve.memset(node_stats[:, :, :], 0.0))
                    st.link(dve.memset(turn[:, :], 0.0))
                    dve.sem_inc(zeroed, 1)
                    dve.wait_ge(numbered, 1)
                    st.link(dve.tensor_copy(lane[:, :], rid_lane[:, :]))
                    st.link(dve.tensor_scalar(stat[:, 0:1], lane[:, :], 4.0, -7.0, ALU.is_ge, ALU.mult))
                    st.link(dve.scalar_tensor_tensor(relrow[:, :], lane[:, :], 2.0, stat[:, 0:1], ALU.mult, ALU.add))
                    dve.wait_ge(weights, WEIGHTS)
                    st.link(dve.reduce_sum(wmean[:, :], wrel[:, 0, :, :], AX.X))
                    for h in range(2):
                        st.mark(dve.tensor_scalar(wsel[h * D:(h + 1) * D, h * 4:h * 4 + 4], wmean[h * D:(h + 1) * D, :],
                                                  1.0 / D, None, ALU.mult))
                    st.wait()
                    dve.sem_inc(mm_ask, 1)
                    dve.wait_ge(mm_done, 1)
                    st.mark(dve.tensor_tensor(relk[:, :], m_ps[0:REL, 0:D], bk_rows[:, :], ALU.add))
                    dve.wait_ge(ruled, 16)
                    st.link(dve.tensor_copy(turn[0:RULES, 0:D], hrule[0:RULES, :]))
                    t = turner()
                    st.link(dve.tensor_copy(hrule_t[:, :], t[0:D, 0:RULES]))
                    dve.sem_inc(mm_ask, 1)
                    st.mark(dve.memset(turn[:, :], 0.0))
                    st.wait()
                    st.link(dve.tensor_copy(turn[0:D, 0:D], wq[:, :]))
                    t = turner()
                    st.mark(dve.tensor_copy(wq_t[:, :], t[0:D, 0:D]))
                    st.mark(dve.tensor_copy(bq_all[:, :], bq_col[:, :].broadcast_to([D, P])))
                    dve.wait_ge(mm_done, 2)
                    st.link(dve.tensor_copy(krule[:, :], m_ps[0:D, 64:64 + RULES]))
                    dve.sem_inc(mm_ask, 1)
                    dve.wait_ge(mm_done, 4)
                    for h in range(2):
                        st.mark(dve.tensor_copy(wrule[h * D:(h + 1) * D, h * RULES:(h + 1) * RULES],
                                                m_ps[0:D, 96:96 + RULES]))
                    st.mark(dve.tensor_copy(brule[:, :], m_ps[:, 128:128 + RULES]))
                    st.link(dve.tensor_copy(turn[0:D, :], wa[0:D, :]))
                    t = turner()
                    st.mark(dve.tensor_copy(watt[:, :], t[:, 0:D]))
                    st.link(dve.reduce_sum(stat[:, 0:1], row[:, BIAS_L1, :], AX.X))
                    st.link(dve.tensor_scalar(stat[:, 0:1], stat[:, 0:1], 1.0 / D, None, ALU.mult))
                    st.link(dve.tensor_scalar(xc[:, :], row[:, BIAS_L1, :], stat[:, 0:1], None, ALU.subtract))
                    dve.sem_inc(centred, 1)
                    dve.wait_ge(squared, 1)
                    st.link(dve.reduce_sum(stat[:, 1:2], sq[:, :], AX.X))
                    dve.sem_inc(summed, 1)
                    dve.wait_ge(rooted, 1)
                    st.link(dve.reciprocal(stat[:, 3:4], stat[:, 2:3]))
                    st.link(dve.scalar_tensor_tensor(xc[:, :], xc[:, :], stat[:, 3:4], row[:, LN_G, :],
                                                     ALU.mult, ALU.mult))
                    st.link(dve.tensor_tensor(xc[:, :], xc[:, :], row[:, LN_B, :], ALU.add))
                    st.link(dve.tensor_scalar(row[:, INACTIVE_L1, :], xc[:, :], 0.0, None, ALU.max))
                    st.link(dve.tensor_tensor(row[:, INACTIVE_X2, :], row[:, INACTIVE_L1, :], row[:, B2_L0, :], ALU.add))
                    dve.sem_inc(act_done, 1)

        def centre(dve, st, x, mean, n, centred, c):
            st.link(dve.reduce_sum(mean, x, AX.X))
            st.link(dve.tensor_scalar(mean, mean, 1.0 / D, None, ALU.mult))
            dve.tensor_tensor(x, x, bc(mean, n), ALU.subtract).then_inc(centred[c.k], 1)

        def squares(act, x, sq, centred, squared, c):
            ready(act, centred, c)
            nc.scalar.activation(sq, x, ACT.Square).then_inc(squared[c.k], 1)

        def variance(dve, sq, var, squared, summed, c):
            ready(dve, squared, c)
            dve.reduce_sum(var, sq, AX.X).then_inc(summed[c.k], 1)

        def deviation(act, var, sd, summed, rooted, c):
            ready(act, summed, c)
            nc.scalar.activation(sd, var, ACT.Sqrt, bias=eps[:, :], scale=1.0 / D).then_inc(rooted[c.k], 1)

        def nodes_first():
            ctx = ExitStack()
            with ctx:
                def two(name, shape, dt=F32):
                    return [sb(f"nf_{name}{k}", shape, dt, ctx) for k in range(2)]
                idx = two("idx", [P, T], I32)
                got = two("got", [P, T, D])
                x = two("x", [P, TN, D + 2])
                info = two("info", [P, TN, 2])
                x2 = two("x2", [P, TN, D])
                sq = two("sq", [P, TN, D])
                h = two("h", [P, TN, D])
                mean = two("mean", [P, TN])
                var = two("var", [P, TN])
                sd = two("sd", [P, TN])
                scale = two("scale", [P, TN])
                ht = two("ht", [P, TN * D])
                z = two("z", [P, TN * D])
                t_ps = [ps(f"nf_t_ps{k}", [P, TN * D], ctx) for k in range(2)]
                z_ps = [ps(f"nf_z_ps{k}", [P, TN * D], ctx) for k in range(2)]
                step = sem("nf_step", ctx)
                begun = sem("nf_begun", ctx)
                blank = sem("nf_blank", ctx)
                (idx_in, gathered, got_out, x_in, x_out, merged, centred, squared, summed, rooted, h_ready,
                 h_turned, ht_ready, z_made, z_ready, z_seen, z_out) = [sems("nf_" + n, ctx) for n in (
                     "idx_in", "gathered", "got_out", "x_in", "x_out", "merged", "centred", "squared", "summed",
                     "rooted", "h_ready", "h_turned", "ht_ready", "z_made", "z_ready", "z_seen", "z_out")]
                block = ctx.enter_context(nc.Block())
                whole = (CH - 1) * NODES

                def nodes_of(v, c):
                    if isinstance(c.index, int) and c.index == CH - 1:
                        return v[whole:N, :].rearrange("(p t) d -> p t d", t=TN)
                    return v[bass.ds(c.index * NODES, NODES), :].rearrange("(p t) d -> p t d", t=TN)

                def parts(c):
                    return REST if isinstance(c.index, int) and c.index == CH - 1 else P

                @block.sync
                def _(sp):
                    def loads(c):
                        free(sp, gathered, c, 16 * T)
                        sp.dma_start(idx[c.k][:, :], edge_cols(idx_dst, c)).then_inc(idx_in[c.k], 16)
                        free(sp, merged, c)
                        free(sp, x_out, c, 16)
                        n = parts(c)
                        if n < P:
                            sp.wait_ge(blank, 2)
                        sp.dma_start(x[c.k][0:n, :, 0:D], nodes_of(A["x"], c)).then_inc(x_in[c.k], 16)
                        sp.dma_start(info[c.k][0:n, :, :], nodes_of(node_info, c).bitcast(F32)).then_inc(x_in[c.k], 16)

                    def early(c):
                        ready(sp, merged, c)
                        sp.dma_start(nodes_of(x_info, c), x[c.k][0:parts(c), :, :]).then_inc(x_out[c.k], 16)
                        ready(sp, gathered, c, 16 * T)
                        sp.dma_start(edge_cols(rows(xd), c), got[c.k][:, :, :]).then_inc(got_out[c.k], 16)

                    def late(c):
                        ready(sp, z_ready, c)
                        sp.dma_start(z_nodes[bass.ds(c.index, 1)].rearrange("o p n -> (o p) n"),
                                     z[c.k][:, :]).then_inc(z_out[c.k], 16)

                    streamed(sp, CH, loads, early, late)
                    for k in range(2):
                        n = CH // 2 + (1 - k)
                        sp.wait_ge(x_out[k], 16 * n)
                        sp.wait_ge(z_out[k], 16 * n)
                        sp.wait_ge(got_out[k], 16 * n)

                @block.gpsimd
                def _(pool):
                    def get(c):
                        if parts(c) < P:
                            free(pool, merged, c)
                            free(pool, x_out, c, 16)
                            pool.memset(x[c.k][:, :, 0:D], 0.0).then_inc(blank, 1)
                            pool.memset(info[c.k][:, :, :], 1.0).then_inc(blank, 1)
                        ready(pool, idx_in, c, 16)
                        free(pool, got_out, c, 16)
                        pool.sem_inc(begun, 1)
                        for t in range(T):
                            gather(pool, got[c.k][:, t, :], A["x"], idx[c.k][:, t:t + 1]).then_inc(gathered[c.k], 16)
                    each_chunk(pool, CH, get)

                @block.scalar
                def _(act):
                    def norm(c):
                        squares(act, x2[c.k][:, :, :], sq[c.k][:, :, :], centred, squared, c)
                        deviation(act, var[c.k][:, :], sd[c.k][:, :], summed, rooted, c)

                    def product(c):
                        ready(act, h_turned, c)
                        free(act, z_made, c)
                        nc.scalar.activation(ht[c.k][:, :], t_ps[c.k][:, :], ACT.Copy).then_inc(ht_ready[c.k], 1)
                        ready(act, z_made, c)
                        free(act, z_out, c, 16)
                        free(act, z_seen, c)
                        nc.scalar.activation(z[c.k][:, :], z_ps[c.k][:, :], ACT.Copy).then_inc(z_ready[c.k], 1)
                    leading(act, CH, norm, product)

                @block.tensor
                def _(pe):
                    def both(c):
                        ready(pe, h_ready, c)
                        free(pe, ht_ready, c)
                        for j in range(TN // 2):
                            last = nc.tensor.transpose(t_ps[c.k][:, j * P:(j + 1) * P],
                                                       h[c.k][:, 2 * j:2 * j + 2, :].rearrange("p t d -> p (t d)"),
                                                       ident[:, :])
                        last.then_inc(h_turned[c.k], 1)
                        ready(pe, ht_ready, c)
                        free(pe, z_ready, c)
                        for j in range(2):
                            last = nc.tensor.matmul(z_ps[c.k][:, j * 512:(j + 1) * 512], wblock[:, ROOT1, :],
                                                    ht[c.k][:, j * 512:(j + 1) * 512], start=True, stop=True)
                        last.then_inc(z_made[c.k], 1)
                    each_chunk(pe, CH, both)

                @block.vector
                def _(dve):
                    st = Steps(dve, step)

                    def front(c):
                        ready(dve, x_in, c, 32)
                        st.mark(dve.tensor_copy(x[c.k][:, :, D:D + 2].bitcast(I32), info[c.k][:, :, :].bitcast(I32)))
                        st.mark(dve.tensor_scalar(scale[c.k][:, :], info[c.k][:, :, 1], 0.0, None, ALU.is_equal))
                        st.link(dve.tensor_tensor(x2[c.k][:, :, :], x[c.k][:, :, 0:D], rb(INACTIVE_X2, TN), ALU.add))
                        dve.sem_inc(merged[c.k], 1)
                        centre(dve, st, x2[c.k][:, :, :], mean[c.k][:, :], TN, centred, c)

                    def middle(c):
                        pass

                    def back(c):
                        variance(dve, sq[c.k][:, :, :], var[c.k][:, :], squared, summed, c)
                        ready(dve, rooted, c)
                        st.link(dve.reciprocal(mean[c.k][:, :], sd[c.k][:, :]))
                        st.link(dve.tensor_tensor(scale[c.k][:, :], scale[c.k][:, :], mean[c.k][:, :], ALU.mult))
                        free(dve, h_turned, c)
                        dve.scalar_tensor_tensor(h[c.k][:, :, :], x2[c.k][:, :, :], 0.0, bc(scale[c.k][:, :], TN),
                                                 ALU.max, ALU.mult).then_inc(h_ready[c.k], 1)

                    def finish(c):
                        ready(dve, z_ready, c)
                        for j in range(2):
                            last = dve.bn_stats(node_stats[:, bass.ds(2 * c.index + j, 1), :].rearrange("p o s -> p (o s)"),
                                                z[c.k][:, j * 512:(j + 1) * 512])
                        last.then_inc(z_seen[c.k], 1)
                    skewed(dve, st, CH, front, middle, back, finish)

        def convolution(first):
            ctx = ExitStack()
            tag = "ca" if first else "cb"
            result = rows(sum0a if first else sum0b)
            with ctx:
                def two(name, shape, dt=F32):
                    return [sb(f"{tag}_{name}{k}", shape, dt, ctx) for k in range(2)]
                width = D + 2 if first else D
                idx = two("idx", [P, T], I32)
                g = two("g", [P, T, width])
                x = two("x", [P, T, D])
                sq = two("sq", [P, T, D])
                h = two("h", [P, T, D])
                mean = two("mean", [P, T])
                var = two("var", [P, T])
                sd = two("sd", [P, T])
                ptr = two("ptr", [P, T], I32)
                cur = two("cur", [P, SLOTS, T])
                fcur = sb(f"{tag}_fcur", [P, T], F32, ctx)
                ht = two("ht", [P, T * D])
                m = two("m", [P, T, D])
                s = two("s", [P, T, D])
                t_ps = [ps(f"{tag}_t_ps{k}", [P, T * D], ctx) for k in range(2)]
                m_ps = [ps(f"{tag}_m_ps{k}", [P, T * D], ctx) for k in range(2)]
                step = sem(tag + "_step", ctx)
                begun = sem(tag + "_begun", ctx)
                (idx_in, gathered, used, kept, split, x_out, centred, squared, summed, rooted, h_ready,
                 h_turned, ht_ready, m_made, m_ready, s_ready, s_out) = [sems(f"{tag}_{n}", ctx) for n in (
                     "idx_in", "gathered", "used", "kept", "split", "x_out", "centred", "squared", "summed",
                     "rooted", "h_ready", "h_turned", "ht_ready", "m_made", "m_ready", "s_ready", "s_out")]
                block = ctx.enter_context(nc.Block())
                stores = 2 if first else 0

                @block.sync
                def _(sp):
                    def loads(c):
                        free(sp, gathered, c, 16 * T)
                        sp.dma_start(idx[c.k][:, :], edge_cols(idx_src if first else idx_last, c)).then_inc(idx_in[c.k], 16)

                    def early(c):
                        if first:
                            ready(sp, split, c)
                            sp.dma_start(edge_cols(rows(xs), c), g[c.k][:, :, 0:D]).then_inc(x_out[c.k], 16)
                            sp.dma_start(edge_cols(idx_last, c), ptr[c.k][:, :]).then_inc(x_out[c.k], 16)

                    def late(c):
                        ready(sp, s_ready, c)
                        sp.dma_start(edge_cols(result, c), s[c.k][:, :, :]).then_inc(s_out[c.k], 16)
                    streamed(sp, CH, loads, early, late)
                    for k in range(2):
                        n = CH // 2 + (1 - k)
                        if first:
                            sp.wait_ge(x_out[k], 32 * n)
                        sp.wait_ge(s_out[k], 16 * n)

                @block.gpsimd
                def _(pool):
                    def get(c):
                        ready(pool, idx_in, c, 16)
                        free(pool, used, c)
                        if first:
                            free(pool, x_out, c, 32)
                        pool.sem_inc(begun, 1)
                        for t in range(T):
                            gather(pool, g[c.k][:, t, :], x_info if first else sum0a,
                                   idx[c.k][:, t:t + 1]).then_inc(gathered[c.k], 16)
                    each_chunk(pool, CH, get)

                @block.scalar
                def _(act):
                    def norm(c):
                        if first:
                            squares(act, x[c.k][:, :, :], sq[c.k][:, :, :], centred, squared, c)
                            deviation(act, var[c.k][:, :], sd[c.k][:, :], summed, rooted, c)

                    def product(c):
                        ready(act, h_turned, c)
                        free(act, m_made, c)
                        nc.scalar.activation(ht[c.k][:, :], t_ps[c.k][:, :], ACT.Copy).then_inc(ht_ready[c.k], 1)
                        ready(act, m_made, c)
                        free(act, s_ready, c)
                        nc.scalar.activation(m[c.k][:, :, :], m_ps[c.k][:, :].rearrange("p (t d) -> p t d", d=D),
                                             ACT.Copy).then_inc(m_ready[c.k], 1)
                    leading(act, CH, norm, product)

                @block.tensor
                def _(pe):
                    def both(c):
                        ready(pe, h_ready, c)
                        free(pe, ht_ready, c)
                        for j in range(T // 2):
                            last = nc.tensor.transpose(t_ps[c.k][:, j * P:(j + 1) * P],
                                                       h[c.k][:, 2 * j:2 * j + 2, :].rearrange("p t d -> p (t d)"),
                                                       ident[:, :])
                        last.then_inc(h_turned[c.k], 1)
                        ready(pe, ht_ready, c)
                        free(pe, m_ready, c)
                        for j in range(T // 2):
                            last = nc.tensor.matmul(m_ps[c.k][:, j * P:(j + 1) * P], ht[c.k][:, j * P:(j + 1) * P],
                                                    wblock[:, W1_L0 if first else W2_L0, :], start=True, stop=True)
                        last.then_inc(m_made[c.k], 1)
                    each_chunk(pe, CH, both)

                @block.vector
                def _(dve):
                    st = Steps(dve, step)
                    st.link(dve.memset(s[1][:, :, :], 0.0))

                    def front(c):
                        ready(dve, gathered, c, 16 * T)
                        if first:
                            free(dve, x_out, c, 32)
                            st.mark(dve.tensor_copy(ptr[c.k][:, :], g[c.k][:, :, D].bitcast(I32)))
                            st.mark(dve.tensor_copy(cur[c.k][:, DINV_SRC, :], g[c.k][:, :, D + 1]))
                            dve.tensor_copy(slots[:, bass.ds(c.index, 1), DINV_SRC, :].rearrange("p o t -> p (o t)"),
                                            g[c.k][:, :, D + 1]).then_inc(split[c.k], 1)
                            st.link(dve.tensor_copy(x[c.k][:, :, :], g[c.k][:, :, 0:D]))
                            dve.sem_inc(used[c.k], 1)
                            centre(dve, st, x[c.k][:, :, :], mean[c.k][:, :], T, centred, c)
                        else:
                            st.link(dve.tensor_copy(cur[c.k][:, :, :],
                                                    slots[:, bass.ds(c.index, 1), :, :].rearrange("p o s t -> p (o s) t")))
                            d = bc(cur[c.k][:, DINV_SRC, :], T)
                            st.link(dve.tensor_tensor(x[c.k][:, :, :], g[c.k][:, :, :], d, ALU.mult))
                            dve.sem_inc(used[c.k], 1)
                            st.link(dve.tensor_tensor(x[c.k][:, :, :], x[c.k][:, :, :], rb(B1_L0, T), ALU.add))
                            free(dve, h_turned, c)
                            dve.scalar_tensor_tensor(h[c.k][:, :, :], x[c.k][:, :, :], 0.0, d,
                                                     ALU.max, ALU.mult).then_inc(h_ready[c.k], 1)

                    def middle(c):
                        pass

                    def back(c):
                        if first:
                            variance(dve, sq[c.k][:, :, :], var[c.k][:, :], squared, summed, c)
                            ready(dve, rooted, c)
                            st.link(dve.reciprocal(mean[c.k][:, :], sd[c.k][:, :]))
                            st.link(dve.tensor_tensor(mean[c.k][:, :], mean[c.k][:, :], cur[c.k][:, DINV_SRC, :], ALU.mult))
                            free(dve, h_turned, c)
                            dve.scalar_tensor_tensor(h[c.k][:, :, :], x[c.k][:, :, :], 0.0, bc(mean[c.k][:, :], T),
                                                     ALU.max, ALU.mult).then_inc(h_ready[c.k], 1)

                    def finish(c):
                        st.link(dve.tensor_copy(fcur[:, :], slots[:, bass.ds(c.index, 1), SAME_PREV, :].rearrange("p o t -> p (o t)")))
                        ready(dve, m_ready, c)
                        free(dve, s_out, c, 16)
                        sum_along(dve, st, s, m[c.k], fcur, c)
                        dve.sem_inc(s_ready[c.k], 1)
                    skewed(dve, st, CH, front, middle, back, finish)
                    st.link(dve.tensor_copy(tail[:, :], s[0][:, T - 1, :]))

        def sum_along(dve, st, s, m, same, c):
            before = s[1 - c.k][:, T - 1, :]
            for t in range(T):
                st.link(dve.scalar_tensor_tensor(s[c.k][:, t, :], before, same[:, t:t + 1], m[:, t, :],
                                                 ALU.mult, ALU.add))
                before = s[c.k][:, t, :]

        def carry(tag, raw, table=None, more=None, stats=False):
            ctx = ExitStack()
            with ctx:
                t_ps = ps(tag + "_t_ps", [P, 512], ctx)
                m_ps = ps(tag + "_m_ps", [P, 512], ctx)
                extra = sb(tag + "_extra", [P, D], F32, ctx)
                pair = sb(tag + "_pair", [P, 2 * D], F32, ctx)
                work = sb(tag + "_work", [P, 3 * D], F32, ctx)
                step = sem(tag + "_step", ctx)
                blank = sem(tag + "_blank", ctx)
                got = sem(tag + "_got", ctx)
                made = sem(tag + "_made", ctx)
                put = sem(tag + "_put", ctx)
                asked = sem(tag + "_asked", ctx)
                turned = sem(tag + "_turned", ctx)
                act_go = sem(tag + "_act_go", ctx)
                act_done = sem(tag + "_act_done", ctx)
                counted = sem(tag + "_counted", ctx)
                summed = sem(tag + "_summed", ctx)
                block = ctx.enter_context(nc.Block())

                @block.gpsimd
                def _(pool):
                    pool.wait_ge(blank, 2)
                    gather_valid(pool, lead[:, :], raw, lead_idx[:, :]).then_inc(got, 16)
                    if stats or more == "final":
                        gather_valid(pool, extra[:, :], zd if stats else x3d, lead_idx[:, :]).then_inc(got, 16)
                    pool.wait_ge(made, 1)
                    to = table if table is not None else raw
                    scatter_valid(pool, to, lead_idx[:, :], lead[:, :]).then_inc(put, 16)
                    pool.wait_ge(put, 16)

                @block.tensor
                def _(pe):
                    turn_all(pe, asked, turned, t_ps, 2)
                    if stats:
                        pe.wait_ge(counted, 1)
                        nc.tensor.matmul(m_ps[:, 0:2 * D], lead_has[:, 0:1].broadcast_to([P, P]), pair[:, :],
                                         start=True, stop=True).then_inc(summed, 1)

                @block.scalar
                def _(act):
                    if stats:
                        act.wait_ge(act_go, 1)
                        nc.scalar.activation(pair[:, D:2 * D], pair[:, 0:D], ACT.Square).then_inc(act_done, 1)
                    if more == "layer1":
                        act.wait_ge(act_go, 1)
                        nc.scalar.activation(work[:, D:2 * D], work[:, 0:D], ACT.Square).then_inc(act_done, 1)
                        act.wait_ge(act_go, 2)
                        nc.scalar.activation(work[:, 2 * D + 1:2 * D + 2], work[:, 2 * D:2 * D + 1], ACT.Sqrt,
                                             bias=eps[:, :], scale=1.0 / D).then_inc(act_done, 1)

                @block.vector
                def _(dve):
                    st = Steps(dve, step)
                    turner = Turner(dve, st, asked, turned, t_ps)
                    dve.memset(lead[:, :], 0.0).then_inc(blank, 1)
                    dve.memset(extra[:, :], 0.0).then_inc(blank, 1)
                    clear_turn(dve, st)
                    carry_sum(dve, st, turner, tail[:, :], carried[:, :])
                    dve.wait_ge(got, 32 if stats or more == "final" else 16)
                    st.link(dve.tensor_tensor(lead[:, :], lead[:, :], carried[:, :], ALU.add))
                    if more == "final":
                        st.link(dve.tensor_tensor(lead[:, :], lead[:, :], extra[:, :], ALU.add))
                    if more == "layer1":
                        x, mu, sd, inv = work[:, 0:D], work[:, 2 * D + 2:2 * D + 3], work[:, 2 * D + 1:2 * D + 2], work[:, 2 * D + 3:2 * D + 4]
                        st.link(dve.tensor_tensor(x, lead[:, :], row[:, BIAS_L1, :], ALU.add))
                        st.link(dve.reduce_sum(mu, x, AX.X))
                        st.link(dve.tensor_scalar(mu, mu, 1.0 / D, None, ALU.mult))
                        st.link(dve.tensor_scalar(x, x, mu, None, ALU.subtract))
                        dve.sem_inc(act_go, 1)
                        dve.wait_ge(act_done, 1)
                        st.link(dve.reduce_sum(work[:, 2 * D:2 * D + 1], work[:, D:2 * D], AX.X))
                        dve.sem_inc(act_go, 1)
                        dve.wait_ge(act_done, 2)
                        st.link(dve.reciprocal(inv, sd))
                        st.link(dve.scalar_tensor_tensor(x, x, inv, row[:, LN_G, :], ALU.mult, ALU.mult))
                        st.link(dve.tensor_tensor(x, x, row[:, LN_B, :], ALU.add))
                        st.link(dve.tensor_scalar(lead[:, :], x, 0.0, None, ALU.max))
                    dve.sem_inc(made, 1)
                    if stats:
                        st.link(dve.tensor_tensor(pair[:, 0:D], lead[:, :], extra[:, :], ALU.add))
                        dve.sem_inc(act_go, 1)
                        dve.wait_ge(act_done, 1)
                        dve.sem_inc(counted, 1)
                        dve.wait_ge(summed, 1)
                        st.link(dve.tensor_copy(bn_sums[:, 1, :], m_ps[:, 0:2 * D]))

        def seeds(tag, first_table, second_table=None):
            ctx = ExitStack()
            with ctx:
                got = sem(tag + "_got", ctx)
                step = sem(tag + "_step", ctx)
                block = ctx.enter_context(nc.Block())

                @block.gpsimd
                def _(pool):
                    gather(pool, seed[:, :], first_table, seed_idx[:, :]).then_inc(got, 16)
                    if second_table is not None:
                        gather(pool, seed2[:, :], second_table, seed_idx[:, :]).then_inc(got, 16)

                @block.vector
                def _(dve):
                    dve.wait_ge(got, 16 if second_table is None else 32)
                    if second_table is not None:
                        dve.tensor_tensor(seed[:, :], seed[:, :], seed2[:, :], ALU.add).then_inc(step, 1)
                        dve.wait_ge(step, 1)


        def behind_cols(v, c):
            return v[:, bass.ds((CH - 1 - c.index) * T, T)]

        def prev(c):
            return at(c.half, c.k - 1)

        def ready_prev(eng, sems, c, each=1):
            if not (isinstance(c.index, int) and c.index == 0):
                ready(eng, sems, prev(c), each)

        def types_of(c, forward):
            first = (c.index if forward else CH - 1 - c.index) * T
            return types_t[bass.ds(first, T), :].rearrange("(o t) p -> o (t p)", o=1).broadcast_to([P, T * P])

        def broadcast_back(dve, st, b, tl, cur, c):
            before = b[1 - c.k][:, 0, :]
            for t in reversed(range(T)):
                st.link(dve.scalar_tensor_tensor(b[c.k][:, t, :], before, cur[:, SAME_NEXT, t:t + 1], tl[:, t, :],
                                                 ALU.mult, ALU.add))
                before = b[c.k][:, t, :]

        def centre_apart(dve, st, x, xc, mean, n, centred, c):
            st.link(dve.reduce_sum(mean, x, AX.X))
            st.link(dve.tensor_scalar(mean, mean, 1.0 / D, None, ALU.mult))
            dve.tensor_tensor(xc, x, bc(mean, n), ALU.subtract).then_inc(centred[c.k], 1)

        def layer1_scores():
            ctx = ExitStack()
            with ctx:
                def two(name, shape, dt=F32):
                    return [sb(f"a1_{name}{k}", shape, dt, ctx) for k in range(2)]
                idx = two("idx", [P, T], I32)
                g = two("g", [P, T, D])
                x0 = two("x0", [P, 2 * T, D])
                sums = two("sums", [P, T, D])
                types = two("types", [P, T * P], BF16)
                x = two("x", [P, 2 * T, D])
                xc = two("xc", [P, 2 * T, D])
                sq = two("sq", [P, 2 * T, D])
                b = two("b", [P, T, D])
                tl = sb("a1_tl", [P, T, D], F32, ctx)
                mean = two("mean", [P, 2 * T])
                var = two("var", [P, 2 * T])
                sd = two("sd", [P, 2 * T])
                cur = two("cur", [P, SLOTS, T])
                hs = two("hs", [P, T, 2, D])
                hd = two("hd", [P, T, D])
                hst = two("hst", [D, T * P])
                hdt = two("hdt", [P, T * D])
                by_rel = two("by_rel", [P, REL // 2, T * P])
                one_hot = two("one_hot", [REL, T * P])
                m = two("m", [P, T, D])
                key = two("key", [P, T, D])
                query = two("query", [P, T, D])
                rule = two("rule", [P, T, RULES])
                base = sb("a1_base", [P, T], F32, ctx)
                ts_ps = ps("a1_ts_ps", [P, T * P], ctx)
                td_ps = ps("a1_td_ps", [P, T * D], ctx)
                m_ps = ps("a1_m_ps", [P, T * D], ctx)
                k_ps = ps("a1_k_ps", [P, T * D], ctx)
                q_ps = ps("a1_q_ps", [P, T * D], ctx)
                r_ps = ps("a1_r_ps", [P, 512], ctx)
                step = sem("a1_step", ctx)
                begun = sem("a1_begun", ctx)
                (idx_in, gathered, g_used, x_in, x_used, types_in, types_used, x_ready, x_out, centred, squared,
                 summed, rooted, h_ready, h_twice, h_turned, ht_ready, parted, m_made, kq_made, m_ready,
                 kq_ready, kq_used, m_out) = [sems("a1_" + n, ctx) for n in (
                     "idx_in", "gathered", "g_used", "x_in", "x_used", "types_in", "types_used", "x_ready", "x_out",
                     "centred", "squared", "summed", "rooted", "h_ready", "h_twice", "h_turned", "ht_ready",
                     "parted", "m_made", "kq_made", "m_ready", "kq_ready", "kq_used", "m_out")]
                block = ctx.enter_context(nc.Block())

                @block.sync
                def _(sp):
                    def loads(c):
                        free(sp, gathered, c, 16 * T)
                        sp.dma_start(idx[c.k][:, :], behind_cols(idx_last, c)).then_inc(idx_in[c.k], 16)
                        free(sp, x_used, c)
                        sp.dma_start(x0[c.k][:, 0:T, :], behind_cols(rows(xs), c)).then_inc(x_in[c.k], 16)
                        sp.dma_start(x0[c.k][:, T:2 * T, :], behind_cols(rows(xd), c)).then_inc(x_in[c.k], 16)
                        sp.dma_start(sums[c.k][:, :, :], behind_cols(rows(sum0b), c)).then_inc(x_in[c.k], 16)

                    def early(c):
                        ready(sp, x_ready, c)
                        sp.dma_start(behind_cols(rows(x1s), c), x[c.k][:, 0:T, :]).then_inc(x_out[c.k], 16)
                        sp.dma_start(behind_cols(rows(x1d), c), x[c.k][:, T:2 * T, :]).then_inc(x_out[c.k], 16)
                        free(sp, types_used, c)
                        sp.dma_start(types[c.k][:, :], types_of(c, False)).then_inc(types_in[c.k], 16)

                    def late(c):
                        ready(sp, m_ready, c)
                        sp.dma_start(behind_cols(rows(msg), c), m[c.k][:, :, :]).then_inc(m_out[c.k], 16)
                    streamed(sp, CH, loads, early, late)
                    for k in range(2):
                        n = CH // 2 + (1 - k)
                        sp.wait_ge(x_out[k], 32 * n)
                        sp.wait_ge(m_out[k], 16 * n)

                @block.gpsimd
                def _(pool):
                    def get(c):
                        ready(pool, idx_in, c, 16)
                        free(pool, g_used, c)
                        pool.sem_inc(begun, 1)
                        for t in range(T):
                            gather(pool, g[c.k][:, t, :], sum0b, idx[c.k][:, t:t + 1]).then_inc(gathered[c.k], 16)
                    each_chunk(pool, CH, get)

                @block.scalar
                def _(act):
                    def norm(c):
                        squares(act, xc[c.k][:, :, :], sq[c.k][:, :, :], centred, squared, c)
                        deviation(act, var[c.k][:, :], sd[c.k][:, :], summed, rooted, c)
                        ready(act, h_ready, c)
                        nc.scalar.activation(hs[c.k][:, :, 1, :], hs[c.k][:, :, 0, :], ACT.Copy).then_inc(h_twice[c.k], 1)

                    def product(c):
                        ready(act, h_turned, c)
                        free(act, kq_made, c)
                        ready(act, parted, c)
                        nc.scalar.activation(hst[c.k][:, :], ts_ps[0:D, :], ACT.Copy)
                        nc.scalar.activation(hdt[c.k][:, :], td_ps[:, :], ACT.Copy).then_inc(ht_ready[c.k], 1)
                        ready(act, kq_made, c)
                        free(act, kq_used, c)
                        nc.scalar.activation(key[c.k][:, :, :], k_ps[:, :].rearrange("p (t d) -> p t d", d=D), ACT.Copy)
                        nc.scalar.activation(query[c.k][:, :, :], q_ps[:, :].rearrange("p (t d) -> p t d", d=D), ACT.Copy)
                        nc.scalar.activation(rule[c.k][:, :, :],
                                             r_ps[:, 0:T * RULES].rearrange("p (t r) -> p t r", r=RULES),
                                             ACT.Copy).then_inc(kq_ready[c.k], 1)
                        ready(act, m_made, c)
                        free(act, m_out, c, 16)
                        nc.scalar.activation(m[c.k][:, :, :], m_ps[:, :].rearrange("p (t d) -> p t d", d=D),
                                             ACT.Copy).then_inc(m_ready[c.k], 1)
                    leading(act, CH, norm, product)

                @block.tensor
                def _(pe):
                    def all_of(c):
                        ready(pe, h_twice, c)
                        ready_prev(pe, parted, c)
                        ready_prev(pe, ht_ready, c)
                        for t in range(T):
                            nc.tensor.transpose(ts_ps[:, t * P:(t + 1) * P],
                                                hs[c.k][:, t, :, :].rearrange("p a d -> p (a d)"), ident[:, :])
                        for j in range(T // 2):
                            last = nc.tensor.transpose(td_ps[:, j * P:(j + 1) * P],
                                                       hd[c.k][:, 2 * j:2 * j + 2, :].rearrange("p t d -> p (t d)"),
                                                       ident[:, :])
                        last.then_inc(h_turned[c.k], 1)
                        ready(pe, ht_ready, c)
                        ready(pe, parted, c)
                        ready_prev(pe, kq_ready, c)
                        for t in range(T):
                            nc.tensor.matmul(k_ps[:, t * D:(t + 1) * D], hst[c.k][:, t * P:(t + 1) * P], wk1[:, :],
                                             start=True, stop=False)
                            nc.tensor.matmul(k_ps[:, t * D:(t + 1) * D], one_hot[c.k][:, t * P:(t + 1) * P],
                                             relk[:, :], start=False, stop=True)
                        for j in range(T // 2):
                            w = hdt[c.k][:, j * P:(j + 1) * P]
                            nc.tensor.matmul(q_ps[:, j * P:(j + 1) * P], w, wblock[:, WQ, :], start=True, stop=True)
                            last = nc.tensor.matmul(r_ps[:, j * 2 * RULES:(j + 1) * 2 * RULES], w, wrule[:, :],
                                                    start=True, stop=True)
                        last.then_inc(kq_made[c.k], 1)
                        ready_prev(pe, m_ready, c)
                        relation_products(pe, m_ps, by_rel[c.k], 0).then_inc(m_made[c.k], 1)
                    each_chunk(pe, CH, all_of)

                @block.vector
                def _(dve):
                    st = Steps(dve, step)
                    st.link(dve.tensor_copy(b[1][:, 0, :], seed[:, :]))

                    def front(c):
                        st.link(dve.tensor_copy(cur[c.k][:, :, :], slots[:, bass.ds(CH - 1 - c.index, 1), :, :]
                                                .rearrange("p o s t -> p (o s) t")))
                        ready(dve, x_in, c, 48)
                        ready(dve, gathered, c, 16 * T)
                        free(dve, x_out, c, 32)
                        source, target = x[c.k][:, 0:T, :], x[c.k][:, T:2 * T, :]
                        st.mark(dve.tensor_tensor(source, g[c.k][:, :, :], bc(cur[c.k][:, DINV_SRC, :], T), ALU.mult))
                        st.link(dve.tensor_tensor(tl[:, :, :], sums[c.k][:, :, :], bc(cur[c.k][:, LAST, :], T), ALU.mult))
                        dve.sem_inc(g_used[c.k], 1)
                        broadcast_back(dve, st, b, tl, cur[c.k], c)
                        st.link(dve.tensor_tensor(target, b[c.k][:, :, :], bc(cur[c.k][:, DINV_DST, :], T), ALU.mult))
                        st.link(dve.tensor_tensor(x[c.k][:, :, :], x[c.k][:, :, :], x0[c.k][:, :, :], ALU.add))
                        dve.sem_inc(x_used[c.k], 1)
                        st.link(dve.tensor_tensor(x[c.k][:, :, :], x[c.k][:, :, :], rb(B2_L0, 2 * T), ALU.add))
                        dve.sem_inc(x_ready[c.k], 1)
                        centre_apart(dve, st, x[c.k][:, :, :], xc[c.k][:, :, :], mean[c.k][:, :], 2 * T, centred, c)

                    def middle(c):
                        ready(dve, h_turned, c)
                        ready(dve, types_in, c, 16)
                        free(dve, m_made, c)
                        part_relations(dve, st, by_rel[c.k], types[c.k], ts_ps)
                        st.mark(dve.tensor_scalar(one_hot[c.k][:, :], types[c.k][0:REL, :], relrow[0:REL, :], None,
                                                  ALU.is_equal))
                        st.wait()
                        dve.sem_inc(parted[c.k], 1)
                        dve.sem_inc(types_used[c.k], 1)

                    def back(c):
                        variance(dve, sq[c.k][:, :, :], var[c.k][:, :], squared, summed, c)
                        ready(dve, rooted, c)
                        st.link(dve.reciprocal(mean[c.k][:, :], sd[c.k][:, :]))
                        free(dve, h_turned, c)
                        st.mark(dve.scalar_tensor_tensor(hs[c.k][:, :, 0, :], xc[c.k][:, 0:T, :], 0.0,
                                                         bc(mean[c.k][:, 0:T], T), ALU.max, ALU.mult))
                        st.link(dve.scalar_tensor_tensor(hd[c.k][:, :, :], xc[c.k][:, T:2 * T, :], 0.0,
                                                         bc(mean[c.k][:, T:2 * T], T), ALU.max, ALU.mult))
                        dve.sem_inc(h_ready[c.k], 1)

                    def finish(c):
                        ready(dve, kq_ready, c)
                        q, r = query[c.k][:, :, :], rule[c.k][:, :, :]
                        st.link(dve.tensor_tensor(q, q, rb(BQ, T), ALU.add))
                        st.link(dve.tensor_tensor(q, q, key[c.k][:, :, :], ALU.mult))
                        st.link(dve.reduce_sum(base[:, :], q, AX.X))
                        st.link(dve.tensor_tensor(r, r, brule[:, None, :].broadcast_to([P, T, RULES]), ALU.add))
                        st.link(dve.tensor_tensor(r, r, base[:, :, None].broadcast_to([P, T, RULES]), ALU.add))
                        settle(dve)
                        st.link(dve.tensor_scalar(scores[:, bass.ds((CH - 1 - c.index) * T, T), :], r,
                                                  1.0 / D ** 0.5, None, ALU.mult))
                        dve.sem_inc(kq_used[c.k], 1)
                    skewed(dve, st, CH, front, middle, back, finish)

        def part_relations(dve, st, by_rel, types, turned):
            for rr in range(REL // 2):
                st.mark(dve.scalar_tensor_tensor(by_rel[:, rr, :], types[:, :], relid[:, rr:rr + 1], turned[:, :],
                                                 ALU.is_equal, ALU.mult))

        def relation_products(pe, m_ps, by_rel, which):
            for t in range(T):
                for rr in range(REL // 2):
                    last = nc.tensor.matmul(m_ps[:, t * D:(t + 1) * D], by_rel[:, rr, t * P:(t + 1) * P],
                                            wrel[:, which, rr, :], start=(rr == 0), stop=(rr == REL // 2 - 1))
            return last

        def softmax(tag, heads):
            ctx = ExitStack()
            with ctx:
                val = sb(tag + "_val", [P, heads, STEPS], F32, ctx)
                fwd = sb(tag + "_fwd", [P, heads, STEPS], F32, ctx)
                bwd = sb(tag + "_bwd", [P, heads, STEPS], F32, ctx)
                stop_p = sb(tag + "_stop_p", [P, STEPS], F32, ctx)
                stop_n = sb(tag + "_stop_n", [P, STEPS], F32, ctx)
                out_p = sb(tag + "_out_p", [P, STEPS], F32, ctx)
                out_n = sb(tag + "_out_n", [P, STEPS], F32, ctx)
                att = sb(tag + "_att", [P, STEPS], F32, ctx)
                cf = sb(tag + "_cf", [P, heads], F32, ctx)
                cb = sb(tag + "_cb", [P, heads], F32, ctx)
                ends = sb(tag + "_ends", [P, heads], F32, ctx)
                t_ps = ps(tag + "_t_ps", [P, 512], ctx)
                step = sem(tag + "_step", ctx)
                asked = sem(tag + "_asked", ctx)
                turned = sem(tag + "_turned", ctx)
                shifted = sem(tag + "_shifted", ctx)
                powers = sem(tag + "_powers", ctx)
                block = ctx.enter_context(nc.Block())

                @block.tensor
                def _(pe):
                    turn_all(pe, asked, turned, t_ps, 8)

                @block.scalar
                def _(act):
                    act.wait_ge(shifted, 1)
                    nc.scalar.activation(val[:, :, :], val[:, :, :], ACT.Exp).then_inc(powers, 1)

                @block.vector
                def _(dve):
                    st = Steps(dve, step)
                    turner = Turner(dve, st, asked, turned, t_ps)
                    for switch, to in ((same_prev, stop_p), (same_next, stop_n), (prefix, out_p), (suffix, out_n)):
                        st.mark(dve.tensor_scalar(to[:, :], switch[:, :], 1.0, HUGE, ALU.subtract, ALU.mult))
                    for h in range(heads):
                        st.mark(dve.tensor_copy(val[:, h, :], scores[:, :, h]))
                    st.wait()
                    for h in range(heads):
                        st.mark(dve.tensor_tensor_scan(fwd[:, h, :], stop_p[:, :], val[:, h, :], -HUGE,
                                                       ALU.add, ALU.max))
                        st.mark(dve.tensor_tensor_scan(bwd[:, h, ::-1], stop_n[:, ::-1], val[:, h, ::-1], -HUGE,
                                                       ALU.add, ALU.max))
                    st.wait()
                    clear_turn(dve, st)
                    st.link(dve.tensor_copy(ends[:, :], fwd[:, :, STEPS - 1]))
                    carry_max(dve, st, turner, ends[:, :], cf[:, :])
                    clear_turn(dve, st)
                    st.link(dve.tensor_copy(ends[:, :], bwd[:, :, 0]))
                    carry_max(dve, st, turner, ends[:, :], cb[:, :], backward=True)
                    for h in range(heads):
                        st.link(dve.tensor_tensor(fwd[:, h, :], fwd[:, h, :], bwd[:, h, :], ALU.max))
                        st.link(dve.scalar_tensor_tensor(fwd[:, h, :], out_p[:, :], cf[:, h:h + 1], fwd[:, h, :],
                                                         ALU.add, ALU.max))
                        st.link(dve.scalar_tensor_tensor(fwd[:, h, :], out_n[:, :], cb[:, h:h + 1], fwd[:, h, :],
                                                         ALU.add, ALU.max))
                    st.link(dve.tensor_tensor(val[:, :, :], val[:, :, :], fwd[:, :, :], ALU.subtract))
                    dve.sem_inc(shifted, 1)
                    dve.wait_ge(powers, 1)
                    for h in range(heads):
                        st.mark(dve.tensor_tensor_scan(fwd[:, h, :], same_prev[:, :], val[:, h, :], 0.0,
                                                       ALU.mult, ALU.add))
                        st.mark(dve.tensor_tensor_scan(bwd[:, h, ::-1], same_next[:, ::-1], val[:, h, ::-1], 0.0,
                                                       ALU.mult, ALU.add))
                    st.wait()
                    clear_turn(dve, st)
                    st.link(dve.tensor_copy(ends[:, :], fwd[:, :, STEPS - 1]))
                    carry_sum(dve, st, turner, ends[:, :], cf[:, :])
                    clear_turn(dve, st)
                    st.link(dve.tensor_copy(ends[:, :], bwd[:, :, 0]))
                    carry_sum(dve, st, turner, ends[:, :], cb[:, :], backward=True)
                    for h in range(heads):
                        st.link(dve.tensor_tensor(fwd[:, h, :], fwd[:, h, :], bwd[:, h, :], ALU.add))
                        st.link(dve.tensor_tensor(fwd[:, h, :], fwd[:, h, :], val[:, h, :], ALU.subtract))
                        st.link(dve.scalar_tensor_tensor(fwd[:, h, :], prefix[:, :], cf[:, h:h + 1], fwd[:, h, :],
                                                         ALU.mult, ALU.add))
                        st.link(dve.scalar_tensor_tensor(fwd[:, h, :], suffix[:, :], cb[:, h:h + 1], fwd[:, h, :],
                                                         ALU.mult, ALU.add))
                    st.link(dve.scalar_tensor_tensor(fwd[:, :, :], fwd[:, :, :], 0.0, fwd[:, :, :],
                                                     ALU.is_equal, ALU.add))
                    st.link(dve.reciprocal(fwd[:, :, :], fwd[:, :, :]))
                    st.link(dve.tensor_tensor(val[:, :, :], val[:, :, :], fwd[:, :, :], ALU.mult))
                    st.link(dve.tensor_scalar(att[:, :], val[:, 0, :], 1.0 / heads, None, ALU.mult))
                    for h in range(1, heads):
                        st.link(dve.scalar_tensor_tensor(att[:, :], val[:, h, :], 1.0 / heads, att[:, :],
                                                         ALU.mult, ALU.add))
                    st.link(dve.tensor_copy(slot(ATTENTION), flat(att[:, :])))

        def weighted(layer1):
            ctx = ExitStack()
            tag = "w1" if layer1 else "w3"
            with ctx:
                def two(name, shape, dt=F32):
                    return [sb(f"{tag}_{name}{k}", shape, dt, ctx) for k in range(2)]
                m = two("m", [P, T, D])
                x = two("x", [P, T, D])
                y = two("y", [P, T, D])
                s = two("s", [P, T, D])
                sq = two("sq", [P, T, D])
                am = sb(tag + "_am", [P, T, D], F32, ctx)
                mean = two("mean", [P, T])
                var = two("var", [P, T])
                sd = two("sd", [P, T])
                cur = sb(tag + "_cur", [P, SLOTS, T], F32, ctx)
                step = sem(tag + "_step", ctx)
                (m_in, m_used, s_ready, s_out, centred, squared, summed, rooted, y_ready, y_out) = [
                    sems(f"{tag}_{n}", ctx) for n in ("m_in", "m_used", "s_ready", "s_out", "centred", "squared",
                                                      "summed", "rooted", "y_ready", "y_out")]
                block = ctx.enter_context(nc.Block())
                ins = 1 if layer1 else 2

                @block.sync
                def _(sp):
                    def loads(c):
                        free(sp, m_used, c)
                        sp.dma_start(m[c.k][:, :, :], edge_cols(rows(msg if layer1 else hs3), c)).then_inc(m_in[c.k], 16)
                        if not layer1:
                            sp.dma_start(x[c.k][:, :, :], edge_cols(rows(x3d), c)).then_inc(m_in[c.k], 16)

                    def early(c):
                        if layer1:
                            ready(sp, s_ready, c)
                            sp.dma_start(edge_cols(rows(raw1), c), s[c.k][:, :, :]).then_inc(s_out[c.k], 16)
                        ready(sp, y_ready, c)
                        sp.dma_start(edge_cols(rows(act1 if layer1 else fin), c), y[c.k][:, :, :]).then_inc(y_out[c.k], 16)

                    streamed(sp, CH, loads, early, lambda c: None)
                    for k in range(2):
                        n = CH // 2 + (1 - k)
                        if layer1:
                            sp.wait_ge(s_out[k], 16 * n)
                        sp.wait_ge(y_out[k], 16 * n)

                if layer1:
                    @block.scalar
                    def _(act):
                        def norm(c):
                            squares(act, y[c.k][:, :, :], sq[c.k][:, :, :], centred, squared, c)
                            deviation(act, var[c.k][:, :], sd[c.k][:, :], summed, rooted, c)
                        each_chunk(act, CH, norm)

                @block.vector
                def _(dve):
                    st = Steps(dve, step)
                    st.link(dve.memset(s[1][:, :, :], 0.0))

                    def front(c):
                        st.link(dve.tensor_copy(cur[:, :, :], slots[:, bass.ds(c.index, 1), :, :]
                                                .rearrange("p o s t -> p (o s) t")))
                        ready(dve, m_in, c, 16 * ins)
                        st.link(dve.tensor_tensor(am[:, :, :], m[c.k][:, :, :], bc(cur[:, ATTENTION, :], T), ALU.mult))
                        if layer1:
                            dve.sem_inc(m_used[c.k], 1)
                            free(dve, s_out, c, 16)
                        sum_along(dve, st, s, am, cur[:, SAME_PREV, :], c)
                        free(dve, y_out, c, 16)
                        if layer1:
                            dve.sem_inc(s_ready[c.k], 1)
                            st.link(dve.tensor_tensor(y[c.k][:, :, :], s[c.k][:, :, :], rb(BIAS_L1, T), ALU.add))
                            centre(dve, st, y[c.k][:, :, :], mean[c.k][:, :], T, centred, c)
                        else:
                            st.link(dve.tensor_tensor(y[c.k][:, :, :], s[c.k][:, :, :], x[c.k][:, :, :], ALU.add))
                            dve.sem_inc(m_used[c.k], 1)
                            dve.sem_inc(y_ready[c.k], 1)

                    def back(c):
                        if layer1:
                            v = y[c.k][:, :, :]
                            variance(dve, sq[c.k][:, :, :], var[c.k][:, :], squared, summed, c)
                            ready(dve, rooted, c)
                            st.link(dve.reciprocal(mean[c.k][:, :], sd[c.k][:, :]))
                            st.link(dve.tensor_tensor(v, v, bc(mean[c.k][:, :], T), ALU.mult))
                            st.link(dve.tensor_tensor(v, v, rb(LN_G, T), ALU.mult))
                            st.link(dve.tensor_tensor(v, v, rb(LN_B, T), ALU.add))
                            st.link(dve.tensor_scalar(v, v, 0.0, None, ALU.max))
                            dve.sem_inc(y_ready[c.k], 1)
                    skewed(dve, st, CH, front, lambda c: None, back, lambda c: None)
                    st.link(dve.tensor_copy(tail[:, :], s[0][:, T - 1, :]))

        def relational(first):
            ctx = ExitStack()
            tag = "ra" if first else "rb"
            with ctx:
                def two(name, shape, dt=F32):
                    return [sb(f"{tag}_{name}{k}", shape, dt, ctx) for k in range(2)]
                idx = two("idx", [P, T], I32)
                g = two("g", [P, T, D])
                x0 = two("x0", [P, 2 * T, D])
                sums = two("sums", [P, T, D])
                types = two("types", [P, T * P], BF16)
                x = two("x", [P, 2 * T, D])
                xc = two("xc", [P, 2 * T, D])
                sq = two("sq", [P, 2 * T, D])
                mean = two("mean", [P, 2 * T])
                var = two("var", [P, 2 * T])
                sd = two("sd", [P, 2 * T])
                hs = two("hs", [P, T, 2, D])
                hd = two("hd", [P, T, D])
                hst = two("hst", [D, T * P])
                hdt = two("hdt", [P, T * D])
                by_rel = two("by_rel", [P, REL // 2, T * P])
                m = two("m", [P, T, D])
                s = two("s", [P, T, D])
                roots = two("roots", [P, 2, T, D])
                pair = two("pair", [P, T, 2, D])
                fcur = two("fcur", [P, SLOTS, T])
                zero = sb(tag + "_zero", [P, P], F32, ctx)
                ts_ps = ps(tag + "_ts_ps", [P, T * P], ctx)
                td_ps = ps(tag + "_td_ps", [P, T * D], ctx)
                m_ps = ps(tag + "_m_ps", [P, T * D], ctx)
                zs_ps = ps(tag + "_zs_ps", [P, T * D], ctx)
                zd_ps = ps(tag + "_zd_ps", [P, T * D], ctx)
                st_ps = ps(tag + "_st_ps", [P, 512], ctx)
                step = sem(tag + "_step", ctx)
                begun = sem(tag + "_begun", ctx)
                blank = sem(tag + "_blank", ctx)
                counted_all = sem(tag + "_counted_all", ctx)
                (idx_in, gathered, g_used, x_in, x_used, types_in, types_used, x_ready, x_out, centred, squared,
                 summed, rooted, h_ready, h_twice, h_turned, ht_ready, parted, z_made, m_made, z_ready, m_ready,
                 z_out, s_ready, s_out, total_ready, pair_ready, counted) = [sems(f"{tag}_{n}", ctx) for n in (
                     "idx_in", "gathered", "g_used", "x_in", "x_used", "types_in", "types_used", "x_ready", "x_out",
                     "centred", "squared", "summed", "rooted", "h_ready", "h_twice", "h_turned", "ht_ready",
                     "parted", "z_made", "m_made", "z_ready", "m_ready", "z_out", "s_ready", "s_out",
                     "total_ready", "pair_ready", "counted")]
                block = ctx.enter_context(nc.Block())
                if first:
                    table, source_in, target_in, target_sums, result = act1, x1s, x1d, act1, sum2a
                    root, which, root_s, root_d = ROOT1, 1, zs, zd
                else:
                    table, source_in, target_in, target_sums, result = sum2a, zs, zd, sum2a, sum2b
                    root, which, root_s, root_d = ROOT2, 2, p3s, p3d

                @block.sync
                def _(sp):
                    def loads(c):
                        free(sp, gathered, c, 16 * T)
                        sp.dma_start(idx[c.k][:, :], edge_cols(idx_last, c)).then_inc(idx_in[c.k], 16)
                        free(sp, x_used, c)
                        sp.dma_start(x0[c.k][:, 0:T, :], edge_cols(rows(source_in), c)).then_inc(x_in[c.k], 16)
                        sp.dma_start(x0[c.k][:, T:2 * T, :], edge_cols(rows(target_in), c)).then_inc(x_in[c.k], 16)
                        sp.dma_start(sums[c.k][:, :, :], edge_cols(rows(target_sums), c)).then_inc(x_in[c.k], 16)

                    def early(c):
                        if first:
                            ready(sp, x_ready, c)
                            sp.dma_start(edge_cols(rows(x2s), c), x[c.k][:, 0:T, :]).then_inc(x_out[c.k], 16)
                            sp.dma_start(edge_cols(rows(x2d), c), x[c.k][:, T:2 * T, :]).then_inc(x_out[c.k], 16)
                        free(sp, types_used, c)
                        sp.dma_start(types[c.k][:, :], types_of(c, True)).then_inc(types_in[c.k], 16)

                    def late(c):
                        ready(sp, z_ready, c)
                        sp.dma_start(edge_cols(rows(root_s), c), roots[c.k][:, 0, :, :]).then_inc(z_out[c.k], 16)
                        sp.dma_start(edge_cols(rows(root_d), c), roots[c.k][:, 1, :, :]).then_inc(z_out[c.k], 16)
                        ready(sp, s_ready, c)
                        sp.dma_start(edge_cols(rows(result), c), s[c.k][:, :, :]).then_inc(s_out[c.k], 16)
                    streamed(sp, CH, loads, early, late)
                    for k in range(2):
                        n = CH // 2 + (1 - k)
                        if first:
                            sp.wait_ge(x_out[k], 32 * n)
                        sp.wait_ge(z_out[k], 32 * n)
                        sp.wait_ge(s_out[k], 16 * n)

                @block.gpsimd
                def _(pool):
                    def get(c):
                        ready(pool, idx_in, c, 16)
                        free(pool, g_used, c)
                        pool.sem_inc(begun, 1)
                        for t in range(T):
                            gather(pool, g[c.k][:, t, :], table, idx[c.k][:, t:t + 1]).then_inc(gathered[c.k], 16)
                    each_chunk(pool, CH, get)

                @block.scalar
                def _(act):
                    def norm(c):
                        if first:
                            squares(act, xc[c.k][:, :, :], sq[c.k][:, :, :], centred, squared, c)
                            deviation(act, var[c.k][:, :], sd[c.k][:, :], summed, rooted, c)
                        ready(act, h_ready, c)
                        nc.scalar.activation(hs[c.k][:, :, 1, :], hs[c.k][:, :, 0, :], ACT.Copy).then_inc(h_twice[c.k], 1)

                    def square_sums(c):
                        ready(act, total_ready, c)
                        nc.scalar.activation(pair[c.k][:, :, 1, :], pair[c.k][:, :, 0, :], ACT.Square).then_inc(pair_ready[c.k], 1)

                    def product(c):
                        ready(act, h_turned, c)
                        free(act, z_made, c)
                        ready(act, parted, c)
                        nc.scalar.activation(hst[c.k][:, :], ts_ps[0:D, :], ACT.Copy)
                        nc.scalar.activation(hdt[c.k][:, :], td_ps[:, :], ACT.Copy).then_inc(ht_ready[c.k], 1)
                        ready(act, z_made, c)
                        free(act, z_out, c, 32)
                        free(act, s_ready, c)
                        for half, of in ((0, zs_ps), (1, zd_ps)):
                            last = nc.scalar.activation(roots[c.k][:, half, :, :],
                                                        of[:, :].rearrange("p (t d) -> p t d", d=D), ACT.Copy)
                        last.then_inc(z_ready[c.k], 1)
                        ready(act, m_made, c)
                        nc.scalar.activation(m[c.k][:, :, :], m_ps[:, :].rearrange("p (t d) -> p t d", d=D),
                                             ACT.Copy).then_inc(m_ready[c.k], 1)
                        if first and not (isinstance(c.index, int) and c.index == 0):
                            square_sums(prev(c))
                    leading(act, CH, norm, product)
                    if first:
                        square_sums(at(CH // 2, 0))

                @block.tensor
                def _(pe):
                    def count(c, final=False):
                        ready(pe, pair_ready, c)
                        for t in range(T):
                            last = nc.tensor.matmul(st_ps[:, 0:P], fcur[c.k][:, COUNTED, t:t + 1].broadcast_to([P, P]),
                                                    pair[c.k][:, t, :, :].rearrange("p a d -> p (a d)"),
                                                    start=False, stop=final and t == T - 1, skip_group_check=True)
                        last.then_inc(counted[c.k], 1)

                    def all_of(c):
                        ready(pe, h_twice, c)
                        ready_prev(pe, parted, c)
                        ready_prev(pe, ht_ready, c)
                        for t in range(T):
                            nc.tensor.transpose(ts_ps[:, t * P:(t + 1) * P],
                                                hs[c.k][:, t, :, :].rearrange("p a d -> p (a d)"), ident[:, :])
                        for j in range(T // 2):
                            last = nc.tensor.transpose(td_ps[:, j * P:(j + 1) * P],
                                                       hd[c.k][:, 2 * j:2 * j + 2, :].rearrange("p t d -> p (t d)"),
                                                       ident[:, :])
                        last.then_inc(h_turned[c.k], 1)
                        ready(pe, ht_ready, c)
                        ready_prev(pe, z_ready, c)
                        for t in range(T):
                            nc.tensor.matmul(zs_ps[:, t * D:(t + 1) * D], hst[c.k][:, t * P:(t + 1) * P],
                                             wblock[0:D, root, 0:D], start=True, stop=True)
                        for j in range(T // 2):
                            last = nc.tensor.matmul(zd_ps[:, j * P:(j + 1) * P], hdt[c.k][:, j * P:(j + 1) * P],
                                                    wblock[:, root, :], start=True, stop=True)
                        last.then_inc(z_made[c.k], 1)
                        ready(pe, parted, c)
                        ready_prev(pe, m_ready, c)
                        relation_products(pe, m_ps, by_rel[c.k], which).then_inc(m_made[c.k], 1)
                        if first and not (isinstance(c.half, int) and c.half == 0):
                            count(at(c.half - 1, c.k))

                    if first:
                        pe.wait_ge(blank, 1)
                        nc.tensor.matmul(st_ps[:, 0:P], zero[:, :], zero[:, :], start=True, stop=False,
                                         skip_group_check=True)
                    each_chunk(pe, CH, all_of)
                    if first:
                        count(at(CH // 2 - 1, 1))
                        count(at(CH // 2, 0), True)

                @block.vector
                def _(dve):
                    st = Steps(dve, step)
                    st.link(dve.memset(s[1][:, :, :], 0.0))
                    dve.memset(zero[:, :], 0.0).then_inc(blank, 1)

                    def front(c):
                        ready(dve, x_in, c, 48)
                        ready(dve, gathered, c, 16 * T)
                        v = x[c.k][:, :, :]
                        if first:
                            free(dve, x_out, c, 32)
                        st.mark(dve.tensor_tensor(x[c.k][:, 0:T, :], g[c.k][:, :, :], x0[c.k][:, 0:T, :], ALU.add))
                        st.link(dve.tensor_tensor(x[c.k][:, T:2 * T, :], sums[c.k][:, :, :], x0[c.k][:, T:2 * T, :], ALU.add))
                        dve.sem_inc(g_used[c.k], 1)
                        dve.sem_inc(x_used[c.k], 1)
                        if first:
                            dve.sem_inc(x_ready[c.k], 1)
                            centre_apart(dve, st, v, xc[c.k][:, :, :], mean[c.k][:, :], 2 * T, centred, c)
                        else:
                            st.link(dve.tensor_tensor(v, v, rb(BN_SCALE, 2 * T), ALU.mult))
                            st.link(dve.tensor_tensor(v, v, rb(BN_SHIFT, 2 * T), ALU.add))

                    def middle(c):
                        ready(dve, h_turned, c)
                        ready(dve, types_in, c, 16)
                        free(dve, m_made, c)
                        part_relations(dve, st, by_rel[c.k], types[c.k], ts_ps)
                        st.wait()
                        dve.sem_inc(parted[c.k], 1)
                        dve.sem_inc(types_used[c.k], 1)

                    def back(c):
                        if first:
                            variance(dve, sq[c.k][:, :, :], var[c.k][:, :], squared, summed, c)
                            ready(dve, rooted, c)
                            st.link(dve.reciprocal(mean[c.k][:, :], sd[c.k][:, :]))
                        free(dve, h_turned, c)
                        for to, a in ((hs[c.k][:, :, 0, :], 0), (hd[c.k][:, :, :], T)):
                            if first:
                                st.mark(dve.scalar_tensor_tensor(to, xc[c.k][:, a:a + T, :], 0.0,
                                                                 bc(mean[c.k][:, a:a + T], T), ALU.max, ALU.mult))
                            else:
                                st.mark(dve.tensor_scalar(to, x[c.k][:, a:a + T, :], 0.0, None, ALU.max))
                        st.wait()
                        dve.sem_inc(h_ready[c.k], 1)

                    def finish(c):
                        if first:
                            free(dve, counted, c)
                            settle(dve)
                        st.link(dve.tensor_copy(fcur[c.k][:, :, :], slots[:, bass.ds(c.index, 1), :, :]
                                                .rearrange("p o s t -> p (o s) t")))
                        ready(dve, m_ready, c)
                        free(dve, s_out, c, 16)
                        st.link(dve.tensor_tensor(m[c.k][:, :, :], m[c.k][:, :, :], bc(fcur[c.k][:, REL_WEIGHT, :], T), ALU.mult))
                        sum_along(dve, st, s, m[c.k], fcur[c.k][:, SAME_PREV, :], c)
                        if first:
                            ready(dve, z_ready, c)
                            st.link(dve.tensor_tensor(pair[c.k][:, :, 0, :], s[c.k][:, :, :], roots[c.k][:, 1, :, :], ALU.add))
                            dve.sem_inc(total_ready[c.k], 1)
                        dve.sem_inc(s_ready[c.k], 1)
                    skewed(dve, st, CH, front, middle, back, finish)
                    st.link(dve.tensor_copy(tail[:, :], s[0][:, T - 1, :]))
                    if first:
                        ready(dve, counted, at(CH // 2 - 1, 1))
                        ready(dve, counted, at(CH // 2, 0))
                        st.link(dve.tensor_copy(bn_sums[:, 0, :], st_ps[:, 0:P]))

        def batch_norm():
            ctx = ExitStack()
            with ctx:
                mv = sb("bn_mv", [P, 2], F32, ctx)
                ds = sb("bn_ds", [P, 2], F32, ctx)
                fold = sb("bn_fold", [P, D], F32, ctx)
                a = sb("bn_a", [P, 2, D], F32, ctx)
                sd = sb("bn_sd", [P, D], F32, ctx)
                r_ps = ps("bn_r_ps", [P, 512], ctx)
                t_ps = ps("bn_t_ps", [P, 512], ctx)
                step = sem("bn_step", ctx)
                asked = sem("bn_asked", ctx)
                turned = sem("bn_turned", ctx)
                go = sem("bn_go", ctx)
                spread = sem("bn_spread", ctx)
                var_ready = sem("bn_var", ctx)
                rooted = sem("bn_rooted", ctx)
                block = ctx.enter_context(nc.Block())
                each = CH * TN * P / 2

                @block.tensor
                def _(pe):
                    pe.wait_ge(go, 1)
                    for j in range(2):
                        last = nc.tensor.matmul(r_ps[:, j * D:(j + 1) * D], ds[:, j:j + 1].broadcast_to([P, P]),
                                                fold[:, :], start=True, stop=True)
                    last.then_inc(spread, 1)
                    turn_all(pe, asked, turned, t_ps, 2)

                @block.scalar
                def _(act):
                    act.wait_ge(var_ready, 1)
                    nc.scalar.activation(sd[:, :], a[:, 1, :], ACT.Sqrt, bias=eps[:, :]).then_inc(rooted, 1)

                @block.vector
                def _(dve):
                    st = Steps(dve, step)
                    turner = Turner(dve, st, asked, turned, t_ps)
                    st.mark(dve.tensor_tensor(fold[:, :], ident[:, 0:D], ident[:, D:P], ALU.add))
                    st.link(dve.bn_aggr(mv[:, :], node_stats[:, :, :]))
                    st.link(dve.tensor_scalar(ds[:, 0:1], mv[:, 0:1], each, None, ALU.mult))
                    st.link(dve.scalar_tensor_tensor(ds[:, 1:2], mv[:, 0:1], mv[:, 0:1], mv[:, 1:2], ALU.mult, ALU.add))
                    st.link(dve.tensor_scalar(ds[:, 1:2], ds[:, 1:2], each, None, ALU.mult))
                    dve.sem_inc(go, 1)
                    dve.wait_ge(spread, 1)
                    v = a[:, :, :].rearrange("p a d -> p (a d)")
                    st.link(dve.tensor_tensor(v, r_ps[:, 0:2 * D], bn_sums[:, 0, :], ALU.add))
                    st.link(dve.tensor_tensor(v, v, bn_sums[:, 1, :], ALU.add))
                    st.link(dve.tensor_scalar(v, v, 1.0 / N, None, ALU.mult))
                    mean, var, scale, shift = a[:, 0, :], a[:, 1, :], row[:, BN_SCALE, :], row[:, BN_SHIFT, :]
                    st.link(dve.tensor_tensor(shift, mean, mean, ALU.mult))
                    st.link(dve.tensor_tensor(var, var, shift, ALU.subtract))
                    dve.sem_inc(var_ready, 1)
                    dve.wait_ge(rooted, 1)
                    st.link(dve.reciprocal(scale, sd[:, :]))
                    st.link(dve.tensor_tensor(scale, scale, row[:, GAMMA, :], ALU.mult))
                    st.link(dve.tensor_tensor(mean, mean, row[:, B1_L2, :], ALU.add))
                    st.link(dve.tensor_tensor(shift, row[:, B1_L2, :], mean, ALU.subtract))
                    st.link(dve.tensor_tensor(shift, shift, scale, ALU.mult))
                    st.link(dve.tensor_tensor(shift, shift, row[:, BETA, :], ALU.add))
                    st.mark(dve.tensor_tensor(row[:, INACTIVE_OUT, :], row[:, INACTIVE_X2, :], row[:, B2_L2, :], ALU.add))
                    for j, of in ((0, scale), (1, shift)):
                        for h in range(2):
                            st.mark(dve.tensor_copy(turn[:, h * D:(h + 1) * D], of))
                        st.wait()
                        t = turner()
                        st.link(dve.tensor_copy(bn_col[:, j:j + 1], t[:, 0:1]))

        def layer3_scores():
            ctx = ExitStack()
            with ctx:
                def two(name, shape, dt=F32):
                    return [sb(f"a3_{name}{k}", shape, dt, ctx) for k in range(2)]
                idx = two("idx", [P, T], I32)
                g = two("g", [P, 2 * T, D])
                x0 = two("x0", [P, 2 * T, D])
                p0 = two("p0", [P, 2 * T, D])
                x = two("x", [P, 2 * T, D])
                xc = two("xc", [P, 2 * T, D])
                sq = two("sq", [P, 2 * T, D])
                tl = sb("a3_tl", [P, T, D], F32, ctx)
                b = two("b", [P, T, D])
                mean = two("mean", [P, 2 * T])
                var = two("var", [P, 2 * T])
                sd = two("sd", [P, 2 * T])
                cur = two("cur", [P, SLOTS, T])
                h = two("h", [P, T, 2, D])
                ht = two("ht", [P, T * P])
                m = two("m", [P, T, D])
                extra = sb("a3_extra", [P, D], F32, ctx)
                t_ps = ps("a3_t_ps", [P, T * P], ctx)
                m_ps = [ps(f"a3_m_ps{k}", [P, T * D], ctx) for k in range(2)]
                step = sem("a3_step", ctx)
                begun = sem("a3_begun", ctx)
                seeded = sem("a3_seeded", ctx)
                (idx_in, gathered, g_used, x_in, x_used, x_ready, x_out, centred, squared, summed, rooted, h_ready,
                 h_out, h_turned, ht_ready, m_made, biased, tanhed, m_used) = [sems("a3_" + n, ctx) for n in (
                     "idx_in", "gathered", "g_used", "x_in", "x_used", "x_ready", "x_out", "centred", "squared",
                     "summed", "rooted", "h_ready", "h_out", "h_turned", "ht_ready", "m_made", "biased", "tanhed",
                     "m_used")]
                block = ctx.enter_context(nc.Block())

                @block.sync
                def _(sp):
                    def loads(c):
                        free(sp, gathered, c, 16 * T)
                        sp.dma_start(idx[c.k][:, :], behind_cols(idx_last, c)).then_inc(idx_in[c.k], 16)
                        free(sp, x_used, c)
                        for to, of in ((x0[c.k][:, 0:T, :], x2s), (x0[c.k][:, T:2 * T, :], x2d),
                                       (p0[c.k][:, 0:T, :], p3s), (p0[c.k][:, T:2 * T, :], p3d),
                                       (g[c.k][:, T:2 * T, :], sum2b)):
                            sp.dma_start(to, behind_cols(rows(of), c)).then_inc(x_in[c.k], 16)

                    def early(c):
                        ready(sp, x_ready, c)
                        sp.dma_start(behind_cols(rows(x3d), c), b[c.k][:, :, :]).then_inc(x_out[c.k], 16)
                        ready(sp, h_ready, c)
                        sp.dma_start(behind_cols(rows(hs3), c), h[c.k][:, :, 0, :]).then_inc(h_out[c.k], 16)
                    streamed(sp, CH, loads, early, lambda c: None)
                    for k in range(2):
                        n = CH // 2 + (1 - k)
                        sp.wait_ge(x_out[k], 16 * n)
                        sp.wait_ge(h_out[k], 16 * n)

                @block.gpsimd
                def _(pool):
                    for to, of in ((seed, x2d), (seed2, p3d), (extra, sum2b)):
                        gather(pool, to[:, :], of, seed_idx[:, :]).then_inc(seeded, 16)

                    def get(c):
                        ready(pool, idx_in, c, 16)
                        free(pool, g_used, c)
                        pool.sem_inc(begun, 1)
                        for t in range(T):
                            gather(pool, g[c.k][:, t, :], sum2b, idx[c.k][:, t:t + 1]).then_inc(gathered[c.k], 16)
                    each_chunk(pool, CH, get)

                @block.scalar
                def _(act):
                    def norm(c):
                        squares(act, xc[c.k][:, :, :], sq[c.k][:, :, :], centred, squared, c)
                        deviation(act, var[c.k][:, :], sd[c.k][:, :], summed, rooted, c)

                    def bend(c):
                        ready(act, biased, c)
                        nc.scalar.activation(m[c.k][:, :, :], m[c.k][:, :, :], ACT.Tanh).then_inc(tanhed[c.k], 1)

                    def product(c):
                        ready(act, h_turned, c)
                        free(act, m_made, c)
                        nc.scalar.activation(ht[c.k][:, :], t_ps[:, :], ACT.Copy).then_inc(ht_ready[c.k], 1)
                        if not (isinstance(c.index, int) and c.index == 0):
                            bend(prev(c))
                    leading(act, CH, norm, product)
                    bend(at(CH // 2, 0))

                @block.tensor
                def _(pe):
                    def both(c):
                        ready(pe, h_ready, c)
                        ready_prev(pe, ht_ready, c)
                        for t in range(T):
                            last = nc.tensor.transpose(t_ps[:, t * P:(t + 1) * P],
                                                       h[c.k][:, t, :, :].rearrange("p a d -> p (a d)"), ident[:, :])
                        last.then_inc(h_turned[c.k], 1)
                        ready(pe, ht_ready, c)
                        free(pe, biased, c)
                        for t in range(T):
                            last = nc.tensor.matmul(m_ps[c.k][:, t * D:(t + 1) * D], ht[c.k][:, t * P:(t + 1) * P],
                                                    watt[:, :], start=True, stop=True)
                        last.then_inc(m_made[c.k], 1)
                    each_chunk(pe, CH, both)

                @block.vector
                def _(dve):
                    st = Steps(dve, step)
                    dve.wait_ge(seeded, 48)
                    st.link(dve.tensor_tensor(seed[:, :], seed[:, :], seed2[:, :], ALU.add))
                    st.link(dve.tensor_tensor(seed[:, :], seed[:, :], extra[:, :], ALU.add))
                    st.link(dve.tensor_tensor(b[1][:, 0, :], seed[:, :], row[:, B2_L2, :], ALU.add))

                    def front(c):
                        st.link(dve.tensor_copy(cur[c.k][:, :, :], slots[:, bass.ds(CH - 1 - c.index, 1), :, :]
                                                .rearrange("p o s t -> p (o s) t")))
                        ready(dve, x_in, c, 80)
                        ready(dve, gathered, c, 16 * T)
                        v = x[c.k][:, :, :]
                        st.link(dve.tensor_tensor(v, x0[c.k][:, :, :], p0[c.k][:, :, :], ALU.add))
                        st.link(dve.tensor_tensor(v, v, g[c.k][:, :, :], ALU.add))
                        dve.sem_inc(g_used[c.k], 1)
                        dve.sem_inc(x_used[c.k], 1)
                        st.link(dve.tensor_tensor(v, v, rb(B2_L2, 2 * T), ALU.add))
                        st.link(dve.tensor_tensor(tl[:, :, :], x[c.k][:, T:2 * T, :], bc(cur[c.k][:, LAST, :], T), ALU.mult))
                        free(dve, x_out, c, 16)
                        broadcast_back(dve, st, b, tl, cur[c.k], c)
                        dve.sem_inc(x_ready[c.k], 1)
                        st.link(dve.tensor_copy(x[c.k][:, T:2 * T, :], b[c.k][:, :, :]))
                        centre_apart(dve, st, v, xc[c.k][:, :, :], mean[c.k][:, :], 2 * T, centred, c)

                    def back(c):
                        variance(dve, sq[c.k][:, :, :], var[c.k][:, :], squared, summed, c)
                        ready(dve, rooted, c)
                        st.link(dve.reciprocal(mean[c.k][:, :], sd[c.k][:, :]))
                        free(dve, h_turned, c)
                        free(dve, h_out, c, 16)
                        for a in range(2):
                            st.mark(dve.scalar_tensor_tensor(h[c.k][:, :, a, :], xc[c.k][:, a * T:(a + 1) * T, :], 0.0,
                                                             bc(mean[c.k][:, a * T:(a + 1) * T], T), ALU.max, ALU.mult))
                        st.wait()
                        dve.sem_inc(h_ready[c.k], 1)

                    def finish(c):
                        ready(dve, m_made, c)
                        v = m[c.k][:, :, :]
                        dve.tensor_tensor(v, m_ps[c.k][:, :].rearrange("p (t d) -> p t d", d=D), rb(B_ATT, T),
                                          ALU.add).then_inc(biased[c.k], 1)
                        ready(dve, tanhed, c)
                        st.link(dve.tensor_tensor(v, v, rb(W_OUT, T), ALU.mult))
                        settle(dve)
                        st.mark(dve.reduce_sum(scores[:, bass.ds((CH - 1 - c.index) * T, T), 0], v, AX.X))
                    skewed(dve, st, CH, front, lambda c: None, back, finish)

        def nodes_last():
            ctx = ExitStack()
            with ctx:
                def two(name, shape, dt=F32):
                    return [sb(f"nz_{name}{k}", shape, dt, ctx) for k in range(2)]
                z = two("z", [P, TN * D])
                x = two("x", [P, TN, D])
                ht = two("ht", [P, TN * D])
                y = two("y", [P, TN, D])
                o_ps = [ps(f"nz_o_ps{k}", [P, TN * D], ctx) for k in range(2)]
                step = sem("nz_step", ctx)
                blank = sem("nz_blank", ctx)
                (z_in, x_in, h_ready, made, y_ready, y_out) = [sems("nz_" + n, ctx) for n in (
                    "z_in", "x_in", "h_ready", "made", "y_ready", "y_out")]
                block = ctx.enter_context(nc.Block())

                def nodes_of(v, c):
                    if isinstance(c.index, int) and c.index == CH - 1:
                        return v[(CH - 1) * NODES:N, :].rearrange("(p t) d -> p t d", t=TN)
                    return v[bass.ds(c.index * NODES, NODES), :].rearrange("(p t) d -> p t d", t=TN)

                def parts(c):
                    return REST if isinstance(c.index, int) and c.index == CH - 1 else P

                @block.sync
                def _(sp):
                    def loads(c):
                        free(sp, h_ready, c)
                        sp.dma_start(z[c.k][:, :], z_nodes[bass.ds(c.index, 1)].rearrange("o p n -> (o p) n")).then_inc(z_in[c.k], 16)
                        free(sp, y_ready, c)
                        sp.dma_start(x[c.k][0:parts(c), :, :], nodes_of(A["x"], c)).then_inc(x_in[c.k], 16)

                    def early(c):
                        ready(sp, y_ready, c)
                        sp.dma_start(nodes_of(out, c), y[c.k][0:parts(c), :, :]).then_inc(y_out[c.k], 16)
                    sp.wait_ge(blank, 1)
                    streamed(sp, CH, loads, early, lambda c: None)
                    for k in range(2):
                        sp.wait_ge(y_out[k], 16 * (CH // 2 + (1 - k)))

                @block.scalar
                def _(act):
                    def norm(c):
                        ready(act, z_in, c, 16)
                        free(act, made, c)
                        nc.scalar.activation(ht[c.k][:, :], z[c.k][:, :], ACT.Relu, bias=bn_col[:, 1:2],
                                             scale=bn_col[:, 0:1]).then_inc(h_ready[c.k], 1)
                    each_chunk(act, CH, norm)

                @block.tensor
                def _(pe):
                    def product(c):
                        ready(pe, h_ready, c)
                        free(pe, y_ready, c)
                        for j in range(TN // 2):
                            last = nc.tensor.matmul(o_ps[c.k][:, j * P:(j + 1) * P], ht[c.k][:, j * P:(j + 1) * P],
                                                    wblock[:, ROOT2, :], start=True, stop=True)
                        last.then_inc(made[c.k], 1)
                    each_chunk(pe, CH, product)

                @block.vector
                def _(dve):
                    st = Steps(dve, step)

                    def add(c):
                        ready(dve, x_in, c, 16)
                        ready(dve, made, c)
                        free(dve, y_out, c, 16)
                        v = y[c.k][:, :, :]
                        st.link(dve.tensor_tensor(v, o_ps[c.k][:, :].rearrange("p (t d) -> p t d", d=D),
                                                  x[c.k][:, :, :], ALU.add))
                        st.link(dve.tensor_tensor(v, v, rb(INACTIVE_OUT, TN), ALU.add))
                        dve.sem_inc(y_ready[c.k], 1)
                    for k in range(2):
                        st.mark(dve.memset(x[k][:, :, :], 0.0))
                    st.wait()
                    dve.sem_inc(blank, 1)
                    skewed(dve, st, CH, add, lambda c: None, lambda c: None, lambda c: None)

        def targets_out():
            ctx = ExitStack()
            with ctx:
                def two(name, shape, dt=F32):
                    return [sb(f"to_{name}{k}", shape, dt, ctx) for k in range(2)]
                idx = two("idx", [P, T], I32)
                y = two("y", [P, T, D])
                begun = sem("to_begun", ctx)
                loaded, scattered = sems("to_loaded", ctx), sems("to_scattered", ctx)
                block = ctx.enter_context(nc.Block())

                @block.sync
                def _(sp):
                    def load(c):
                        free(sp, scattered, c, 16 * T)
                        sp.dma_start(idx[c.k][:, :], edge_cols(idx_out, c)).then_inc(loaded[c.k], 16)
                        sp.dma_start(y[c.k][:, :, :], edge_cols(rows(fin), c)).then_inc(loaded[c.k], 16)
                    each_chunk(sp, CH, load)

                @block.gpsimd
                def _(pool):
                    def scatter(c):
                        ready(pool, loaded, c, 32)
                        pool.sem_inc(begun, 1)
                        for t in range(T):
                            scatter_valid(pool, out, idx[c.k][:, t:t + 1], y[c.k][:, t, :]).then_inc(scattered[c.k], 16)
                    each_chunk(pool, CH, scatter)
                    for k in range(2):
                        pool.wait_ge(scattered[k], 16 * T * (CH // 2 + (1 - k)))

        WEIGHTS = 16 * (10 + 3 + 7 + 12 + 1)
        edge_structure()
        node_links()
        nodes_first()
        convolution(True)
        carry("c0a", sum0a)
        convolution(False)
        carry("c0b", sum0b)
        seeds("se", sum0b)
        layer1_scores()
        softmax("s1", RULES)
        weighted(True)
        carry("c1", raw1, act1, "layer1")
        relational(True)
        carry("c2a", sum2a, stats=True)
        batch_norm()
        relational(False)
        carry("c2b", sum2b)
        layer3_scores()
        softmax("s3", 1)
        weighted(False)
        carry("c3", fin)
        nodes_last()
        targets_out()


_OUTS = [((100000, 64), "float32")]


def kernel(**inputs):
    import concourse.bacc as bacc
    from concourse.bass_utils import run_bass_kernel_spmd

    nc = bacc.Bacc("TRN2", target_bir_lowering=False, num_devices=1)
    arrays, args = {}, {}
    for name, value in inputs.items():
        a = np.ascontiguousarray(value)
        arrays[f"in_{name}"] = a
        args[name] = nc.dram_tensor(f"in_{name}", a.shape, mybir.dt.from_np(a.dtype), kind="ExternalInput").ap()
    shape, dtype = _OUTS[0]
    out = nc.dram_tensor("out", shape, mybir.dt.from_np(np.dtype(dtype)), kind="ExternalOutput").ap()
    build(nc, args, out)
    r = run_bass_kernel_spmd(nc, [arrays], core_ids=[0])
    return r.results[0]["out"]
```

```python
import numpy as np
import concourse.bass as bass
from concourse import mybir
from contextlib import ExitStack

F32 = mybir.dt.float32
I32 = mybir.dt.int32
BF16 = mybir.dt.bfloat16
ALU = mybir.AluOpType
ACT = mybir.ActivationFunctionType
AX = mybir.AxisListType

P = 128
D = 64
REL = 8
RULES = 4
T = 8
HUGE = 1.0e30
OUT_OF_RANGE = 1.0e6
EPS = 1e-5

SAME_PREV, SAME_NEXT, LAST, DINV_SRC, DINV_DST, REL_WEIGHT, ATTENTION, COUNTED = range(8)
SLOTS = 8
(B1_L0, B2_L0, BQ, BIAS_L1, LN_G, LN_B, B1_L2, GAMMA, BETA, B2_L2, B_ATT, W_OUT,
 INACTIVE_L1, BN_SCALE, BN_SHIFT, INACTIVE_X2, INACTIVE_OUT) = range(17)
ADD_B_ATT, ADD_INACTIVE = range(2)


class Chunk:

    def __init__(self, half, parity):
        self.half, self.k = half, parity
        self.index = half * 2 + parity


def at(i, k):
    return Chunk(i + k // 2, k % 2)


PASSED = []


def hold(eng, sem, value):
    eng.wait_ge(sem, value)
    if eng.engine == mybir.EngineType.SP:
        eng.sem_inc(PASSED[0], 1)


def settle(dve):
    dve.sem_inc(PASSED[1], 1)


def ready(eng, sems, c, each=1):
    hold(eng, sems[c.k], (c.half + 1) * each)


def free(eng, sems, c, each=1):
    if not (isinstance(c.half, int) and c.half == 0):
        hold(eng, sems[c.k], c.half * each)


def each_chunk(eng, chunks, step):
    pairs = chunks // 2
    step(at(0, 0))
    step(at(0, 1))
    with eng.Fori(1, pairs) as i:
        step(at(i, 0))
        step(at(i, 1))
    if chunks % 2:
        step(at(pairs, 0))


def leading(eng, chunks, first, second):
    pairs = chunks // 2
    first(at(0, 0))
    for k in range(2):
        first(at(0, k + 1))
        second(at(0, k))
    with eng.Fori(1, pairs) as i:
        for k in range(2):
            first(at(i, k + 1))
            second(at(i, k))
    second(at(pairs, 0))


def streamed(eng, chunks, loads, early, late):
    pairs = chunks // 2
    loads(at(0, 0))
    for k in range(3):
        loads(at(0, k + 1))
        early(at(0, k))
    with eng.Fori(2, pairs) as i:
        for k in range(2):
            loads(at(i, k))
            early(at(i, k - 1))
            late(at(i - 2, k))
    loads(at(pairs, 0))
    early(at(pairs, -1))
    late(at(pairs - 2, 0))
    early(at(pairs, 0))
    for k in range(1, 5):
        late(at(pairs - 2, k))


def trailing(eng, chunks, first, second, third):
    pairs = chunks // 2
    first(at(0, 0))
    first(at(0, 1))
    second(at(0, 0))
    for k in range(1, 4):
        first(at(0, k + 1))
        second(at(0, k))
        third(at(0, k - 1))
    with eng.Fori(2, pairs) as i:
        for k in range(2):
            first(at(i, k + 1))
            second(at(i, k))
            third(at(i, k - 1))
    second(at(pairs, 0))
    third(at(pairs, -1))
    third(at(pairs, 0))


class Steps:

    def __init__(self, eng, sem):
        self.eng, self.sem, self.n, self.before = eng, sem, 0, 0

    def mark(self, ins):
        self.n += 1
        return ins.then_inc(self.sem, 1)

    def wait(self):
        self.eng.wait_ge(self.sem, self.before + self.n)

    def link(self, ins):
        self.mark(ins)
        self.wait()

    def repeat(self, i, first, per):
        self.before = (i - first) * per

    def repeated(self, trips, per):
        self.before = 0
        self.n += (trips - 1) * per


def skewed(dve, st, chunks, front, middle, back, finish, lag=1):
    pairs = chunks // 2
    assert chunks == 2 * pairs + 1 and 1 <= lag <= 3

    def all_parts(half, k):
        front(at(half, k + 1))
        middle(at(half, k))
        back(at(half, k + 1))
        if not (isinstance(half, int) and 2 * half + k < lag):
            finish(at(half, k - lag))
    front(at(0, 0))
    back(at(0, 0))
    all_parts(0, 0)
    all_parts(0, 1)
    n = st.n
    all_parts(1, 0)
    all_parts(1, 1)
    per = st.n - n
    with dve.Fori(2, pairs) as i:
        st.repeat(i, 2, per)
        all_parts(i, 0)
        all_parts(i, 1)
    st.repeated(pairs - 2, per)
    middle(at(pairs, 0))
    for k in range(lag, -1, -1):
        finish(at(pairs, -k))


def build(nc, A, out):
    N = A["x"].shape[0]
    E = A["src"].shape[0]
    STEPS = -(-E // (P * T)) * T
    CH = STEPS // T
    EP = P * STEPS
    TN = 2 * T
    NODES = P * TN
    REST = (N - (CH - 1) * NODES) // TN
    assert 0 < N - (CH - 1) * NODES <= NODES and (N - (CH - 1) * NODES) % TN == 0 and CH % 2 == 1

    def dram(name, shape, dt=F32):
        return nc.dram_tensor(name, shape, dt).ap()

    dst_pad = dram("dst_pad", (EP + 2,), I32)
    idx_src = dram("idx_src", (P, STEPS), I32)
    idx_dst = dram("idx_dst", (P, STEPS), I32)
    idx_last = dram("idx_last", (P, STEPS), I32)
    idx_out = dram("idx_out", (P, STEPS), I32)
    info_src = dram("info_src", (P, STEPS, 2), I32)
    types_t = dram("types_t", (STEPS, P), BF16)
    node_info = dram("node_info", (N, 2), I32)
    x_info = dram("x_info", (N, D + 2))
    z_nodes = dram("z_nodes", (CH, P, TN * D))

    def table(name):
        return dram(name, (EP + 1, D))

    def rows(t):
        return t[0:EP, :].rearrange("(p t) d -> p t d", p=P)

    sum0a, sum0b, raw1, act1, sum2a, sum2b, fin = [
        table(n) for n in ("sum0a", "sum0b", "raw1", "act1", "sum2a", "sum2b", "fin")]
    xs, xd, x1s, x1d, msg, x2s, x2d, zs, zd, p3s, p3d, hs3, x3d = [
        dram(n, (EP, D)) for n in ("xs", "xd", "x1s", "x1d", "msg", "x2s", "x2d", "zs", "zd", "p3s", "p3d", "hs3", "x3d")]

    top = ExitStack()
    with top:
        def sb(name, shape, dt=F32, ctx=top):
            return ctx.enter_context(nc.sbuf_tensor(name, shape, dt))

        def ps(name, shape, ctx, dt=F32):
            return ctx.enter_context(nc.psum_tensor(name, shape, dt))

        in_phase = {}

        def sem(name, ctx):
            if ctx is top:
                return ctx.enter_context(nc.semaphore(name))
            if id(ctx) not in in_phase:
                in_phase[id(ctx)] = []
                ctx.callback(clear, ctx)
            in_phase[id(ctx)].append(nc.alloc_semaphore(name))
            return in_phase[id(ctx)][-1]

        def clear(ctx):
            nc.clear_and_free_semaphores(in_phase.pop(id(ctx)))
            nc.all_engine_barrier()

        def sems(name, ctx):
            return [sem(f"{name}{k}", ctx) for k in range(2)]

        PASSED[:] = [sem("sp_passed", top), sem("dve_passed", top)]

        slots = sb("slots", [P, CH, SLOTS, T])
        ident = sb("ident", [P, P])
        row = sb("row", [P, 17, D])
        wblock = sb("wblock", [P, 5, P])
        W1_L0, W2_L0, ROOT1, ROOT2, WQ = range(5)
        wrel = sb("wrel", [P, 3, REL // 2, D])
        wkey = sb("wkey", [D + REL, D])
        wrule = sb("wrule", [P, 2 * RULES])
        brule = sb("brule", [P, RULES])
        watt = sb("watt", [P, D])
        relid = sb("relid", [P, REL // 2])
        relrow = sb("relrow", [P, 1])
        eps = sb("eps", [P, 1])
        one_col = sb("one_col", [P, 1])
        ones = sb("ones", [1, P], BF16)
        row_parts = sb("row_parts", [1, 2, 3, D], BF16)
        row_rest = sb("row_rest", [1, D])
        lead_idx = sb("lead_idx", [P, 1], I32)
        seed_idx = sb("seed_idx", [P, 1], I32)
        lead_has = sb("lead_has", [P, 1])
        bk_rows = sb("bk_rows", [D + REL, D])
        rid_lane = sb("rid_lane", [P, 1], I32)
        lead_out = sb("lead_out", [P, 1], I32)
        prefix = sb("prefix", [P, STEPS])
        suffix = sb("suffix", [P, STEPS])
        same_prev = sb("same_prev", [P, STEPS])
        same_next = sb("same_next", [P, STEPS])
        join_prev = sb("join_prev", [P, P])
        join_next = sb("join_next", [P, P])
        pass_prev = sb("pass_prev", [P, P])
        pass_next = sb("pass_next", [P, P])
        scores = sb("scores", [P, STEPS, RULES])
        turn = sb("turn", [P, P])
        chain = sb("chain", [P, P])
        chain_in = sb("chain_in", [P, P])
        tail = sb("tail", [P, D])
        carried = sb("carried", [P, D])
        lead = sb("lead", [P, D])
        seed = sb("seed", [P, D])
        seed2 = sb("seed2", [P, D])
        node_stats = sb("node_stats", [P, 2 * CH, 6])
        bn_sums = sb("bn_sums", [P, 2, 2 * D])
        bn_col = sb("bn_col", [P, 2])

        def cut_row(dve, st, which, of):
            st.link(dve.tensor_copy(row_rest[:, :], row[0:1, of, :]))
            for part in range(3):
                st.link(dve.tensor_copy(row_parts[:, which, part, :], row_rest[:, :]))
                if part < 2:
                    st.link(dve.tensor_tensor(row_rest[:, :], row_rest[:, :], row_parts[:, which, part, :],
                                              ALU.subtract))

        def add_row(to, which):
            for part in range(3):
                last = nc.tensor.matmul(to.rearrange("p (t d) -> p t d", d=D), ones[:, :],
                                        row_parts[:, which, part, None, :].broadcast_to([1, T, D]),
                                        start=False, stop=part == 2, skip_group_check=True)
            return last

        def bc(v, n):
            return v[:, :, None].broadcast_to([P, n, D])

        def rb(which, n):
            return row[:, which, None, :].broadcast_to([P, n, D])

        def slot(which):
            return slots[:, :, which, :]

        def flat(v):
            return v.rearrange("p (c t) -> p c t", t=T)

        class Turner:

            def __init__(self, dve, st, asked, turned, result):
                self.dve, self.st, self.asked, self.turned, self.result, self.n = dve, st, asked, turned, result, 0

            def __call__(self):
                self.st.wait()
                self.dve.sem_inc(self.asked, 1)
                self.n += 1
                self.dve.wait_ge(self.turned, self.n)
                return self.result

        def turn_all(pe, asked, turned, result, n):
            for j in range(n):
                pe.wait_ge(asked, j + 1)
                nc.tensor.transpose(result[:, 0:P], turn[:, :], ident[:, :]).then_inc(turned, 1)

        def carry_sum(dve, st, turner, columns, result, backward=False):
            n = columns.shape[-1]
            join, passed = (join_next, pass_next) if backward else (join_prev, pass_prev)
            st.link(dve.tensor_copy(turn[:, 0:n], columns))
            t = turner()
            a, b = (slice(0, P - 1), slice(1, P)) if backward else (slice(1, P), slice(0, P - 1))
            st.link(dve.tensor_tensor(chain_in[:, a], join[:, a], t[:, b], ALU.mult))
            edge = slice(P - 1, P) if backward else slice(0, 1)
            st.link(dve.memset(chain_in[:, edge], 0.0))
            if backward:
                st.link(dve.tensor_tensor_scan(turn[:, ::-1], passed[:, ::-1], chain_in[:, ::-1], 0.0,
                                               ALU.mult, ALU.add))
            else:
                st.link(dve.tensor_tensor_scan(turn[:, :], passed[:, :], chain_in[:, :], 0.0,
                                               ALU.mult, ALU.add))
            t = turner()
            st.link(dve.tensor_copy(result, t[:, 0:n]))

        def carry_max(dve, st, turner, columns, result, backward=False):
            n = columns.shape[-1]
            join, passed = (join_next, pass_next) if backward else (join_prev, pass_prev)
            st.link(dve.tensor_copy(turn[:, 0:n], columns))
            t = turner()
            a, b = (slice(0, P - 1), slice(1, P)) if backward else (slice(1, P), slice(0, P - 1))
            st.link(dve.tensor_scalar(chain[:, :], join[:, :], 1.0, HUGE, ALU.subtract, ALU.mult))
            st.link(dve.memset(chain_in[:, :], -HUGE))
            st.link(dve.tensor_tensor(chain_in[:, a], chain[:, a], t[:, b], ALU.add))
            st.link(dve.tensor_scalar(chain[:, :], passed[:, :], 1.0, HUGE, ALU.subtract, ALU.mult))
            if backward:
                st.link(dve.tensor_tensor_scan(turn[:, ::-1], chain[:, ::-1], chain_in[:, ::-1], -HUGE,
                                               ALU.add, ALU.max))
            else:
                st.link(dve.tensor_tensor_scan(turn[:, :], chain[:, :], chain_in[:, :], -HUGE,
                                               ALU.add, ALU.max))
            t = turner()
            st.link(dve.tensor_copy(result, t[:, 0:n]))

        def clear_turn(dve, st):
            st.link(dve.memset(turn[:, :], 0.0))

        def edge_structure():
            ctx = ExitStack()
            with ctx:
                H = 1 + REL
                dst_i = sb("dst_i", [P, STEPS], I32, ctx)
                src_i = sb("src_i", [P, STEPS], I32, ctx)
                type_i = sb("type_i", [P, STEPS], I32, ctx)
                prev_i = sb("prev_i", [P, STEPS], I32, ctx)
                next_i = sb("next_i", [P, STEPS], I32, ctx)
                dst_f = sb("dst_f", [P, STEPS], F32, ctx)
                type_f = sb("type_f", [P, STEPS + P], F32, ctx)
                other = sb("other", [P, STEPS], F32, ctx)
                edge_no = sb("edge_no", [P, STEPS], F32, ctx)
                last = sb("last", [P, STEPS], F32, ctx)
                one = sb("one", [P, STEPS], F32, ctx)
                val = sb("val", [P, H, STEPS], F32, ctx)
                fwd = sb("fwd", [P, H, STEPS], F32, ctx)
                bwd = sb("bwd", [P, H, STEPS], F32, ctx)
                cf = sb("cf", [P, H], F32, ctx)
                cb = sb("cb", [P, H], F32, ctx)
                ends = sb("ends", [P, H], F32, ctx)
                tmp = sb("tmp", [P, STEPS], F32, ctx)
                tot = sb("tot", [P, STEPS], F32, ctx)
                weight = sb("weight", [P, STEPS], F32, ctx)
                root = sb("root", [P, STEPS], F32, ctx)
                idx_i = sb("idx_i", [P, STEPS], I32, ctx)
                idx_j = sb("idx_j", [P, STEPS], I32, ctx)
                types_b = sb("types_b", [P, 4, P], BF16, ctx)
                marks = sb("marks", [1, 2], I32, ctx)
                info = sb("info", [80, N // 80, 2], I32, ctx)
                info_rows = sb("info_rows", [P, STEPS, 2], I32, ctx)
                info_f = info_rows[:, :, :].bitcast(F32)
                out_idx = sb("out_idx", [P, STEPS], I32, ctx)
                zero = sb("zero", [1, D], F32, ctx)
                turned_ps = ps("turned_ps", [P, 512], ctx)
                step = sem("es_step", ctx)
                blank = sem("es_blank", ctx)
                loaded = sem("es_loaded", ctx)
                padded = sem("es_padded", ctx)
                shifted = sem("es_shifted", ctx)
                asked = sem("es_asked", ctx)
                turned = sem("es_turned", ctx)
                made = sem("es_made", ctx)
                deg = sem("es_deg", ctx)
                rooted = sem("es_rooted", ctx)
                types_ready = sem("es_types", ctx)
                idx_ready = sem("es_idx", ctx)
                stored = sem("es_stored", ctx)
                listed = sem("es_listed", ctx)
                info_set = sem("es_info", ctx)
                full = E // STEPS
                part = E - full * STEPS
                wide = full // 16 * 16
                block = ctx.enter_context(nc.Block())

                @block.sync
                def _(sp):
                    sp.wait_ge(blank, 7)
                    for dram_v, tile in ((A["dst"], dst_i), (A["src"], src_i), (A["edge_type_8"], type_i)):
                        v = dram_v[0:full * STEPS].rearrange("(p t) -> p t", t=STEPS)
                        sp.dma_start(tile[0:wide, :], v[0:wide, :]).then_inc(loaded, 16)
                        sp.dma_start(tile[wide:full, :], v[wide:full, :]).then_inc(loaded, 16)
                        sp.dma_start(tile[full:full + 1, 0:part],
                                     dram_v[full * STEPS:E].rearrange("(p t) -> p t", p=1)).then_inc(loaded, 16)
                    sp.dma_start(node_info.rearrange("(p r) c -> p r c", p=80), info[:, :, :]).then_inc(info_set, 16)
                    sp.wait_ge(loaded, 144)
                    sp.dma_start(dst_pad[1:EP + 1].rearrange("(p t) -> p t", p=P), dst_i[:, :]).then_inc(padded, 16)
                    sp.dma_start(dst_pad[0:1].rearrange("(p t) -> p t", p=1), marks[:, 0:1]).then_inc(padded, 16)
                    sp.dma_start(dst_pad[EP + 1:EP + 2].rearrange("(p t) -> p t", p=1),
                                 marks[:, 1:2]).then_inc(padded, 16)
                    sp.dma_start(idx_src, src_i[:, :]).then_inc(stored, 16)
                    for t in (sum0a, raw1, sum2a, fin):
                        sp.dma_start(t[EP:EP + 1, :], zero[:, :]).then_inc(stored, 16)
                    sp.wait_ge(padded, 48)
                    sp.dma_start(prev_i[:, :], dst_pad[0:EP].rearrange("(p t) -> p t", p=P)).then_inc(shifted, 16)
                    sp.dma_start(next_i[:, :], dst_pad[2:EP + 2].rearrange("(p t) -> p t", p=P)).then_inc(shifted, 16)
                    sp.wait_ge(types_ready, 4)
                    for j in range(4):
                        n = min(P, STEPS - j * P)
                        sp.dma_start(types_t[j * P:j * P + n, :], types_b[0:n, j, :]).then_inc(stored, 16)
                    sp.wait_ge(idx_ready, 1)
                    sp.dma_start(idx_dst, idx_j[:, :]).then_inc(stored, 16)
                    sp.wait_ge(listed, 1)
                    sp.dma_start(idx_out, out_idx[:, :]).then_inc(stored, 16)
                    sp.dma_start(info_src, info_rows[:, :, :]).then_inc(stored, 16)
                    sp.wait_ge(stored, 16 * 12)
                    sp.wait_ge(info_set, 16)

                @block.gpsimd
                def _(pool):
                    pool.memset(ident[:, :], 0.0).then_inc(made, 1)
                    pool.wait_ge(made, 1)
                    pool.affine_select(out=ident[:, :], in_=ident[:, :], compare_op=ALU.not_equal, fill=1.0,
                                       base=0, pattern=[[-1, P]], channel_multiplier=1).then_inc(made, 1)
                    pool.iota(idx_i[:, :], pattern=[[1, STEPS]], base=0, channel_multiplier=STEPS).then_inc(made, 1)

                @block.scalar
                def _(act):
                    act.wait_ge(deg, 1)
                    nc.scalar.activation(root[:, :], tot[:, :], ACT.Sqrt).then_inc(rooted, 1)

                @block.tensor
                def _(pe):
                    pe.wait_ge(made, 2)
                    turn_all(pe, asked, turned, turned_ps, 12)

                @block.vector
                def _(dve):
                    st = Steps(dve, step)
                    turner = Turner(dve, st, asked, turned, turned_ps)
                    dve.memset(dst_i[:, :], N).then_inc(blank, 1)
                    dve.memset(src_i[:, :], 0).then_inc(blank, 1)
                    dve.memset(type_i[:, :], 0).then_inc(blank, 1)
                    dve.memset(info[:, :, 0], EP).then_inc(blank, 1)
                    dve.memset(info[:, :, 1], 0).then_inc(blank, 1)
                    dve.memset(zero[:, :], 0.0).then_inc(blank, 1)
                    dve.memset(marks[:, :], -1).then_inc(blank, 1)
                    st.mark(dve.memset(slots[:, :, :, :], 0.0))
                    st.mark(dve.memset(one[:, :], 1.0))
                    st.mark(dve.memset(eps[:, :], EPS))
                    st.mark(dve.memset(type_f[:, STEPS:STEPS + P], 0.0))
                    for rr in range(REL // 2):
                        st.mark(dve.memset(relid[0:D, rr:rr + 1], 2.0 * rr))
                        st.mark(dve.memset(relid[D:P, rr:rr + 1], 2.0 * rr + 1.0))
                    dve.wait_ge(loaded, 144)
                    st.mark(dve.tensor_copy(dst_f[:, :], dst_i[:, :]))
                    st.link(dve.tensor_copy(type_f[:, 0:STEPS], type_i[:, :]))
                    dve.tensor_scalar(idx_j[:, :], dst_f[:, :], float(N - 1), None, ALU.min).then_inc(idx_ready, 1)
                    for j in range(4):
                        st.link(dve.tensor_copy(turn[:, :], type_f[:, j * P:(j + 1) * P]))
                        turner()
                        dve.tensor_copy(types_b[:, j, :], turned_ps[:, 0:P]).then_inc(types_ready, 1)
                        dve.wait_ge(types_ready, j + 1)
                    dve.wait_ge(shifted, 32)
                    st.link(dve.tensor_copy(other[:, :], prev_i[:, :]))
                    st.link(dve.tensor_tensor(same_prev[:, :], dst_f[:, :], other[:, :], ALU.is_equal))
                    st.link(dve.tensor_copy(other[:, :], next_i[:, :]))
                    st.link(dve.tensor_tensor(same_next[:, :], dst_f[:, :], other[:, :], ALU.is_equal))
                    st.link(dve.tensor_scalar(last[:, :], same_next[:, :], -1.0, 1.0, ALU.mult, ALU.add))
                    st.link(dve.scalar_tensor_tensor(last[:, :], dst_f[:, :], float(N), last[:, :],
                                                     ALU.is_lt, ALU.mult))
                    st.link(dve.tensor_tensor_scan(prefix[:, :], same_prev[:, :], one[:, :], 1.0, ALU.mult, ALU.mult))
                    st.link(dve.tensor_tensor_scan(suffix[:, ::-1], same_next[:, ::-1], one[:, ::-1], 1.0,
                                                   ALU.mult, ALU.mult))
                    for v, to in ((same_prev[:, 0:1], join_prev), (prefix[:, STEPS - 1:STEPS], pass_prev),
                                  (same_next[:, STEPS - 1:STEPS], join_next), (suffix[:, 0:1], pass_next)):
                        st.link(dve.tensor_copy(turn[:, :], v.broadcast_to([P, P])))
                        t = turner()
                        st.link(dve.tensor_copy(to[:, :], t[:, 0:P]))
                    st.link(dve.tensor_copy(chain[:, :], pass_prev[:, :]))
                    st.link(dve.tensor_tensor(pass_prev[:, 1:P], join_prev[:, 1:P], chain[:, 0:P - 1], ALU.mult))
                    st.link(dve.memset(pass_prev[:, 0:1], 0.0))
                    st.link(dve.tensor_copy(chain[:, :], pass_next[:, :]))
                    st.link(dve.tensor_tensor(pass_next[:, 0:P - 1], join_next[:, 0:P - 1], chain[:, 1:P], ALU.mult))
                    st.link(dve.memset(pass_next[:, P - 1:P], 0.0))
                    st.mark(dve.memset(val[:, 0, :], 1.0))
                    for r in range(REL):
                        st.mark(dve.tensor_scalar(val[:, 1 + r, :], type_f[:, 0:STEPS], float(r), None, ALU.is_equal))
                    st.wait()
                    for h in range(H):
                        st.mark(dve.tensor_tensor_scan(fwd[:, h, :], same_prev[:, :], val[:, h, :], 0.0,
                                                       ALU.mult, ALU.add))
                        st.mark(dve.tensor_tensor_scan(bwd[:, h, ::-1], same_next[:, ::-1], val[:, h, ::-1], 0.0,
                                                       ALU.mult, ALU.add))
                    st.wait()
                    clear_turn(dve, st)
                    st.link(dve.tensor_copy(ends[:, :], fwd[:, :, STEPS - 1]))
                    carry_sum(dve, st, turner, ends[:, :], cf[:, :])
                    clear_turn(dve, st)
                    st.link(dve.tensor_copy(ends[:, :], bwd[:, :, 0]))
                    carry_sum(dve, st, turner, ends[:, :], cb[:, :], backward=True)

                    def total(h):
                        st.link(dve.tensor_tensor(tot[:, :], fwd[:, h, :], bwd[:, h, :], ALU.add))
                        st.link(dve.tensor_tensor(tot[:, :], tot[:, :], val[:, h, :], ALU.subtract))
                        st.link(dve.scalar_tensor_tensor(tot[:, :], prefix[:, :], cf[:, h:h + 1], tot[:, :],
                                                         ALU.mult, ALU.add))
                        st.link(dve.scalar_tensor_tensor(tot[:, :], suffix[:, :], cb[:, h:h + 1], tot[:, :],
                                                         ALU.mult, ALU.add))

                    for h in range(1, H):
                        total(h)
                        if h == 1:
                            st.link(dve.tensor_tensor(weight[:, :], tot[:, :], val[:, h, :], ALU.mult))
                        else:
                            st.link(dve.tensor_tensor(tot[:, :], tot[:, :], val[:, h, :], ALU.mult))
                            st.link(dve.tensor_tensor(weight[:, :], weight[:, :], tot[:, :], ALU.add))
                    st.link(dve.reciprocal(tmp[:, :], weight[:, :]))
                    st.link(dve.tensor_copy(slot(REL_WEIGHT), flat(tmp[:, :])))
                    total(0)
                    dve.sem_inc(deg, 1)
                    dve.wait_ge(rooted, 1)
                    st.link(dve.reciprocal(tmp[:, :], root[:, :]))
                    st.link(dve.tensor_copy(slot(DINV_DST), flat(tmp[:, :])))
                    st.mark(dve.tensor_copy(info_f[:, :, 1], tmp[:, :]))
                    st.mark(dve.tensor_copy(slot(SAME_PREV), flat(same_prev[:, :])))
                    st.mark(dve.tensor_copy(slot(SAME_NEXT), flat(same_next[:, :])))
                    st.mark(dve.tensor_copy(slot(LAST), flat(last[:, :])))
                    dve.wait_ge(made, 3)
                    st.mark(dve.tensor_copy(info_rows[:, :, 0], idx_i[:, :]))
                    st.link(dve.tensor_copy(edge_no[:, :], idx_i[:, :]))
                    def where(result, value, present):
                        st.link(dve.tensor_tensor(tmp[:, :], value, present, ALU.mult))
                        st.link(dve.tensor_scalar(other[:, :], present, -OUT_OF_RANGE, OUT_OF_RANGE,
                                                  ALU.mult, ALU.add))
                        st.link(dve.tensor_tensor(result, tmp[:, :], other[:, :], ALU.add))
                    where(out_idx[:, :], dst_f[:, :], last[:, :])
                    dve.sem_inc(listed, 1)
                    st.link(dve.tensor_tensor(tot[:, :], prefix[:, :], last[:, :], ALU.mult))
                    st.link(dve.tensor_tensor(weight[:, :], last[:, :], tot[:, :], ALU.subtract))
                    st.mark(dve.tensor_copy(slot(COUNTED), flat(weight[:, :])))
                    st.link(dve.reduce_sum(lead_has[:, :], tot[:, :], AX.X))
                    for value, result in ((edge_no, lead_idx), (dst_f, lead_out)):
                        st.link(dve.tensor_tensor(weight[:, :], value[:, :], tot[:, :], ALU.mult))
                        st.link(dve.reduce_sum(ends[:, 0:1], weight[:, :], AX.X))
                        st.link(dve.tensor_scalar(ends[:, 1:2], lead_has[:, :], -OUT_OF_RANGE, OUT_OF_RANGE,
                                                  ALU.mult, ALU.add))
                        st.link(dve.tensor_tensor(result[:, :], ends[:, 0:1], ends[:, 1:2], ALU.add))
                    st.link(dve.tensor_tensor(ends[:, 0:1], cb[:, 0:1], suffix[:, STEPS - 1:STEPS], ALU.mult))
                    st.link(dve.tensor_tensor(seed_idx[:, :], ends[:, 0:1], edge_no[:, STEPS - 1:STEPS], ALU.add))
                    st.wait()
                return

        def gather(pool, tile, dram_t, idx):
            return pool.indirect_dma_start(out=tile, out_offset=None, in_=dram_t,
                                           in_offset=bass.IndirectOffsetOnAxis(ap=idx, axis=0))

        def gather_valid(pool, tile, dram_t, idx):
            return pool.indirect_dma_start(out=tile, out_offset=None, in_=dram_t,
                                           in_offset=bass.IndirectOffsetOnAxis(ap=idx, axis=0),
                                           bounds_check=dram_t.shape[0] - 1, oob_is_err=False)

        def scatter_valid(pool, dram_t, idx, tile):
            return pool.indirect_dma_start(out=dram_t, out_offset=bass.IndirectOffsetOnAxis(ap=idx, axis=0),
                                           in_=tile, in_offset=None,
                                           bounds_check=dram_t.shape[0] - 1, oob_is_err=False)

        def take_rows(pool, idx, idx_all, taken, done, c, cols):
            free(pool, done, c, 16 * T)
            pool.tensor_copy(idx[c.k][:, :], cols(idx_all, c)).then_inc(taken[c.k], 1)
            ready(pool, taken, c)

        def edge_cols(v, c):
            return v[:, bass.ds(c.index * T, T)]

        def node_links():
            ctx = ExitStack()
            with ctx:
                idx = [sb(f"nl_idx{k}", [P, T], I32, ctx) for k in range(2)]
                rows_in = [sb(f"nl_rows{k}", [P, T, 2], I32, ctx) for k in range(2)]
                wk2 = sb("wk2", [P, D], F32, ctx)
                wk3 = sb("wk3", [D, D], F32, ctx)
                wq = sb("wq", [D, D], F32, ctx)
                wmean = sb("wmean", [P, REL // 2], F32, ctx)
                wsel = sb("wsel", [P, D + REL], F32, ctx)
                hrule = sb("hrule", [P, D], F32, ctx)
                hrule_t = sb("hrule_t", [D, RULES], F32, ctx)
                krule = sb("krule", [D, RULES], F32, ctx)
                wq_t = sb("wq_t", [D, D], F32, ctx)
                bq_col = sb("bq_col", [D, 1], F32, ctx)
                bq_all = sb("bq_all", [D, P], F32, ctx)
                wa = sb("wa", [P, P], F32, ctx)
                rid = sb("rid", [RULES, 1], I32, ctx)
                xc = sb("nl_xc", [P, D], F32, ctx)
                sq = sb("nl_sq", [P, D], F32, ctx)
                stat = sb("nl_stat", [P, 4], F32, ctx)
                lane = sb("nl_lane", [P, 1], F32, ctx)
                t_ps = ps("nl_t_ps", [P, 512], ctx)
                m_ps = ps("nl_m_ps", [P, 512], ctx)
                step = sem("nl_step", ctx)
                loaded = sems("nl_loaded", ctx)
                scattered = sems("nl_scattered", ctx)
                begun = sem("nl_begun", ctx)
                zeroed = sem("nl_zeroed", ctx)
                weights = sem("nl_weights", ctx)
                ruled = sem("nl_ruled", ctx)
                rid_in = sem("nl_rid", ctx)
                asked = sem("nl_asked", ctx)
                turned = sem("nl_turned", ctx)
                mm_ask = sem("nl_mm_ask", ctx)
                mm_done = sem("nl_mm_done", ctx)
                numbered = sem("nl_numbered", ctx)
                centred = sem("nl_centred", ctx)
                squared = sem("nl_squared", ctx)
                summed = sem("nl_summed", ctx)
                rooted = sem("nl_rooted", ctx)
                act_done = sem("nl_act_done", ctx)
                stored = sem("nl_stored", ctx)
                block = ctx.enter_context(nc.Block())

                @block.sync
                def _(sp):
                    def load(c):
                        free(sp, scattered, c, 16 * T)
                        sp.dma_start(idx[c.k][:, :], edge_cols(idx_out, c)).then_inc(loaded[c.k], 16)
                        sp.dma_start(rows_in[c.k][:, :, :], edge_cols(info_src, c)).then_inc(loaded[c.k], 16)
                    each_chunk(sp, CH, load)
                    sp.wait_ge(act_done, 1)
                    sp.dma_start(act1[EP:EP + 1, :], row[0:1, INACTIVE_L1, :]).then_inc(stored, 16)
                    sp.dma_start(sum0b[EP:EP + 1, :], row[0:1, B2_L0, :]).then_inc(stored, 16)
                    sp.dma_start(sum2b[EP:EP + 1, :], row[0:1, B2_L2, :]).then_inc(stored, 16)
                    sp.wait_ge(stored, 48)

                @block.gpsimd
                def _(pool):
                    pool.iota(rid_lane[:, :], pattern=[[1, 1]], base=0, channel_multiplier=1).then_inc(numbered, 1)
                    pool.wait_ge(rid_in, 16)
                    pool.wait_ge(zeroed, 1)
                    pool.sem_inc(begun, 1)
                    gather(pool, hrule[0:RULES, :], A["L1_gnn_rule_emb"], rid[:, :]).then_inc(ruled, 16)

                    def scatter(c):
                        ready(pool, loaded, c, 32)
                        pool.sem_inc(begun, 1)
                        for t in range(T):
                            scatter_valid(pool, node_info, idx[c.k][:, t:t + 1],
                                          rows_in[c.k][:, t, :]).then_inc(scattered[c.k], 16)
                    each_chunk(pool, CH, scatter)
                    for k in range(2):
                        pool.wait_ge(scattered[k], 16 * T * (CH // 2 + (1 - k) * (CH % 2)))

                @block.scalar
                def _(act):
                    act.wait_ge(zeroed, 1)
                    n = 0
                    loads = []
                    for j, name in enumerate(("L0_gnn_W1", "L0_gnn_W2", "L2_gnn_root1", "L2_gnn_root2", "L1_gnn_Wq_w")):
                        for h in range(2):
                            loads.append((wblock[h * D:(h + 1) * D, j, h * D:(h + 1) * D], A[name]))
                    for j, name in enumerate(("L1_gnn_W_r", "L2_gnn_w1", "L2_gnn_w2")):
                        loads.append((wrel[:, j, :, :], A[name].rearrange("(a b) i o -> (b i) a o", b=2)))
                    loads += [(wkey[0:D, :], A["L1_gnn_Wk_w"][0:D, :]),
                              (wk2[0:D, :], A["L1_gnn_Wk_w"][D:2 * D, :]),
                              (wk2[D:P, :], A["L1_gnn_Wk_w"][D:2 * D, :]),
                              (wk3[:, :], A["L1_gnn_Wk_w"][2 * D:3 * D, :]),
                              (wq[:, :], A["L1_gnn_Wq_w"]),
                              (wa[0:D, :], A["L3_gnn_W_attn"]),
                              (bq_col[:, :], A["L1_gnn_Wq_bias"].rearrange("(d o) -> d o", o=1))]
                    for j, name in ((B1_L0, "L0_gnn_b1"), (B2_L0, "L0_gnn_b2"), (BQ, "L1_gnn_Wq_bias"),
                                    (BIAS_L1, "L1_gnn_bias"), (LN_G, "L1_gnn_ln_g"), (LN_B, "L1_gnn_ln_b"),
                                    (B1_L2, "L2_gnn_b1"), (GAMMA, "L2_gnn_gamma1"), (BETA, "L2_gnn_beta1"),
                                    (B2_L2, "L2_gnn_b2"), (B_ATT, "L3_gnn_b_attn"), (W_OUT, "L3_gnn_w_out")):
                        loads.append((row[:, j, :], A[name].rearrange("(o d) -> o d", o=1).broadcast_to([P, D])))
                    loads.append((bk_rows[D:D + REL, :], A["L1_gnn_Wk_bias"].rearrange("(o d) -> o d", o=1).broadcast_to([REL, D])))
                    act.dma_start(rid[:, :], A["L1_gnn_rule_ids"].rearrange("(r o) -> r o", o=1)).then_inc(rid_in, 16)
                    for to, of in loads:
                        act.dma_start(to, of).then_inc(weights, 16)
                        n += 16
                    assert n == WEIGHTS
                    act.wait_ge(centred, 1)
                    nc.scalar.activation(sq[:, :], xc[:, :], ACT.Square).then_inc(squared, 1)
                    act.wait_ge(summed, 1)
                    nc.scalar.activation(stat[:, 2:3], stat[:, 1:2], ACT.Sqrt, bias=eps[:, :],
                                         scale=1.0 / D).then_inc(rooted, 1)

                @block.tensor
                def _(pe):
                    pe.wait_ge(mm_ask, 1)
                    nc.tensor.matmul(m_ps[0:D + REL, 0:D], wsel[:, :], wk2[:, :], start=True, stop=True).then_inc(mm_done, 1)
                    pe.wait_ge(asked, 1)
                    nc.tensor.transpose(t_ps[:, 0:P], turn[:, :], ident[:, :]).then_inc(turned, 1)
                    pe.wait_ge(mm_ask, 2)
                    nc.tensor.matmul(m_ps[0:D, 64:64 + RULES], wk3[:, :], hrule_t[:, :],
                                     start=True, stop=True).then_inc(mm_done, 1)
                    pe.wait_ge(asked, 2)
                    nc.tensor.transpose(t_ps[:, 0:P], turn[:, :], ident[:, :]).then_inc(turned, 1)
                    pe.wait_ge(mm_ask, 3)
                    nc.tensor.matmul(m_ps[0:D, 96:96 + RULES], wq_t[:, :], krule[:, :],
                                     start=True, stop=True).then_inc(mm_done, 1)
                    nc.tensor.matmul(m_ps[:, 128:128 + RULES], bq_all[:, :], krule[:, :],
                                     start=True, stop=True).then_inc(mm_done, 1)
                    pe.wait_ge(asked, 3)
                    nc.tensor.transpose(t_ps[:, 0:P], turn[:, :], ident[:, :]).then_inc(turned, 1)

                @block.vector
                def _(dve):
                    st = Steps(dve, step)
                    turner = Turner(dve, st, asked, turned, t_ps)
                    st.mark(dve.memset(wblock[:, :, :], 0.0))
                    st.mark(dve.memset(wsel[:, :], 0.0))
                    st.mark(dve.memset(one_col[:, :], 1.0))
                    st.mark(dve.memset(wrule[:, :], 0.0))
                    st.mark(dve.memset(node_stats[:, :, :], 0.0))
                    st.link(dve.memset(turn[:, :], 0.0))
                    dve.sem_inc(zeroed, 1)
                    dve.wait_ge(numbered, 1)
                    st.link(dve.tensor_copy(lane[:, :], rid_lane[:, :]))
                    st.link(dve.tensor_scalar(lane[:, :], lane[:, :], 1.0 * D, None, ALU.subtract))
                    st.link(dve.tensor_scalar(stat[:, 0:1], lane[:, :], 4.0, -7.0, ALU.is_ge, ALU.mult))
                    st.link(dve.scalar_tensor_tensor(relrow[:, :], lane[:, :], 2.0, stat[:, 0:1], ALU.mult, ALU.add))
                    st.link(dve.tensor_scalar(relrow[:, :], relrow[:, :], -1.0, None, ALU.mult))
                    dve.wait_ge(weights, WEIGHTS)
                    st.mark(dve.memset(ones[:, :], 1.0))
                    cut_row(dve, st, ADD_B_ATT, B_ATT)
                    st.link(dve.reduce_sum(wmean[:, :], wrel[:, 0, :, :], AX.X))
                    for h in range(2):
                        st.mark(dve.tensor_scalar(wsel[h * D:(h + 1) * D, D + h * 4:D + h * 4 + 4], wmean[h * D:(h + 1) * D, :],
                                                  1.0 / D, None, ALU.mult))
                    st.wait()
                    dve.sem_inc(mm_ask, 1)
                    dve.wait_ge(mm_done, 1)
                    st.mark(dve.tensor_tensor(wkey[D:D + REL, :], m_ps[D:D + REL, 0:D], bk_rows[D:D + REL, :], ALU.add))
                    dve.wait_ge(ruled, 16)
                    st.link(dve.tensor_copy(turn[0:RULES, 0:D], hrule[0:RULES, :]))
                    t = turner()
                    st.link(dve.tensor_copy(hrule_t[:, :], t[0:D, 0:RULES]))
                    dve.sem_inc(mm_ask, 1)
                    st.mark(dve.memset(turn[:, :], 0.0))
                    st.wait()
                    st.link(dve.tensor_copy(turn[0:D, 0:D], wq[:, :]))
                    t = turner()
                    st.mark(dve.tensor_copy(wq_t[:, :], t[0:D, 0:D]))
                    st.mark(dve.tensor_copy(bq_all[:, :], bq_col[:, :].broadcast_to([D, P])))
                    dve.wait_ge(mm_done, 2)
                    st.link(dve.tensor_copy(krule[:, :], m_ps[0:D, 64:64 + RULES]))
                    dve.sem_inc(mm_ask, 1)
                    dve.wait_ge(mm_done, 4)
                    for h in range(2):
                        st.mark(dve.tensor_copy(wrule[h * D:(h + 1) * D, h * RULES:(h + 1) * RULES],
                                                m_ps[0:D, 96:96 + RULES]))
                    st.mark(dve.tensor_copy(brule[:, :], m_ps[:, 128:128 + RULES]))
                    st.link(dve.tensor_copy(turn[0:D, :], wa[0:D, :]))
                    t = turner()
                    st.mark(dve.tensor_copy(watt[:, :], t[:, 0:D]))
                    st.link(dve.reduce_sum(stat[:, 0:1], row[:, BIAS_L1, :], AX.X))
                    st.link(dve.tensor_scalar(stat[:, 0:1], stat[:, 0:1], 1.0 / D, None, ALU.mult))
                    st.link(dve.tensor_scalar(xc[:, :], row[:, BIAS_L1, :], stat[:, 0:1], None, ALU.subtract))
                    dve.sem_inc(centred, 1)
                    dve.wait_ge(squared, 1)
                    st.link(dve.reduce_sum(stat[:, 1:2], sq[:, :], AX.X))
                    dve.sem_inc(summed, 1)
                    dve.wait_ge(rooted, 1)
                    st.link(dve.reciprocal(stat[:, 3:4], stat[:, 2:3]))
                    st.link(dve.scalar_tensor_tensor(xc[:, :], xc[:, :], stat[:, 3:4], row[:, LN_G, :],
                                                     ALU.mult, ALU.mult))
                    st.link(dve.tensor_tensor(xc[:, :], xc[:, :], row[:, LN_B, :], ALU.add))
                    st.link(dve.tensor_scalar(row[:, INACTIVE_L1, :], xc[:, :], 0.0, None, ALU.max))
                    st.link(dve.tensor_tensor(row[:, INACTIVE_X2, :], row[:, INACTIVE_L1, :], row[:, B2_L0, :], ALU.add))
                    dve.sem_inc(act_done, 1)

        def centre(dve, st, x, mean, n, centred, c):
            centre_apart(dve, st, x, x, mean, n, centred, c)

        def squares(act, x, sq, centred, squared, c):
            ready(act, centred, c)
            nc.scalar.activation(sq, x, ACT.Square).then_inc(squared[c.k], 1)

        def variance(dve, sq, var, squared, summed, c):
            ready(dve, squared, c)
            dve.reduce_sum(var, sq, AX.X).then_inc(summed[c.k], 1)

        def deviation(act, var, sd, summed, rooted, c):
            ready(act, summed, c)
            nc.scalar.activation(sd, var, ACT.Sqrt, bias=eps[:, :], scale=1.0 / D).then_inc(rooted[c.k], 1)

        def nodes_first():
            ctx = ExitStack()
            with ctx:
                def two(name, shape, dt=F32):
                    return [sb(f"nf_{name}{k}", shape, dt, ctx) for k in range(2)]
                idx = two("idx", [P, T], I32)
                idx_all = sb("nf_idx_all", [P, STEPS], I32, ctx)
                rows_loaded = sem("nf_rows_loaded", ctx)
                got = two("got", [P, T, D])
                x = two("x", [P, TN, D + 2])
                info = two("info", [P, TN, 2])
                x2 = two("x2", [P, TN, D])
                sq = two("sq", [P, TN, D])
                h = two("h", [P, TN, D])
                mean = two("mean", [P, TN])
                var = two("var", [P, TN])
                sd = two("sd", [P, TN])
                scale = two("scale", [P, TN])
                ht = two("ht", [P, TN * D])
                z = two("z", [P, TN * D])
                t_ps = [ps(f"nf_t_ps{k}", [P, TN * D], ctx) for k in range(2)]
                z_ps = [ps(f"nf_z_ps{k}", [P, TN * D], ctx) for k in range(2)]
                step = sem("nf_step", ctx)
                begun = sem("nf_begun", ctx)
                blank = sem("nf_blank", ctx)
                (idx_in, gathered, got_out, x_in, x_out, merged, centred, squared, summed, rooted, h_ready,
                 h_turned, ht_ready, z_made, z_ready, z_seen, z_out) = [sems("nf_" + n, ctx) for n in (
                     "idx_in", "gathered", "got_out", "x_in", "x_out", "merged", "centred", "squared", "summed",
                     "rooted", "h_ready", "h_turned", "ht_ready", "z_made", "z_ready", "z_seen", "z_out")]
                block = ctx.enter_context(nc.Block())
                whole = (CH - 1) * NODES

                def nodes_of(v, c):
                    if isinstance(c.index, int) and c.index == CH - 1:
                        return v[whole:N, :].rearrange("(p t) d -> p t d", t=TN)
                    return v[bass.ds(c.index * NODES, NODES), :].rearrange("(p t) d -> p t d", t=TN)

                def parts(c):
                    return REST if isinstance(c.index, int) and c.index == CH - 1 else P

                @block.sync
                def _(sp):
                    sp.dma_start(idx_all[:, :], idx_dst).then_inc(rows_loaded, 16)

                    def loads(c):
                        free(sp, merged, c)
                        free(sp, x_out, c, 16)
                        n = parts(c)
                        if n < P:
                            sp.wait_ge(blank, 2)
                        sp.dma_start(x[c.k][0:n, :, 0:D], nodes_of(A["x"], c)).then_inc(x_in[c.k], 16)
                        sp.dma_start(info[c.k][0:n, :, :], nodes_of(node_info, c).bitcast(F32)).then_inc(x_in[c.k], 16)

                    def early(c):
                        ready(sp, merged, c)
                        sp.dma_start(nodes_of(x_info, c), x[c.k][0:parts(c), :, :]).then_inc(x_out[c.k], 16)
                        ready(sp, gathered, c, 16 * T)
                        sp.dma_start(edge_cols(rows(xd), c), got[c.k][:, :, :]).then_inc(got_out[c.k], 16)

                    def late(c):
                        ready(sp, z_ready, c)
                        sp.dma_start(z_nodes[bass.ds(c.index, 1)].rearrange("o p n -> (o p) n"),
                                     z[c.k][:, :]).then_inc(z_out[c.k], 16)

                    streamed(sp, CH, loads, early, late)
                    for k in range(2):
                        n = CH // 2 + (1 - k)
                        sp.wait_ge(x_out[k], 16 * n)
                        sp.wait_ge(z_out[k], 16 * n)
                        sp.wait_ge(got_out[k], 16 * n)

                @block.gpsimd
                def _(pool):
                    pool.wait_ge(rows_loaded, 16)
                    def get(c):
                        if parts(c) < P:
                            free(pool, merged, c)
                            free(pool, x_out, c, 16)
                            pool.memset(x[c.k][:, :, 0:D], 0.0).then_inc(blank, 1)
                            pool.memset(info[c.k][:, :, :], 1.0).then_inc(blank, 1)
                        take_rows(pool, idx, idx_all, idx_in, gathered, c, edge_cols)
                        free(pool, got_out, c, 16)
                        pool.sem_inc(begun, 1)
                        for t in range(T):
                            gather(pool, got[c.k][:, t, :], A["x"], idx[c.k][:, t:t + 1]).then_inc(gathered[c.k], 16)
                    each_chunk(pool, CH, get)

                @block.scalar
                def _(act):
                    def norm(c):
                        squares(act, x2[c.k][:, :, :], sq[c.k][:, :, :], centred, squared, c)
                        deviation(act, var[c.k][:, :], sd[c.k][:, :], summed, rooted, c)

                    def product(c):
                        ready(act, h_turned, c)
                        free(act, z_made, c)
                        nc.scalar.activation(ht[c.k][:, :], t_ps[c.k][:, :], ACT.Copy).then_inc(ht_ready[c.k], 1)
                        ready(act, z_made, c)
                        free(act, z_out, c, 16)
                        free(act, z_seen, c)
                        nc.scalar.activation(z[c.k][:, :], z_ps[c.k][:, :], ACT.Copy).then_inc(z_ready[c.k], 1)
                    leading(act, CH, norm, product)

                @block.tensor
                def _(pe):
                    def both(c):
                        ready(pe, h_ready, c)
                        free(pe, ht_ready, c)
                        for j in range(TN // 2):
                            last = nc.tensor.transpose(t_ps[c.k][:, j * P:(j + 1) * P],
                                                       h[c.k][:, 2 * j:2 * j + 2, :].rearrange("p t d -> p (t d)"),
                                                       ident[:, :])
                        last.then_inc(h_turned[c.k], 1)
                        ready(pe, ht_ready, c)
                        free(pe, z_ready, c)
                        for j in range(2):
                            last = nc.tensor.matmul(z_ps[c.k][:, j * 512:(j + 1) * 512], wblock[:, ROOT1, :],
                                                    ht[c.k][:, j * 512:(j + 1) * 512], start=True, stop=True)
                        last.then_inc(z_made[c.k], 1)
                    each_chunk(pe, CH, both)

                @block.vector
                def _(dve):
                    st = Steps(dve, step)

                    def front(c):
                        ready(dve, x_in, c, 32)
                        st.mark(dve.tensor_copy(x[c.k][:, :, D:D + 2].bitcast(I32), info[c.k][:, :, :].bitcast(I32)))
                        st.mark(dve.tensor_scalar(scale[c.k][:, :], info[c.k][:, :, 1], 0.0, None, ALU.is_equal))
                        st.link(dve.tensor_tensor(x2[c.k][:, :, :], x[c.k][:, :, 0:D], rb(INACTIVE_X2, TN), ALU.add))
                        dve.sem_inc(merged[c.k], 1)
                        centre(dve, st, x2[c.k][:, :, :], mean[c.k][:, :], TN, centred, c)

                    def middle(c):
                        pass

                    def back(c):
                        variance(dve, sq[c.k][:, :, :], var[c.k][:, :], squared, summed, c)
                        ready(dve, rooted, c)
                        st.link(dve.reciprocal(mean[c.k][:, :], sd[c.k][:, :]))
                        st.link(dve.tensor_tensor(scale[c.k][:, :], scale[c.k][:, :], mean[c.k][:, :], ALU.mult))
                        free(dve, h_turned, c)
                        dve.scalar_tensor_tensor(h[c.k][:, :, :], x2[c.k][:, :, :], 0.0, bc(scale[c.k][:, :], TN),
                                                 ALU.max, ALU.mult).then_inc(h_ready[c.k], 1)

                    def finish(c):
                        ready(dve, z_ready, c)
                        for j in range(2):
                            last = dve.bn_stats(node_stats[:, bass.ds(2 * c.index + j, 1), :].rearrange("p o s -> p (o s)"),
                                                z[c.k][:, j * 512:(j + 1) * 512])
                        last.then_inc(z_seen[c.k], 1)
                    skewed(dve, st, CH, front, middle, back, finish)

        def convolution(first):
            ctx = ExitStack()
            tag = "ca" if first else "cb"
            result = rows(sum0a if first else sum0b)
            with ctx:
                def two(name, shape, dt=F32):
                    return [sb(f"{tag}_{name}{k}", shape, dt, ctx) for k in range(2)]
                width = D + 2 if first else D
                idx = two("idx", [P, T], I32)
                g = two("g", [P, T, width])
                x = two("x", [P, T, D])
                sq = two("sq", [P, T, D])
                h = two("h", [P, T, D])
                mean = two("mean", [P, T])
                var = two("var", [P, T])
                sd = two("sd", [P, T])
                ptr = two("ptr", [P, T], I32)
                cur = two("cur", [P, SLOTS, T])
                fcur = sb(f"{tag}_fcur", [P, SLOTS, T], F32, ctx)
                y = two("y", [P, T, D])
                ht = two("ht", [P, T * D])
                m = two("m", [P, T, D])
                s = two("s", [P, T, D])
                t_ps = [ps(f"{tag}_t_ps{k}", [P, T * D], ctx) for k in range(2)]
                m_ps = [ps(f"{tag}_m_ps{k}", [P, T * D], ctx) for k in range(2)]
                step = sem(tag + "_step", ctx)
                begun = sem(tag + "_begun", ctx)
                (idx_in, gathered, used, split, x_out, centred, squared, summed, rooted, h_ready,
                 h_turned, ht_ready, m_made, m_ready, s_ready, s_out) = [sems(f"{tag}_{n}", ctx) for n in (
                     "idx_in", "gathered", "used", "split", "x_out", "centred", "squared", "summed",
                     "rooted", "h_ready", "h_turned", "ht_ready", "m_made", "m_ready", "s_ready", "s_out")]
                block = ctx.enter_context(nc.Block())

                @block.sync
                def _(sp):
                    def loads(c):
                        free(sp, gathered, c, 16 * T)
                        sp.dma_start(idx[c.k][:, :], edge_cols(idx_src if first else idx_last, c)).then_inc(idx_in[c.k], 16)

                    def early(c):
                        if first:
                            ready(sp, split, c)
                            sp.dma_start(edge_cols(rows(xs), c), g[c.k][:, :, 0:D]).then_inc(x_out[c.k], 16)
                            sp.dma_start(edge_cols(idx_last, c), ptr[c.k][:, :]).then_inc(x_out[c.k], 16)

                    def late(c):
                        ready(sp, s_ready, c)
                        sp.dma_start(edge_cols(result, c), (s if first else y)[c.k][:, :, :]).then_inc(s_out[c.k], 16)
                    streamed(sp, CH, loads, early, late)
                    for k in range(2):
                        n = CH // 2 + (1 - k)
                        if first:
                            sp.wait_ge(x_out[k], 32 * n)
                        sp.wait_ge(s_out[k], 16 * n)

                @block.gpsimd
                def _(pool):
                    def get(c):
                        ready(pool, idx_in, c, 16)
                        free(pool, used, c)
                        if first:
                            free(pool, x_out, c, 32)
                        pool.sem_inc(begun, 1)
                        for t in range(T):
                            gather(pool, g[c.k][:, t, :], x_info if first else sum0a,
                                   idx[c.k][:, t:t + 1]).then_inc(gathered[c.k], 16)
                    each_chunk(pool, CH, get)

                @block.scalar
                def _(act):
                    def norm(c):
                        if first:
                            squares(act, x[c.k][:, :, :], sq[c.k][:, :, :], centred, squared, c)
                            deviation(act, var[c.k][:, :], sd[c.k][:, :], summed, rooted, c)

                    def product(c):
                        ready(act, h_turned, c)
                        free(act, m_made, c)
                        nc.scalar.activation(ht[c.k][:, :], t_ps[c.k][:, :], ACT.Copy).then_inc(ht_ready[c.k], 1)
                        ready(act, m_made, c)
                        free(act, s_ready, c)
                        nc.scalar.activation(m[c.k][:, :, :], m_ps[c.k][:, :].rearrange("p (t d) -> p t d", d=D),
                                             ACT.Copy).then_inc(m_ready[c.k], 1)
                    leading(act, CH, norm, product)

                @block.tensor
                def _(pe):
                    def turn_rows(c):
                        ready(pe, h_ready, c)
                        free(pe, ht_ready, c)
                        for j in range(T // 2):
                            last = nc.tensor.transpose(t_ps[c.k][:, j * P:(j + 1) * P],
                                                       h[c.k][:, 2 * j:2 * j + 2, :].rearrange("p t d -> p (t d)"),
                                                       ident[:, :])
                        last.then_inc(h_turned[c.k], 1)

                    def product(c):
                        ready(pe, ht_ready, c)
                        free(pe, m_ready, c)
                        for j in range(T // 2):
                            last = nc.tensor.matmul(m_ps[c.k][:, j * P:(j + 1) * P], ht[c.k][:, j * P:(j + 1) * P],
                                                    wblock[:, W1_L0 if first else W2_L0, :], start=True, stop=True)
                        last.then_inc(m_made[c.k], 1)
                    leading(pe, CH, turn_rows, product)

                @block.vector
                def _(dve):
                    st = Steps(dve, step)
                    st.link(dve.memset(s[1][:, :, :], 0.0))

                    def front(c):
                        ready(dve, gathered, c, 16 * T)
                        if first:
                            free(dve, x_out, c, 32)
                            st.mark(dve.tensor_copy(ptr[c.k][:, :], g[c.k][:, :, D].bitcast(I32)))
                            st.mark(dve.tensor_copy(cur[c.k][:, DINV_SRC, :], g[c.k][:, :, D + 1]))
                            dve.tensor_copy(slots[:, bass.ds(c.index, 1), DINV_SRC, :].rearrange("p o t -> p (o t)"),
                                            g[c.k][:, :, D + 1]).then_inc(split[c.k], 1)
                            st.link(dve.tensor_copy(x[c.k][:, :, :], g[c.k][:, :, 0:D]))
                            dve.sem_inc(used[c.k], 1)
                            centre(dve, st, x[c.k][:, :, :], mean[c.k][:, :], T, centred, c)
                        else:
                            st.link(dve.tensor_copy(cur[c.k][:, :, :],
                                                    slots[:, bass.ds(c.index, 1), :, :].rearrange("p o s t -> p (o s) t")))
                            d = bc(cur[c.k][:, DINV_SRC, :], T)
                            st.link(dve.tensor_tensor(x[c.k][:, :, :], g[c.k][:, :, :], d, ALU.mult))
                            dve.sem_inc(used[c.k], 1)
                            st.link(dve.tensor_tensor(x[c.k][:, :, :], x[c.k][:, :, :], rb(B1_L0, T), ALU.add))
                            free(dve, h_turned, c)
                            dve.scalar_tensor_tensor(h[c.k][:, :, :], x[c.k][:, :, :], 0.0, d,
                                                     ALU.max, ALU.mult).then_inc(h_ready[c.k], 1)

                    def middle(c):
                        pass

                    def back(c):
                        if first:
                            variance(dve, sq[c.k][:, :, :], var[c.k][:, :], squared, summed, c)
                            ready(dve, rooted, c)
                            st.link(dve.reciprocal(mean[c.k][:, :], sd[c.k][:, :]))
                            st.link(dve.tensor_tensor(mean[c.k][:, :], mean[c.k][:, :], cur[c.k][:, DINV_SRC, :], ALU.mult))
                            free(dve, h_turned, c)
                            dve.scalar_tensor_tensor(h[c.k][:, :, :], x[c.k][:, :, :], 0.0, bc(mean[c.k][:, :], T),
                                                     ALU.max, ALU.mult).then_inc(h_ready[c.k], 1)

                    def finish(c):
                        st.link(dve.tensor_copy(fcur[:, :, :], slots[:, bass.ds(c.index, 1), :, :]
                                                .rearrange("p o s t -> p (o s) t")))
                        ready(dve, m_ready, c)
                        free(dve, s_out, c, 16)
                        sum_along(dve, st, s, m[c.k], fcur[:, SAME_PREV, :], c)
                        if not first:
                            st.link(dve.tensor_tensor(y[c.k][:, :, :], s[c.k][:, :, :], bc(fcur[:, DINV_DST, :], T),
                                                      ALU.mult))
                            st.link(dve.tensor_tensor(y[c.k][:, :, :], y[c.k][:, :, :], rb(B2_L0, T), ALU.add))
                        dve.sem_inc(s_ready[c.k], 1)
                    skewed(dve, st, CH, front, middle, back, finish)
                    st.link(dve.tensor_copy(tail[:, :], s[0][:, T - 1, :]))

        def sum_along(dve, st, s, m, same, c):
            before = s[1 - c.k][:, T - 1, :]
            for t in range(T):
                st.link(dve.scalar_tensor_tensor(s[c.k][:, t, :], before, same[:, t:t + 1], m[:, t, :],
                                                 ALU.mult, ALU.add))
                before = s[c.k][:, t, :]

        def carry(tag, raw, table=None, more=None, stats=False):
            ctx = ExitStack()
            with ctx:
                t_ps = ps(tag + "_t_ps", [P, 512], ctx)
                m_ps = ps(tag + "_m_ps", [P, 512], ctx)
                extra = sb(tag + "_extra", [P, D], F32, ctx)
                pair = sb(tag + "_pair", [P, 2 * D], F32, ctx)
                work = sb(tag + "_work", [P, 3 * D], F32, ctx)
                step = sem(tag + "_step", ctx)
                blank = sem(tag + "_blank", ctx)
                got = sem(tag + "_got", ctx)
                made = sem(tag + "_made", ctx)
                put = sem(tag + "_put", ctx)
                asked = sem(tag + "_asked", ctx)
                turned = sem(tag + "_turned", ctx)
                act_go = sem(tag + "_act_go", ctx)
                act_done = sem(tag + "_act_done", ctx)
                counted = sem(tag + "_counted", ctx)
                summed = sem(tag + "_summed", ctx)
                block = ctx.enter_context(nc.Block())

                @block.gpsimd
                def _(pool):
                    pool.wait_ge(blank, 2)
                    gather_valid(pool, lead[:, :], raw, lead_idx[:, :]).then_inc(got, 16)
                    if stats:
                        gather_valid(pool, extra[:, :], zd, lead_idx[:, :]).then_inc(got, 16)
                    pool.wait_ge(made, 1)
                    to = table if table is not None else raw
                    scatter_valid(pool, to, (lead_out if more == "final" else lead_idx)[:, :], lead[:, :]).then_inc(put, 16)
                    pool.wait_ge(put, 16)

                @block.tensor
                def _(pe):
                    turn_all(pe, asked, turned, t_ps, 2)
                    if stats:
                        pe.wait_ge(counted, 1)
                        nc.tensor.matmul(m_ps[:, 0:2 * D], lead_has[:, 0:1].broadcast_to([P, P]), pair[:, :],
                                         start=True, stop=True).then_inc(summed, 1)

                @block.scalar
                def _(act):
                    if stats:
                        act.wait_ge(act_go, 1)
                        nc.scalar.activation(pair[:, D:2 * D], pair[:, 0:D], ACT.Square).then_inc(act_done, 1)
                    if more == "layer1":
                        act.wait_ge(act_go, 1)
                        nc.scalar.activation(work[:, D:2 * D], work[:, 0:D], ACT.Square).then_inc(act_done, 1)
                        act.wait_ge(act_go, 2)
                        nc.scalar.activation(work[:, 2 * D + 1:2 * D + 2], work[:, 2 * D:2 * D + 1], ACT.Sqrt,
                                             bias=eps[:, :], scale=1.0 / D).then_inc(act_done, 1)

                @block.vector
                def _(dve):
                    st = Steps(dve, step)
                    turner = Turner(dve, st, asked, turned, t_ps)
                    dve.memset(lead[:, :], 0.0).then_inc(blank, 1)
                    dve.memset(extra[:, :], 0.0).then_inc(blank, 1)
                    clear_turn(dve, st)
                    carry_sum(dve, st, turner, tail[:, :], carried[:, :])
                    dve.wait_ge(got, 32 if stats else 16)
                    if more == "scaled":
                        st.link(dve.scalar_tensor_tensor(lead[:, :], carried[:, :], slots[:, 0, DINV_DST, 0:1],
                                                         lead[:, :], ALU.mult, ALU.add))
                    else:
                        st.link(dve.tensor_tensor(lead[:, :], lead[:, :], carried[:, :], ALU.add))
                    if more == "layer1":
                        x, mu, sd, inv = work[:, 0:D], work[:, 2 * D + 2:2 * D + 3], work[:, 2 * D + 1:2 * D + 2], work[:, 2 * D + 3:2 * D + 4]
                        st.link(dve.tensor_tensor(x, lead[:, :], row[:, BIAS_L1, :], ALU.add))
                        st.link(dve.reduce_sum(mu, x, AX.X))
                        st.link(dve.tensor_scalar(mu, mu, 1.0 / D, None, ALU.mult))
                        st.link(dve.tensor_scalar(x, x, mu, None, ALU.subtract))
                        dve.sem_inc(act_go, 1)
                        dve.wait_ge(act_done, 1)
                        st.link(dve.reduce_sum(work[:, 2 * D:2 * D + 1], work[:, D:2 * D], AX.X))
                        dve.sem_inc(act_go, 1)
                        dve.wait_ge(act_done, 2)
                        st.link(dve.reciprocal(inv, sd))
                        st.link(dve.scalar_tensor_tensor(x, x, inv, row[:, LN_G, :], ALU.mult, ALU.mult))
                        st.link(dve.tensor_tensor(x, x, row[:, LN_B, :], ALU.add))
                        st.link(dve.tensor_scalar(lead[:, :], x, 0.0, None, ALU.max))
                    dve.sem_inc(made, 1)
                    if stats:
                        st.link(dve.tensor_tensor(pair[:, 0:D], lead[:, :], extra[:, :], ALU.add))
                        dve.sem_inc(act_go, 1)
                        dve.wait_ge(act_done, 1)
                        dve.sem_inc(counted, 1)
                        dve.wait_ge(summed, 1)
                        st.link(dve.tensor_copy(bn_sums[:, 1, :], m_ps[:, 0:2 * D]))

        def seeds(tag, first_table, second_table=None):
            ctx = ExitStack()
            with ctx:
                got = sem(tag + "_got", ctx)
                step = sem(tag + "_step", ctx)
                block = ctx.enter_context(nc.Block())

                @block.gpsimd
                def _(pool):
                    gather(pool, seed[:, :], first_table, seed_idx[:, :]).then_inc(got, 16)
                    if second_table is not None:
                        gather(pool, seed2[:, :], second_table, seed_idx[:, :]).then_inc(got, 16)

                @block.vector
                def _(dve):
                    dve.wait_ge(got, 16 if second_table is None else 32)
                    if second_table is not None:
                        dve.tensor_tensor(seed[:, :], seed[:, :], seed2[:, :], ALU.add).then_inc(step, 1)
                        dve.wait_ge(step, 1)


        def behind_cols(v, c):
            return v[:, bass.ds((CH - 1 - c.index) * T, T)]

        def prev(c):
            return at(c.half, c.k - 1)

        def ready_prev(eng, sems, c, each=1):
            if not (isinstance(c.index, int) and c.index == 0):
                ready(eng, sems, prev(c), each)

        def types_of(c, forward):
            first = (c.index if forward else CH - 1 - c.index) * T
            return types_t[bass.ds(first, T), :].rearrange("(o t) p -> o (t p)", o=1).broadcast_to([P, T * P])

        def broadcast_back(dve, st, b, tl, cur, c):
            before = b[1 - c.k][:, 0, :]
            for t in reversed(range(T)):
                st.link(dve.scalar_tensor_tensor(b[c.k][:, t, :], before, cur[:, SAME_NEXT, t:t + 1], tl[:, t, :],
                                                 ALU.mult, ALU.add))
                before = b[c.k][:, t, :]

        def centre_apart(dve, st, x, xc, mean, n, centred, c):
            st.link(dve.reduce_sum(mean, x, AX.X))
            dve.scalar_tensor_tensor(xc, bc(mean, n), -1.0 / D, x, ALU.mult, ALU.add).then_inc(centred[c.k], 1)

        def layer1_scores():
            ctx = ExitStack()
            with ctx:
                def two(name, shape, dt=F32):
                    return [sb(f"a1_{name}{k}", shape, dt, ctx) for k in range(2)]
                idx = two("idx", [P, T], I32)
                idx_all = sb("a1_idx_all", [P, STEPS], I32, ctx)
                rows_loaded = sem("a1_rows_loaded", ctx)
                g = two("g", [P, T, D])
                x0 = two("x0", [P, 2 * T, D])
                sums = two("sums", [P, T, D])
                types = two("types", [P, T * P], BF16)
                x = two("x", [P, 2 * T, D])
                xc = two("xc", [P, 2 * T, D])
                sq = two("sq", [P, 2 * T, D])
                b = two("b", [P, T, D])
                tl = sb("a1_tl", [P, T, D], F32, ctx)
                mean = two("mean", [P, 2 * T])
                var = two("var", [P, 2 * T])
                sd = two("sd", [P, 2 * T])
                cur = two("cur", [P, SLOTS, T])
                hs = two("hs", [P, T, 2, D])
                hd = two("hd", [P, T, D])
                hst = two("hst", [D + REL, T * P])
                hdt = two("hdt", [P, T * D])
                by_rel = two("by_rel", [P, REL // 2, T * P])
                m = two("m", [P, T, D])
                key = two("key", [P, T, D])
                query = two("query", [P, T, D])
                rule = two("rule", [P, T, RULES])
                base = sb("a1_base", [P, T], F32, ctx)
                ts_ps = ps("a1_ts_ps", [P, T * P], ctx)
                td_ps = ps("a1_td_ps", [P, T * D], ctx)
                m_ps = ps("a1_m_ps", [P, T * D], ctx)
                k_ps = ps("a1_k_ps", [P, T * D], ctx)
                q_ps = ps("a1_q_ps", [P, T * D], ctx)
                r_ps = ps("a1_r_ps", [P, 512], ctx)
                step = sem("a1_step", ctx)
                begun = sem("a1_begun", ctx)
                differ = sem("a1_differ", ctx)
                (idx_in, gathered, g_used, x_in, x_used, types_in, types_used, x_ready, x_out, centred, squared,
                 summed, rooted, h_ready, h_twice, h_turned, ht_ready, parted, m_made, kq_made, m_ready,
                 kq_ready, kq_used, m_out) = [sems("a1_" + n, ctx) for n in (
                     "idx_in", "gathered", "g_used", "x_in", "x_used", "types_in", "types_used", "x_ready", "x_out",
                     "centred", "squared", "summed", "rooted", "h_ready", "h_twice", "h_turned", "ht_ready",
                     "parted", "m_made", "kq_made", "m_ready", "kq_ready", "kq_used", "m_out")]
                block = ctx.enter_context(nc.Block())

                @block.sync
                def _(sp):
                    sp.dma_start(idx_all[:, :], idx_last).then_inc(rows_loaded, 16)

                    def loads(c):
                        free(sp, x_used, c)
                        sp.dma_start(x0[c.k][:, 0:T, :], behind_cols(rows(xs), c)).then_inc(x_in[c.k], 16)
                        sp.dma_start(x0[c.k][:, T:2 * T, :], behind_cols(rows(xd), c)).then_inc(x_in[c.k], 16)
                        sp.dma_start(sums[c.k][:, :, :], behind_cols(rows(sum0b), c)).then_inc(x_in[c.k], 16)

                    def early(c):
                        ready(sp, x_ready, c)
                        sp.dma_start(behind_cols(rows(x1s), c), x[c.k][:, 0:T, :]).then_inc(x_out[c.k], 16)
                        sp.dma_start(behind_cols(rows(x1d), c), x[c.k][:, T:2 * T, :]).then_inc(x_out[c.k], 16)
                        free(sp, ht_ready, c)
                        free(sp, types_used, c)
                        sp.dma_start(types[c.k][:, :], types_of(c, False)).then_inc(types_in[c.k], 16)

                    def late(c):
                        ready(sp, m_ready, c)
                        sp.dma_start(behind_cols(rows(msg), c), m[c.k][:, :, :]).then_inc(m_out[c.k], 16)
                    streamed(sp, CH, loads, early, late)
                    for k in range(2):
                        n = CH // 2 + (1 - k)
                        sp.wait_ge(x_out[k], 32 * n)
                        sp.wait_ge(m_out[k], 16 * n)

                @block.gpsimd
                def _(pool):
                    pool.wait_ge(rows_loaded, 16)
                    def get(c):
                        take_rows(pool, idx, idx_all, idx_in, gathered, c, behind_cols)
                        free(pool, g_used, c)
                        pool.sem_inc(begun, 1)
                        for t in range(T):
                            gather(pool, g[c.k][:, t, :], sum0b, idx[c.k][:, t:t + 1]).then_inc(gathered[c.k], 16)
                    each_chunk(pool, CH, get)

                @block.scalar
                def _(act):
                    def norm(c):
                        squares(act, xc[c.k][:, :, :], sq[c.k][:, :, :], centred, squared, c)
                        deviation(act, var[c.k][:, :], sd[c.k][:, :], summed, rooted, c)
                        ready(act, h_ready, c)
                        nc.scalar.activation(hs[c.k][:, :, 1, :], hs[c.k][:, :, 0, :], ACT.Copy).then_inc(h_twice[c.k], 1)

                    def turn_out(c):
                        ready(act, h_turned, c)
                        free(act, kq_made, c)
                        ready(act, types_in, c, 16)
                        relation = slice(D, D + REL)
                        nc.scalar.activation(hst[c.k][relation, :], types[c.k][relation, :], ACT.Square,
                                             bias=relrow[relation, :]).then_inc(differ, 1)
                        act.wait_ge(differ, c.index + 1)
                        nc.scalar.activation(hst[c.k][relation, :], hst[c.k][relation, :], ACT.Relu,
                                             bias=one_col[relation, :], scale=-1.0)
                        ready(act, parted, c)
                        nc.scalar.activation(hst[c.k][0:D, :], ts_ps[0:D, :], ACT.Copy)
                        nc.scalar.activation(hdt[c.k][:, :], td_ps[:, :], ACT.Copy).then_inc(ht_ready[c.k], 1)

                    def results(c):
                        ready(act, kq_made, c)
                        free(act, kq_used, c)
                        nc.scalar.activation(key[c.k][:, :, :], k_ps[:, :].rearrange("p (t d) -> p t d", d=D), ACT.Copy)
                        nc.scalar.activation(query[c.k][:, :, :], q_ps[:, :].rearrange("p (t d) -> p t d", d=D), ACT.Copy)
                        nc.scalar.activation(rule[c.k][:, :, :],
                                             r_ps[:, 0:T * RULES].rearrange("p (t r) -> p t r", r=RULES),
                                             ACT.Copy).then_inc(kq_ready[c.k], 1)
                        ready(act, m_made, c)
                        free(act, m_out, c, 16)
                        nc.scalar.activation(m[c.k][:, :, :], m_ps[:, :].rearrange("p (t d) -> p t d", d=D),
                                             ACT.Copy).then_inc(m_ready[c.k], 1)
                    trailing(act, CH, norm, turn_out, results)

                @block.tensor
                def _(pe):
                    def turn_rows(c):
                        ready(pe, h_twice, c)
                        ready_prev(pe, parted, c)
                        ready_prev(pe, ht_ready, c)
                        for t in range(T):
                            nc.tensor.transpose(ts_ps[:, t * P:(t + 1) * P],
                                                hs[c.k][:, t, :, :].rearrange("p a d -> p (a d)"), ident[:, :])
                        for j in range(T // 2):
                            last = nc.tensor.transpose(td_ps[:, j * P:(j + 1) * P],
                                                       hd[c.k][:, 2 * j:2 * j + 2, :].rearrange("p t d -> p (t d)"),
                                                       ident[:, :])
                        last.then_inc(h_turned[c.k], 1)

                    def products(c):
                        ready(pe, ht_ready, c)
                        ready(pe, parted, c)
                        ready_prev(pe, kq_ready, c)
                        for t in range(T):
                            nc.tensor.matmul(k_ps[:, t * D:(t + 1) * D], hst[c.k][:, t * P:(t + 1) * P], wkey[:, :],
                                             start=True, stop=True)
                        for j in range(T // 2):
                            w = hdt[c.k][:, j * P:(j + 1) * P]
                            nc.tensor.matmul(q_ps[:, j * P:(j + 1) * P], w, wblock[:, WQ, :], start=True, stop=True)
                            last = nc.tensor.matmul(r_ps[:, j * 2 * RULES:(j + 1) * 2 * RULES], w, wrule[:, :],
                                                    start=True, stop=True)
                        last.then_inc(kq_made[c.k], 1)
                        ready_prev(pe, m_ready, c)
                        relation_products(pe, m_ps, by_rel[c.k], 0).then_inc(m_made[c.k], 1)
                    leading(pe, CH, turn_rows, products)

                @block.vector
                def _(dve):
                    st = Steps(dve, step)
                    st.link(dve.tensor_copy(b[1][:, 0, :], seed[:, :]))

                    def front(c):
                        st.link(dve.tensor_copy(cur[c.k][:, :, :], slots[:, bass.ds(CH - 1 - c.index, 1), :, :]
                                                .rearrange("p o s t -> p (o s) t")))
                        ready(dve, x_in, c, 48)
                        ready(dve, gathered, c, 16 * T)
                        free(dve, x_out, c, 32)
                        source, target = x[c.k][:, 0:T, :], x[c.k][:, T:2 * T, :]
                        st.mark(dve.tensor_tensor(source, g[c.k][:, :, :], x0[c.k][:, 0:T, :], ALU.add))
                        st.link(dve.tensor_tensor(tl[:, :, :], sums[c.k][:, :, :], bc(cur[c.k][:, LAST, :], T), ALU.mult))
                        dve.sem_inc(g_used[c.k], 1)
                        broadcast_back(dve, st, b, tl, cur[c.k], c)
                        st.link(dve.tensor_tensor(target, b[c.k][:, :, :], x0[c.k][:, T:2 * T, :], ALU.add))
                        dve.sem_inc(x_used[c.k], 1)
                        dve.sem_inc(x_ready[c.k], 1)
                        centre_apart(dve, st, x[c.k][:, :, :], xc[c.k][:, :, :], mean[c.k][:, :], 2 * T, centred, c)

                    def middle(c):
                        ready(dve, h_turned, c)
                        ready(dve, types_in, c, 16)
                        free(dve, m_made, c)
                        part_relations(dve, st, by_rel[c.k], types[c.k], ts_ps)
                        st.wait()
                        dve.sem_inc(parted[c.k], 1)
                        dve.sem_inc(types_used[c.k], 1)

                    def back(c):
                        variance(dve, sq[c.k][:, :, :], var[c.k][:, :], squared, summed, c)
                        ready(dve, rooted, c)
                        st.link(dve.reciprocal(mean[c.k][:, :], sd[c.k][:, :]))
                        free(dve, h_turned, c)
                        st.mark(dve.scalar_tensor_tensor(hs[c.k][:, :, 0, :], xc[c.k][:, 0:T, :], 0.0,
                                                         bc(mean[c.k][:, 0:T], T), ALU.max, ALU.mult))
                        st.link(dve.scalar_tensor_tensor(hd[c.k][:, :, :], xc[c.k][:, T:2 * T, :], 0.0,
                                                         bc(mean[c.k][:, T:2 * T], T), ALU.max, ALU.mult))
                        dve.sem_inc(h_ready[c.k], 1)

                    def finish(c):
                        ready(dve, kq_ready, c)
                        q, r = query[c.k][:, :, :], rule[c.k][:, :, :]
                        st.link(dve.tensor_tensor(q, q, rb(BQ, T), ALU.add))
                        st.link(dve.tensor_tensor(q, q, key[c.k][:, :, :], ALU.mult))
                        st.link(dve.reduce_sum(base[:, :], q, AX.X))
                        st.link(dve.tensor_tensor(r, r, brule[:, None, :].broadcast_to([P, T, RULES]), ALU.add))
                        st.link(dve.tensor_tensor(r, r, base[:, :, None].broadcast_to([P, T, RULES]), ALU.add))
                        settle(dve)
                        st.link(dve.tensor_scalar(scores[:, bass.ds((CH - 1 - c.index) * T, T), :], r,
                                                  1.0 / D ** 0.5, None, ALU.mult))
                        dve.sem_inc(kq_used[c.k], 1)
                    skewed(dve, st, CH, front, middle, back, finish, lag=2)

        def part_relations(dve, st, by_rel, types, turned):
            for rr in range(REL // 2):
                st.mark(dve.scalar_tensor_tensor(by_rel[:, rr, :], types[:, :], relid[:, rr:rr + 1], turned[:, :],
                                                 ALU.is_equal, ALU.mult))

        def relation_products(pe, m_ps, by_rel, which):
            for t in range(T):
                for rr in range(REL // 2):
                    last = nc.tensor.matmul(m_ps[:, t * D:(t + 1) * D], by_rel[:, rr, t * P:(t + 1) * P],
                                            wrel[:, which, rr, :], start=(rr == 0), stop=(rr == REL // 2 - 1))
            return last

        def softmax(tag, heads):
            ctx = ExitStack()
            with ctx:
                val = sb(tag + "_val", [P, heads, STEPS], F32, ctx)
                fwd = sb(tag + "_fwd", [P, heads, STEPS], F32, ctx)
                bwd = sb(tag + "_bwd", [P, heads, STEPS], F32, ctx)
                stop_p = sb(tag + "_stop_p", [P, STEPS], F32, ctx)
                stop_n = sb(tag + "_stop_n", [P, STEPS], F32, ctx)
                out_p = sb(tag + "_out_p", [P, STEPS], F32, ctx)
                out_n = sb(tag + "_out_n", [P, STEPS], F32, ctx)
                att = sb(tag + "_att", [P, STEPS], F32, ctx)
                cf = sb(tag + "_cf", [P, heads], F32, ctx)
                cb = sb(tag + "_cb", [P, heads], F32, ctx)
                ends = sb(tag + "_ends", [P, heads], F32, ctx)
                t_ps = ps(tag + "_t_ps", [P, 512], ctx)
                step = sem(tag + "_step", ctx)
                asked = sem(tag + "_asked", ctx)
                turned = sem(tag + "_turned", ctx)
                shifted = sem(tag + "_shifted", ctx)
                powers = sem(tag + "_powers", ctx)
                block = ctx.enter_context(nc.Block())

                @block.tensor
                def _(pe):
                    turn_all(pe, asked, turned, t_ps, 8)

                @block.scalar
                def _(act):
                    act.wait_ge(shifted, 1)
                    nc.scalar.activation(val[:, :, :], val[:, :, :], ACT.Exp).then_inc(powers, 1)

                @block.vector
                def _(dve):
                    st = Steps(dve, step)
                    turner = Turner(dve, st, asked, turned, t_ps)
                    for switch, to in ((same_prev, stop_p), (same_next, stop_n), (prefix, out_p), (suffix, out_n)):
                        st.mark(dve.tensor_scalar(to[:, :], switch[:, :], 1.0, HUGE, ALU.subtract, ALU.mult))
                    for h in range(heads):
                        st.mark(dve.tensor_copy(val[:, h, :], scores[:, :, h]))
                    st.wait()
                    for h in range(heads):
                        st.mark(dve.tensor_tensor_scan(fwd[:, h, :], stop_p[:, :], val[:, h, :], -HUGE,
                                                       ALU.add, ALU.max))
                        st.mark(dve.tensor_tensor_scan(bwd[:, h, ::-1], stop_n[:, ::-1], val[:, h, ::-1], -HUGE,
                                                       ALU.add, ALU.max))
                    st.wait()
                    clear_turn(dve, st)
                    st.link(dve.tensor_copy(ends[:, :], fwd[:, :, STEPS - 1]))
                    carry_max(dve, st, turner, ends[:, :], cf[:, :])
                    clear_turn(dve, st)
                    st.link(dve.tensor_copy(ends[:, :], bwd[:, :, 0]))
                    carry_max(dve, st, turner, ends[:, :], cb[:, :], backward=True)
                    for h in range(heads):
                        st.link(dve.tensor_tensor(fwd[:, h, :], fwd[:, h, :], bwd[:, h, :], ALU.max))
                        st.link(dve.scalar_tensor_tensor(fwd[:, h, :], out_p[:, :], cf[:, h:h + 1], fwd[:, h, :],
                                                         ALU.add, ALU.max))
                        st.link(dve.scalar_tensor_tensor(fwd[:, h, :], out_n[:, :], cb[:, h:h + 1], fwd[:, h, :],
                                                         ALU.add, ALU.max))
                    st.link(dve.tensor_tensor(val[:, :, :], val[:, :, :], fwd[:, :, :], ALU.subtract))
                    dve.sem_inc(shifted, 1)
                    dve.wait_ge(powers, 1)
                    for h in range(heads):
                        st.mark(dve.tensor_tensor_scan(fwd[:, h, :], same_prev[:, :], val[:, h, :], 0.0,
                                                       ALU.mult, ALU.add))
                        st.mark(dve.tensor_tensor_scan(bwd[:, h, ::-1], same_next[:, ::-1], val[:, h, ::-1], 0.0,
                                                       ALU.mult, ALU.add))
                    st.wait()
                    clear_turn(dve, st)
                    st.link(dve.tensor_copy(ends[:, :], fwd[:, :, STEPS - 1]))
                    carry_sum(dve, st, turner, ends[:, :], cf[:, :])
                    clear_turn(dve, st)
                    st.link(dve.tensor_copy(ends[:, :], bwd[:, :, 0]))
                    carry_sum(dve, st, turner, ends[:, :], cb[:, :], backward=True)
                    for h in range(heads):
                        st.link(dve.tensor_tensor(fwd[:, h, :], fwd[:, h, :], bwd[:, h, :], ALU.add))
                        st.link(dve.tensor_tensor(fwd[:, h, :], fwd[:, h, :], val[:, h, :], ALU.subtract))
                        st.link(dve.scalar_tensor_tensor(fwd[:, h, :], prefix[:, :], cf[:, h:h + 1], fwd[:, h, :],
                                                         ALU.mult, ALU.add))
                        st.link(dve.scalar_tensor_tensor(fwd[:, h, :], suffix[:, :], cb[:, h:h + 1], fwd[:, h, :],
                                                         ALU.mult, ALU.add))
                    st.link(dve.scalar_tensor_tensor(fwd[:, :, :], fwd[:, :, :], 0.0, fwd[:, :, :],
                                                     ALU.is_equal, ALU.add))
                    st.link(dve.reciprocal(fwd[:, :, :], fwd[:, :, :]))
                    st.link(dve.tensor_tensor(val[:, :, :], val[:, :, :], fwd[:, :, :], ALU.mult))
                    st.link(dve.tensor_scalar(att[:, :], val[:, 0, :], 1.0 / heads, None, ALU.mult))
                    for h in range(1, heads):
                        st.link(dve.scalar_tensor_tensor(att[:, :], val[:, h, :], 1.0 / heads, att[:, :],
                                                         ALU.mult, ALU.add))
                    st.link(dve.tensor_copy(slot(ATTENTION), flat(att[:, :])))

        def weighted(layer1):
            ctx = ExitStack()
            tag = "w1" if layer1 else "w3"
            with ctx:
                def two(name, shape, dt=F32):
                    return [sb(f"{tag}_{name}{k}", shape, dt, ctx) for k in range(2)]
                m = two("m", [P, T, D])
                x = two("x", [P, T, D])
                y = two("y", [P, T, D])
                s = two("s", [P, T, D])
                relued = two("relued", [P, T, D]) if layer1 else y
                sq = two("sq", [P, T, D])
                am = sb(tag + "_am", [P, T, D], F32, ctx)
                mean = two("mean", [P, T])
                var = two("var", [P, T])
                sd = two("sd", [P, T])
                cur = sb(tag + "_cur", [P, SLOTS, T], F32, ctx)
                step = sem(tag + "_step", ctx)
                idx = two("idx", [P, T], I32)
                begun = sem(tag + "_begun", ctx)
                (m_in, m_used, s_ready, s_out, centred, squared, summed, rooted, y_ready, y_out, idx_in,
                 scattered, inverted, scaled, shifted) = [
                    sems(f"{tag}_{n}", ctx) for n in ("m_in", "m_used", "s_ready", "s_out", "centred", "squared",
                                                      "summed", "rooted", "y_ready", "y_out", "idx_in",
                                                      "scattered", "inverted", "scaled", "shifted")]
                block = ctx.enter_context(nc.Block())
                ins = 1 if layer1 else 2

                @block.sync
                def _(sp):
                    def loads(c):
                        free(sp, m_used, c)
                        sp.dma_start(m[c.k][:, :, :], edge_cols(rows(msg if layer1 else hs3), c)).then_inc(m_in[c.k], 16)
                        if not layer1:
                            sp.dma_start(x[c.k][:, :, :], edge_cols(rows(x3d), c)).then_inc(m_in[c.k], 16)
                            free(sp, scattered, c, 16 * T)
                            sp.dma_start(idx[c.k][:, :], edge_cols(idx_out, c)).then_inc(idx_in[c.k], 16)

                    def early(c):
                        if layer1:
                            ready(sp, s_ready, c)
                            sp.dma_start(edge_cols(rows(raw1), c), s[c.k][:, :, :]).then_inc(s_out[c.k], 16)
                        else:
                            store(c)

                    def late(c):
                        if layer1:
                            store(c)

                    def store(c):
                        ready(sp, y_ready, c)
                        sp.dma_start(edge_cols(rows(act1 if layer1 else fin), c), relued[c.k][:, :, :]).then_inc(y_out[c.k], 16)
                    streamed(sp, CH, loads, early, late)
                    for k in range(2):
                        n = CH // 2 + (1 - k)
                        if layer1:
                            sp.wait_ge(s_out[k], 16 * n)
                        sp.wait_ge(y_out[k], 16 * n)

                if not layer1:
                    @block.gpsimd
                    def _(pool):
                        def put(c):
                            ready(pool, idx_in, c, 16)
                            ready(pool, y_ready, c)
                            pool.sem_inc(begun, 1)
                            for t in range(T):
                                scatter_valid(pool, out, idx[c.k][:, t:t + 1], y[c.k][:, t, :]).then_inc(scattered[c.k], 16)
                        each_chunk(pool, CH, put)
                        for k in range(2):
                            pool.wait_ge(scattered[k], 16 * T * (CH // 2 + (1 - k)))

                if layer1:
                    @block.scalar
                    def _(act):
                        def scale(c):
                            ready(act, inverted, c)
                            for t in range(T):
                                last = nc.scalar.activation(y[c.k][:, t, :], y[c.k][:, t, :], ACT.Copy,
                                                            scale=mean[c.k][:, t:t + 1])
                            last.then_inc(scaled[c.k], 1)

                        def norm(c):
                            if not (isinstance(c.index, int) and c.index == 0):
                                scale(prev(c))
                            squares(act, y[c.k][:, :, :], sq[c.k][:, :, :], centred, squared, c)
                            deviation(act, var[c.k][:, :], sd[c.k][:, :], summed, rooted, c)

                        def bend(c):
                            if isinstance(c.index, int) and c.index == CH - 1:
                                scale(c)
                            ready(act, shifted, c)
                            free(act, y_out, c, 16)
                            nc.scalar.activation(relued[c.k][:, :, :], y[c.k][:, :, :],
                                                 ACT.Relu).then_inc(y_ready[c.k], 1)
                        leading(act, CH, norm, bend)

                @block.vector
                def _(dve):
                    st = Steps(dve, step)
                    st.link(dve.memset(s[1][:, :, :], 0.0))

                    def front(c):
                        st.link(dve.tensor_copy(cur[:, :, :], slots[:, bass.ds(c.index, 1), :, :]
                                                .rearrange("p o s t -> p (o s) t")))
                        ready(dve, m_in, c, 16 * ins)
                        st.link(dve.tensor_tensor(am[:, :, :], m[c.k][:, :, :], bc(cur[:, ATTENTION, :], T), ALU.mult))
                        if layer1:
                            dve.sem_inc(m_used[c.k], 1)
                            free(dve, s_out, c, 16)
                        sum_along(dve, st, s, am, cur[:, SAME_PREV, :], c)
                        if layer1:
                            free(dve, y_ready, c)
                        else:
                            free(dve, y_out, c, 16)
                            free(dve, scattered, c, 16 * T)
                        if layer1:
                            dve.sem_inc(s_ready[c.k], 1)
                            st.link(dve.tensor_tensor(y[c.k][:, :, :], s[c.k][:, :, :], rb(BIAS_L1, T), ALU.add))
                            centre(dve, st, y[c.k][:, :, :], mean[c.k][:, :], T, centred, c)
                        else:
                            st.link(dve.tensor_tensor(y[c.k][:, :, :], s[c.k][:, :, :], x[c.k][:, :, :], ALU.add))
                            dve.sem_inc(m_used[c.k], 1)
                            dve.sem_inc(y_ready[c.k], 1)

                    def middle(c):
                        if layer1:
                            v = y[c.k][:, :, :]
                            ready(dve, scaled, c)
                            st.link(dve.tensor_tensor(v, v, rb(LN_G, T), ALU.mult))
                            st.link(dve.tensor_tensor(v, v, rb(LN_B, T), ALU.add))
                            dve.sem_inc(shifted[c.k], 1)

                    def back(c):
                        if layer1:
                            variance(dve, sq[c.k][:, :, :], var[c.k][:, :], squared, summed, c)
                            ready(dve, rooted, c)
                            dve.reciprocal(mean[c.k][:, :], sd[c.k][:, :]).then_inc(inverted[c.k], 1)
                    skewed(dve, st, CH, front, middle, back, lambda c: None)
                    st.link(dve.tensor_copy(tail[:, :], s[0][:, T - 1, :]))

        def relational(first):
            ctx = ExitStack()
            tag = "ra" if first else "rb"
            with ctx:
                def two(name, shape, dt=F32):
                    return [sb(f"{tag}_{name}{k}", shape, dt, ctx) for k in range(2)]
                idx = two("idx", [P, T], I32)
                idx_all = sb(f"{tag}_idx_all", [P, STEPS], I32, ctx)
                rows_loaded = sem(f"{tag}_rows_loaded", ctx)
                g = two("g", [P, T, D])
                x0 = two("x0", [P, 2 * T, D])
                sums = two("sums", [P, T, D])
                types = two("types", [P, T * P], BF16)
                x = two("x", [P, 2 * T, D])
                xc = two("xc", [P, 2 * T, D])
                sq = two("sq", [P, 2 * T, D])
                mean = two("mean", [P, 2 * T])
                var = two("var", [P, 2 * T])
                sd = two("sd", [P, 2 * T])
                hs = two("hs", [P, T, 2, D])
                hd = two("hd", [P, T, D])
                hst = two("hst", [P, T * P])
                hdt = two("hdt", [P, T * D])
                by_rel = two("by_rel", [P, REL // 2, T * P])
                m = two("m", [P, T, D])
                s = two("s", [P, T, D])
                y = s if first else two("y", [P, T, D])
                roots = two("roots", [P, 2, T, D])
                pair = two("pair", [P, T, 2, D])
                fcur = two("fcur", [P, SLOTS, T])
                wcur = two("wcur", [P, T])
                zero = sb(tag + "_zero", [P, P], F32, ctx)
                ts_ps = ps(tag + "_ts_ps", [P, T * P], ctx)
                td_ps = ps(tag + "_td_ps", [P, T * D], ctx)
                m_ps = ps(tag + "_m_ps", [P, T * D], ctx)
                zs_ps = ps(tag + "_zs_ps", [P, T * D], ctx)
                zd_ps = ps(tag + "_zd_ps", [P, T * D], ctx)
                st_ps = ps(tag + "_st_ps", [P, 512], ctx)
                step = sem(tag + "_step", ctx)
                begun = sem(tag + "_begun", ctx)
                blank = sem(tag + "_blank", ctx)
                (idx_in, gathered, g_used, x_in, x_used, types_in, types_used, x_ready, x_out, centred, squared,
                 summed, rooted, h_ready, h_twice, h_turned, ht_ready, parted, z_made, m_made, z_ready, m_ready,
                 z_out, s_ready, s_out, total_ready, pair_ready, counted) = [sems(f"{tag}_{n}", ctx) for n in (
                     "idx_in", "gathered", "g_used", "x_in", "x_used", "types_in", "types_used", "x_ready", "x_out",
                     "centred", "squared", "summed", "rooted", "h_ready", "h_twice", "h_turned", "ht_ready",
                     "parted", "z_made", "m_made", "z_ready", "m_ready", "z_out", "s_ready", "s_out",
                     "total_ready", "pair_ready", "counted")]
                block = ctx.enter_context(nc.Block())
                if first:
                    table, source_in, target_in, target_sums, result = act1, x1s, x1d, act1, sum2a
                    root, which, root_s, root_d = ROOT1, 1, zs, zd
                else:
                    table, source_in, target_in, target_sums, result = sum2a, zs, zd, sum2a, sum2b
                    root, which, root_s, root_d = ROOT2, 2, p3s, p3d

                @block.sync
                def _(sp):
                    sp.dma_start(idx_all[:, :], idx_last).then_inc(rows_loaded, 16)

                    def loads(c):
                        free(sp, x_used, c)
                        sp.dma_start(x0[c.k][:, 0:T, :], edge_cols(rows(source_in), c)).then_inc(x_in[c.k], 16)
                        sp.dma_start(x0[c.k][:, T:2 * T, :], edge_cols(rows(target_in), c)).then_inc(x_in[c.k], 16)
                        sp.dma_start(sums[c.k][:, :, :], edge_cols(rows(target_sums), c)).then_inc(x_in[c.k], 16)

                    def early(c):
                        if first:
                            ready(sp, x_ready, c)
                            sp.dma_start(edge_cols(rows(x2s), c), x[c.k][:, 0:T, :]).then_inc(x_out[c.k], 16)
                            sp.dma_start(edge_cols(rows(x2d), c), x[c.k][:, T:2 * T, :]).then_inc(x_out[c.k], 16)
                        free(sp, types_used, c)
                        sp.dma_start(types[c.k][:, :], types_of(c, True)).then_inc(types_in[c.k], 16)

                    def late(c):
                        ready(sp, z_ready, c)
                        sp.dma_start(edge_cols(rows(root_s), c), roots[c.k][:, 0, :, :]).then_inc(z_out[c.k], 16)
                        sp.dma_start(edge_cols(rows(root_d), c), roots[c.k][:, 1, :, :]).then_inc(z_out[c.k], 16)
                        ready(sp, s_ready, c)
                        sp.dma_start(edge_cols(rows(result), c), y[c.k][:, :, :]).then_inc(s_out[c.k], 16)
                    streamed(sp, CH, loads, early, late)
                    for k in range(2):
                        n = CH // 2 + (1 - k)
                        if first:
                            sp.wait_ge(x_out[k], 32 * n)
                        sp.wait_ge(z_out[k], 32 * n)
                        sp.wait_ge(s_out[k], 16 * n)

                @block.gpsimd
                def _(pool):
                    pool.wait_ge(rows_loaded, 16)
                    def get(c):
                        take_rows(pool, idx, idx_all, idx_in, gathered, c, edge_cols)
                        free(pool, g_used, c)
                        pool.sem_inc(begun, 1)
                        for t in range(T):
                            gather(pool, g[c.k][:, t, :], table, idx[c.k][:, t:t + 1]).then_inc(gathered[c.k], 16)
                    each_chunk(pool, CH, get)

                @block.scalar
                def _(act):
                    def norm(c):
                        if first:
                            squares(act, xc[c.k][:, :, :], sq[c.k][:, :, :], centred, squared, c)
                            deviation(act, var[c.k][:, :], sd[c.k][:, :], summed, rooted, c)
                        ready(act, h_ready, c)
                        nc.scalar.activation(hs[c.k][:, :, 1, :], hs[c.k][:, :, 0, :], ACT.Copy).then_inc(h_twice[c.k], 1)

                    def square_sums(c):
                        ready(act, total_ready, c)
                        nc.scalar.activation(pair[c.k][:, :, 1, :], pair[c.k][:, :, 0, :], ACT.Square).then_inc(pair_ready[c.k], 1)

                    def turn_out(c):
                        ready(act, h_turned, c)
                        free(act, z_made, c)
                        if first:
                            ready(act, parted, c)
                            nc.scalar.activation(hst[c.k][0:D, :], ts_ps[0:D, :], ACT.Copy)
                            nc.scalar.activation(hdt[c.k][:, :], td_ps[:, :], ACT.Copy).then_inc(ht_ready[c.k], 1)
                        else:
                            free(act, parted, c)
                            nc.scalar.activation(hst[c.k][:, :], ts_ps[:, :], ACT.Relu, bias=bn_col[:, 1:2],
                                                 scale=bn_col[:, 0:1])
                            nc.scalar.activation(hdt[c.k][:, :], td_ps[:, :], ACT.Relu, bias=bn_col[:, 1:2],
                                                 scale=bn_col[:, 0:1]).then_inc(ht_ready[c.k], 1)

                    def results(c):
                        if first and not (isinstance(c.half, int) and c.half == 0):
                            square_sums(at(c.half - 1, c.k))
                        ready(act, z_made, c)
                        free(act, z_out, c, 32)
                        free(act, s_ready, c)
                        for half, of in ((0, zs_ps), (1, zd_ps)):
                            last = nc.scalar.activation(roots[c.k][:, half, :, :],
                                                        of[:, :].rearrange("p (t d) -> p t d", d=D), ACT.Copy)
                        last.then_inc(z_ready[c.k], 1)
                        ready(act, m_made, c)
                        for t in range(T):
                            last = nc.scalar.activation(m[c.k][:, t, :], m_ps[:, t * D:(t + 1) * D], ACT.Copy,
                                                        scale=wcur[c.k][:, t:t + 1])
                        last.then_inc(m_ready[c.k], 1)
                    trailing(act, CH, norm, turn_out, results)
                    if first:
                        square_sums(at(CH // 2 - 1, 1))
                        square_sums(at(CH // 2, 0))

                @block.tensor
                def _(pe):
                    def count(c, final=False):
                        ready(pe, pair_ready, c)
                        for t in range(T):
                            last = nc.tensor.matmul(st_ps[:, 0:P], fcur[c.k][:, COUNTED, t:t + 1].broadcast_to([P, P]),
                                                    pair[c.k][:, t, :, :].rearrange("p a d -> p (a d)"),
                                                    start=False, stop=final and t == T - 1, skip_group_check=True)
                        last.then_inc(counted[c.k], 1)

                    def turn_rows(c):
                        ready(pe, h_twice, c)
                        if first:
                            ready_prev(pe, parted, c)
                        ready_prev(pe, ht_ready, c)
                        for t in range(T):
                            nc.tensor.transpose(ts_ps[:, t * P:(t + 1) * P],
                                                hs[c.k][:, t, :, :].rearrange("p a d -> p (a d)"), ident[:, :])
                        for j in range(T // 2):
                            last = nc.tensor.transpose(td_ps[:, j * P:(j + 1) * P],
                                                       hd[c.k][:, 2 * j:2 * j + 2, :].rearrange("p t d -> p (t d)"),
                                                       ident[:, :])
                        last.then_inc(h_turned[c.k], 1)

                    def products(c):
                        ready(pe, ht_ready, c)
                        ready_prev(pe, z_ready, c)
                        for t in range(T):
                            nc.tensor.matmul(zs_ps[:, t * D:(t + 1) * D], hst[c.k][0:D, t * P:(t + 1) * P],
                                             wblock[0:D, root, 0:D], start=True, stop=True)
                        for j in range(T // 2):
                            last = nc.tensor.matmul(zd_ps[:, j * P:(j + 1) * P], hdt[c.k][:, j * P:(j + 1) * P],
                                                    wblock[:, root, :], start=True, stop=True)
                        last.then_inc(z_made[c.k], 1)
                        ready(pe, parted, c)
                        ready_prev(pe, m_ready, c)
                        relation_products(pe, m_ps, by_rel[c.k], which).then_inc(m_made[c.k], 1)
                        if first and not (isinstance(c.half, int) and c.half == 0):
                            count(at(c.half - 1, c.k))

                    if first:
                        pe.wait_ge(blank, 1)
                        nc.tensor.matmul(st_ps[:, 0:P], zero[:, :], zero[:, :], start=True, stop=False,
                                         skip_group_check=True)
                    leading(pe, CH, turn_rows, products)
                    if first:
                        count(at(CH // 2 - 1, 1))
                        count(at(CH // 2, 0), True)

                @block.vector
                def _(dve):
                    st = Steps(dve, step)
                    st.link(dve.memset(s[1][:, :, :], 0.0))
                    dve.memset(zero[:, :], 0.0).then_inc(blank, 1)

                    def front(c):
                        ready(dve, x_in, c, 48)
                        ready(dve, gathered, c, 16 * T)
                        if first:
                            free(dve, x_out, c, 32)
                            source, target = x[c.k][:, 0:T, :], x[c.k][:, T:2 * T, :]
                        else:
                            free(dve, h_turned, c)
                            source, target = hs[c.k][:, :, 0, :], hd[c.k][:, :, :]
                        st.mark(dve.tensor_tensor(source, g[c.k][:, :, :], x0[c.k][:, 0:T, :], ALU.add))
                        st.link(dve.tensor_tensor(target, sums[c.k][:, :, :], x0[c.k][:, T:2 * T, :], ALU.add))
                        dve.sem_inc(g_used[c.k], 1)
                        dve.sem_inc(x_used[c.k], 1)
                        if first:
                            dve.sem_inc(x_ready[c.k], 1)
                            centre_apart(dve, st, x[c.k][:, :, :], xc[c.k][:, :, :], mean[c.k][:, :], 2 * T, centred, c)
                        else:
                            dve.sem_inc(h_ready[c.k], 1)

                    def middle(c):
                        free(dve, m_ready, c)
                        settle(dve)
                        st.mark(dve.tensor_copy(wcur[c.k][:, :], slots[:, bass.ds(c.index, 1), REL_WEIGHT, :]
                                                .rearrange("p o t -> p (o t)")))
                        ready(dve, h_turned if first else ht_ready, c)
                        ready(dve, types_in, c, 16)
                        free(dve, m_made, c)
                        part_relations(dve, st, by_rel[c.k], types[c.k], ts_ps if first else hst[c.k])
                        st.wait()
                        dve.sem_inc(parted[c.k], 1)
                        dve.sem_inc(types_used[c.k], 1)

                    def back(c):
                        if first:
                            variance(dve, sq[c.k][:, :, :], var[c.k][:, :], squared, summed, c)
                            ready(dve, rooted, c)
                            st.link(dve.reciprocal(mean[c.k][:, :], sd[c.k][:, :]))
                            free(dve, h_turned, c)
                            for to, a in ((hs[c.k][:, :, 0, :], 0), (hd[c.k][:, :, :], T)):
                                st.mark(dve.scalar_tensor_tensor(to, xc[c.k][:, a:a + T, :], 0.0,
                                                                 bc(mean[c.k][:, a:a + T], T), ALU.max, ALU.mult))
                            st.wait()
                            dve.sem_inc(h_ready[c.k], 1)

                    def finish(c):
                        if first:
                            free(dve, counted, c)
                            settle(dve)
                        st.link(dve.tensor_copy(fcur[c.k][:, :, :], slots[:, bass.ds(c.index, 1), :, :]
                                                .rearrange("p o s t -> p (o s) t")))
                        ready(dve, m_ready, c)
                        free(dve, s_out, c, 16)
                        sum_along(dve, st, s, m[c.k], fcur[c.k][:, SAME_PREV, :], c)
                        if not first:
                            st.link(dve.tensor_tensor(y[c.k][:, :, :], s[c.k][:, :, :], rb(B2_L2, T), ALU.add))
                        if first:
                            ready(dve, z_ready, c)
                            st.link(dve.tensor_tensor(pair[c.k][:, :, 0, :], s[c.k][:, :, :], roots[c.k][:, 1, :, :], ALU.add))
                            dve.sem_inc(total_ready[c.k], 1)
                        dve.sem_inc(s_ready[c.k], 1)
                    skewed(dve, st, CH, front, middle, back, finish, lag=2)
                    st.link(dve.tensor_copy(tail[:, :], s[0][:, T - 1, :]))
                    if first:
                        ready(dve, counted, at(CH // 2 - 1, 1))
                        ready(dve, counted, at(CH // 2, 0))
                        st.link(dve.tensor_copy(bn_sums[:, 0, :], st_ps[:, 0:P]))

        def batch_norm():
            ctx = ExitStack()
            with ctx:
                mv = sb("bn_mv", [P, 2], F32, ctx)
                ds = sb("bn_ds", [P, 2], F32, ctx)
                fold = sb("bn_fold", [P, D], F32, ctx)
                a = sb("bn_a", [P, 2, D], F32, ctx)
                sd = sb("bn_sd", [P, D], F32, ctx)
                r_ps = ps("bn_r_ps", [P, 512], ctx)
                t_ps = ps("bn_t_ps", [P, 512], ctx)
                step = sem("bn_step", ctx)
                asked = sem("bn_asked", ctx)
                turned = sem("bn_turned", ctx)
                go = sem("bn_go", ctx)
                spread = sem("bn_spread", ctx)
                var_ready = sem("bn_var", ctx)
                rooted = sem("bn_rooted", ctx)
                block = ctx.enter_context(nc.Block())
                each = CH * TN * P / 2

                @block.tensor
                def _(pe):
                    pe.wait_ge(go, 1)
                    for j in range(2):
                        last = nc.tensor.matmul(r_ps[:, j * D:(j + 1) * D], ds[:, j:j + 1].broadcast_to([P, P]),
                                                fold[:, :], start=True, stop=True)
                    last.then_inc(spread, 1)
                    turn_all(pe, asked, turned, t_ps, 2)

                @block.scalar
                def _(act):
                    act.wait_ge(var_ready, 1)
                    nc.scalar.activation(sd[:, :], a[:, 1, :], ACT.Sqrt, bias=eps[:, :]).then_inc(rooted, 1)

                @block.vector
                def _(dve):
                    st = Steps(dve, step)
                    turner = Turner(dve, st, asked, turned, t_ps)
                    st.mark(dve.tensor_tensor(fold[:, :], ident[:, 0:D], ident[:, D:P], ALU.add))
                    st.link(dve.bn_aggr(mv[:, :], node_stats[:, :, :]))
                    st.link(dve.tensor_scalar(ds[:, 0:1], mv[:, 0:1], each, None, ALU.mult))
                    st.link(dve.scalar_tensor_tensor(ds[:, 1:2], mv[:, 0:1], mv[:, 0:1], mv[:, 1:2], ALU.mult, ALU.add))
                    st.link(dve.tensor_scalar(ds[:, 1:2], ds[:, 1:2], each, None, ALU.mult))
                    dve.sem_inc(go, 1)
                    dve.wait_ge(spread, 1)
                    v = a[:, :, :].rearrange("p a d -> p (a d)")
                    st.link(dve.tensor_tensor(v, r_ps[:, 0:2 * D], bn_sums[:, 0, :], ALU.add))
                    st.link(dve.tensor_tensor(v, v, bn_sums[:, 1, :], ALU.add))
                    st.link(dve.tensor_scalar(v, v, 1.0 / N, None, ALU.mult))
                    mean, var, scale, shift = a[:, 0, :], a[:, 1, :], row[:, BN_SCALE, :], row[:, BN_SHIFT, :]
                    st.link(dve.tensor_tensor(shift, mean, mean, ALU.mult))
                    st.link(dve.tensor_tensor(var, var, shift, ALU.subtract))
                    dve.sem_inc(var_ready, 1)
                    dve.wait_ge(rooted, 1)
                    st.link(dve.reciprocal(scale, sd[:, :]))
                    st.link(dve.tensor_tensor(scale, scale, row[:, GAMMA, :], ALU.mult))
                    st.link(dve.tensor_tensor(mean, mean, row[:, B1_L2, :], ALU.add))
                    st.link(dve.tensor_tensor(shift, row[:, B1_L2, :], mean, ALU.subtract))
                    st.link(dve.tensor_tensor(shift, shift, scale, ALU.mult))
                    st.link(dve.tensor_tensor(shift, shift, row[:, BETA, :], ALU.add))
                    st.mark(dve.tensor_tensor(row[:, INACTIVE_OUT, :], row[:, INACTIVE_X2, :], row[:, B2_L2, :], ALU.add))
                    st.wait()
                    cut_row(dve, st, ADD_INACTIVE, INACTIVE_OUT)
                    for j, of in ((0, scale), (1, shift)):
                        for h in range(2):
                            st.mark(dve.tensor_copy(turn[:, h * D:(h + 1) * D], of))
                        st.wait()
                        t = turner()
                        st.link(dve.tensor_copy(bn_col[:, j:j + 1], t[:, 0:1]))

        def layer3_scores():
            ctx = ExitStack()
            with ctx:
                def two(name, shape, dt=F32):
                    return [sb(f"a3_{name}{k}", shape, dt, ctx) for k in range(2)]
                idx = two("idx", [P, T], I32)
                idx_all = sb("a3_idx_all", [P, STEPS], I32, ctx)
                rows_loaded = sem("a3_rows_loaded", ctx)
                g = two("g", [P, 2 * T, D])
                x0 = two("x0", [P, 2 * T, D])
                p0 = two("p0", [P, 2 * T, D])
                x = two("x", [P, 2 * T, D])
                xc = two("xc", [P, 2 * T, D])
                sq = two("sq", [P, 2 * T, D])
                tl = sb("a3_tl", [P, T, D], F32, ctx)
                b = [v[:, T:2 * T, :] for v in x]
                mean = two("mean", [P, 2 * T])
                var = two("var", [P, 2 * T])
                sd = two("sd", [P, 2 * T])
                cur = two("cur", [P, SLOTS, T])
                h = two("h", [P, T, 2, D])
                ht = two("ht", [P, T * P])
                m = two("m", [P, T, D])
                extra = sb("a3_extra", [P, D], F32, ctx)
                nz = two("nz", [P, TN * D])
                nx = two("nx", [P, TN * D])
                nht = two("nht", [P, TN * D])
                ny = two("ny", [P, TN, D])
                o_ps = [ps(f"a3_o_ps{k}", [P, TN * D], ctx) for k in range(2)]
                t_ps = ps("a3_t_ps", [P, T * P], ctx)
                m_ps = [ps(f"a3_m_ps{k}", [P, T * D], ctx) for k in range(2)]
                step = sem("a3_step", ctx)
                begun = sem("a3_begun", ctx)
                seeded = sem("a3_seeded", ctx)
                (idx_in, gathered, g_used, x_in, x_used, x_ready, x_out, centred, squared, summed, rooted, h_ready,
                 h_out, h_turned, ht_ready, m_made, tanhed, m_used, nz_in, nx_in, nht_ready, n_made,
                 ny_ready, ny_out) = [sems("a3_" + n, ctx) for n in (
                     "idx_in", "gathered", "g_used", "x_in", "x_used", "x_ready", "x_out", "centred", "squared",
                     "summed", "rooted", "h_ready", "h_out", "h_turned", "ht_ready", "m_made", "tanhed",
                     "m_used", "nz_in", "nx_in", "nht_ready", "n_made", "ny_ready", "ny_out")]
                blank = sem("a3_blank", ctx)

                def nodes_of(v, c):
                    if isinstance(c.index, int) and c.index == CH - 1:
                        return v[(CH - 1) * NODES:N, :].rearrange("(p t) d -> p t d", t=TN)
                    return v[bass.ds(c.index * NODES, NODES), :].rearrange("(p t) d -> p t d", t=TN)

                def parts(c):
                    return REST if isinstance(c.index, int) and c.index == CH - 1 else P
                block = ctx.enter_context(nc.Block())

                @block.sync
                def _(sp):
                    sp.dma_start(idx_all[:, :], idx_last).then_inc(rows_loaded, 16)

                    def loads(c):
                        free(sp, x_used, c)
                        for to, of in ((x0[c.k][:, 0:T, :], x2s), (x0[c.k][:, T:2 * T, :], x2d),
                                       (p0[c.k][:, 0:T, :], p3s), (p0[c.k][:, T:2 * T, :], p3d),
                                       (g[c.k][:, T:2 * T, :], sum2b)):
                            sp.dma_start(to, behind_cols(rows(of), c)).then_inc(x_in[c.k], 16)

                    def early(c):
                        ready(sp, x_ready, c)
                        sp.dma_start(behind_cols(rows(x3d), c), b[c.k][:, :, :]).then_inc(x_out[c.k], 16)
                        ready(sp, h_ready, c)
                        sp.dma_start(behind_cols(rows(hs3), c), h[c.k][:, :, 0, :]).then_inc(h_out[c.k], 16)
                        free(sp, nht_ready, c)
                        sp.dma_start(nz[c.k][:, :], z_nodes[bass.ds(c.index, 1)]
                                     .rearrange("o p n -> (o p) n")).then_inc(nz_in[c.k], 16)
                        free(sp, n_made, c)
                        sp.dma_start(nx[c.k][0:parts(c), :].rearrange("p (t d) -> p t d", d=D),
                                     nodes_of(A["x"], c)).then_inc(nx_in[c.k], 16)

                    def late(c):
                        ready(sp, ny_ready, c)
                        sp.dma_start(nodes_of(out, c), ny[c.k][0:parts(c), :, :]).then_inc(ny_out[c.k], 16)
                    sp.wait_ge(blank, 1)
                    streamed(sp, CH, loads, early, late)
                    for k in range(2):
                        n = CH // 2 + (1 - k)
                        sp.wait_ge(x_out[k], 16 * n)
                        sp.wait_ge(h_out[k], 16 * n)
                        sp.wait_ge(ny_out[k], 16 * n)

                @block.gpsimd
                def _(pool):
                    pool.wait_ge(rows_loaded, 16)
                    for to, of in ((seed, x2d), (seed2, p3d), (extra, sum2b)):
                        gather(pool, to[:, :], of, seed_idx[:, :]).then_inc(seeded, 16)

                    def get(c):
                        take_rows(pool, idx, idx_all, idx_in, gathered, c, behind_cols)
                        free(pool, g_used, c)
                        pool.sem_inc(begun, 1)
                        for t in range(T):
                            gather(pool, g[c.k][:, t, :], sum2b, idx[c.k][:, t:t + 1]).then_inc(gathered[c.k], 16)
                    each_chunk(pool, CH, get)

                @block.scalar
                def _(act):
                    def norm(c):
                        squares(act, xc[c.k][:, :, :], sq[c.k][:, :, :], centred, squared, c)
                        deviation(act, var[c.k][:, :], sd[c.k][:, :], summed, rooted, c)

                    def turn_out(c):
                        ready(act, h_turned, c)
                        free(act, m_made, c)
                        nc.scalar.activation(ht[c.k][:, :], t_ps[:, :], ACT.Copy).then_inc(ht_ready[c.k], 1)
                        ready(act, nz_in, c, 16)
                        free(act, n_made, c)
                        nc.scalar.activation(nht[c.k][:, :], nz[c.k][:, :], ACT.Relu, bias=bn_col[:, 1:2],
                                             scale=bn_col[:, 0:1]).then_inc(nht_ready[c.k], 1)

                    def results(c):
                        ready(act, m_made, c)
                        free(act, m_used, c)
                        nc.scalar.activation(m[c.k][:, :, :], m_ps[c.k][:, :].rearrange("p (t d) -> p t d", d=D),
                                             ACT.Tanh).then_inc(tanhed[c.k], 1)
                        ready(act, n_made, c)
                        free(act, ny_out, c, 16)
                        nc.scalar.activation(ny[c.k][:, :, :], o_ps[c.k][:, :].rearrange("p (t d) -> p t d", d=D),
                                             ACT.Copy).then_inc(ny_ready[c.k], 1)
                    trailing(act, CH, norm, turn_out, results)

                @block.tensor
                def _(pe):
                    def turn_rows(c):
                        ready(pe, h_ready, c)
                        ready_prev(pe, ht_ready, c)
                        for t in range(T):
                            last = nc.tensor.transpose(t_ps[:, t * P:(t + 1) * P],
                                                       h[c.k][:, t, :, :].rearrange("p a d -> p (a d)"), ident[:, :])
                        last.then_inc(h_turned[c.k], 1)

                    def products(c):
                        ready(pe, ht_ready, c)
                        free(pe, tanhed, c)
                        for t in range(T):
                            nc.tensor.matmul(m_ps[c.k][:, t * D:(t + 1) * D], ht[c.k][:, t * P:(t + 1) * P],
                                             watt[:, :], start=t == 0, stop=False, skip_group_check=True)
                        last = add_row(m_ps[c.k][:, :], ADD_B_ATT)
                        last.then_inc(m_made[c.k], 1)
                        ready(pe, nht_ready, c)
                        ready(pe, nx_in, c, 16)
                        free(pe, ny_ready, c)
                        for j in range(TN // 2):
                            nc.tensor.matmul(o_ps[c.k][:, j * P:(j + 1) * P], nht[c.k][:, j * P:(j + 1) * P],
                                             wblock[:, ROOT2, :], start=j % 4 == 0, stop=False,
                                             skip_group_check=True)
                            nc.tensor.matmul(o_ps[c.k][:, j * P:(j + 1) * P], ident[:, :],
                                             nx[c.k][:, j * P:(j + 1) * P], start=False, stop=False,
                                             skip_group_check=True)
                        for half in range(2):
                            last = add_row(o_ps[c.k][:, half * T * D:(half + 1) * T * D], ADD_INACTIVE)
                        last.then_inc(n_made[c.k], 1)
                    leading(pe, CH, turn_rows, products)

                @block.vector
                def _(dve):
                    st = Steps(dve, step)
                    dve.memset(nx[0][:, :], 0.0).then_inc(blank, 1)
                    dve.wait_ge(seeded, 48)
                    st.link(dve.tensor_tensor(seed[:, :], seed[:, :], seed2[:, :], ALU.add))
                    st.link(dve.tensor_tensor(b[1][:, 0, :], seed[:, :], extra[:, :], ALU.add))

                    def front(c):
                        st.link(dve.tensor_copy(cur[c.k][:, :, :], slots[:, bass.ds(CH - 1 - c.index, 1), :, :]
                                                .rearrange("p o s t -> p (o s) t")))
                        ready(dve, x_in, c, 80)
                        ready(dve, gathered, c, 16 * T)
                        free(dve, x_out, c, 16)
                        v = x[c.k][:, :, :]
                        st.link(dve.tensor_tensor(v, x0[c.k][:, :, :], p0[c.k][:, :, :], ALU.add))
                        st.link(dve.tensor_tensor(v, v, g[c.k][:, :, :], ALU.add))
                        dve.sem_inc(g_used[c.k], 1)
                        dve.sem_inc(x_used[c.k], 1)
                        st.link(dve.tensor_tensor(tl[:, :, :], x[c.k][:, T:2 * T, :], bc(cur[c.k][:, LAST, :], T), ALU.mult))
                        broadcast_back(dve, st, b, tl, cur[c.k], c)
                        dve.sem_inc(x_ready[c.k], 1)
                        centre_apart(dve, st, v, xc[c.k][:, :, :], mean[c.k][:, :], 2 * T, centred, c)

                    def back(c):
                        variance(dve, sq[c.k][:, :, :], var[c.k][:, :], squared, summed, c)
                        ready(dve, rooted, c)
                        st.link(dve.reciprocal(mean[c.k][:, :], sd[c.k][:, :]))
                        free(dve, h_turned, c)
                        free(dve, h_out, c, 16)
                        for a in range(2):
                            st.mark(dve.scalar_tensor_tensor(h[c.k][:, :, a, :], xc[c.k][:, a * T:(a + 1) * T, :], 0.0,
                                                             bc(mean[c.k][:, a * T:(a + 1) * T], T), ALU.max, ALU.mult))
                        st.wait()
                        dve.sem_inc(h_ready[c.k], 1)

                    def finish(c):
                        ready(dve, tanhed, c)
                        v = m[c.k][:, :, :]
                        st.link(dve.tensor_tensor(v, v, rb(W_OUT, T), ALU.mult))
                        settle(dve)
                        st.link(dve.reduce_sum(scores[:, bass.ds((CH - 1 - c.index) * T, T), 0], v, AX.X))
                        dve.sem_inc(m_used[c.k], 1)
                    skewed(dve, st, CH, front, lambda c: None, back, finish, lag=2)

        WEIGHTS = 16 * (10 + 3 + 7 + 12 + 1)
        edge_structure()
        node_links()
        nodes_first()
        convolution(True)
        carry("c0a", sum0a)
        convolution(False)
        carry("c0b", sum0b, more="scaled")
        seeds("se", sum0b)
        layer1_scores()
        softmax("s1", RULES)
        weighted(True)
        carry("c1", raw1, act1, "layer1")
        relational(True)
        carry("c2a", sum2a, stats=True)
        batch_norm()
        relational(False)
        carry("c2b", sum2b)
        layer3_scores()
        softmax("s3", 1)
        weighted(False)
        carry("c3", fin, out, "final")


_OUTS = [((100000, 64), "float32")]


def kernel(**inputs):
    import concourse.bacc as bacc
    from concourse.bass_utils import run_bass_kernel_spmd

    nc = bacc.Bacc("TRN2", target_bir_lowering=False, num_devices=1)
    arrays, args = {}, {}
    for name, value in inputs.items():
        a = np.ascontiguousarray(value)
        arrays[f"in_{name}"] = a
        args[name] = nc.dram_tensor(f"in_{name}", a.shape, mybir.dt.from_np(a.dtype), kind="ExternalInput").ap()
    shape, dtype = _OUTS[0]
    out = nc.dram_tensor("out", shape, mybir.dt.from_np(np.dtype(dtype)), kind="ExternalOutput").ap()
    build(nc, args, out)
    r = run_bass_kernel_spmd(nc, [arrays], core_ids=[0])
    return r.results[0]["out"]
```
